# Optimizing a Trainium2 kernel written in Bass

```python
import numpy as np
import jax
import jax.numpy as jnp

def _softmax(x, axis=-1):
    return jax.nn.softmax(x, axis=axis)

def _gelu(x):
    return jax.nn.gelu(x, approximate=True)

def _silu(x):
    return jax.nn.silu(x)

def _sigmoid(x):
    return jax.nn.sigmoid(x)

def _layernorm(x, axis=-1, eps=1e-05):
    m = jnp.mean(x, axis=axis, keepdims=True)
    v = jnp.var(x, axis=axis, keepdims=True)
    return (x - m) / jnp.sqrt(v + eps)

def _scatter_add(tgt, idx, src, axis=0):
    return tgt.at[idx].add(src)

def _segment_sum(src, seg, n):
    return jax.ops.segment_sum(src, seg, n)
kernel_name = 'mk_flamingo_gated_d4_seqx_r8_5559b4'

def setup_inputs(seed: int=0):
    np.random.seed(seed)
    _w = jnp.asarray

    def _rec_inputs():
        import jax
        import jax.numpy as jnp
        _rk = jax.random.key(seed)
        x = 7.22e-05 + 1 * jax.random.normal(jax.random.fold_in(_rk, 1), (32, 64, 512), jnp.float32)
        _lenS = 64 - jax.random.randint(jax.random.fold_in(_rk, 7), (32,), 0, max(1, 64 // 4) + 1, jnp.int32)
        _lenS2 = 64 - jax.random.randint(jax.random.fold_in(_rk, 8), (32,), 0, max(1, 64 // 4) + 1, jnp.int32)
        _ctx_4096P = jax.random.normal(jax.random.fold_in(_rk, 11), (32, 16, 512), jnp.float32)
        _ctx_4096c = jax.random.dirichlet(jax.random.fold_in(_rk, 511), 0.3 * jnp.ones((16,), jnp.float32), (32, 64))
        _ctx_4096t = jnp.einsum('bsk,bkd->bsd', _ctx_4096c, _ctx_4096P)
        _ctx_4096t = _ctx_4096t * jax.lax.rsqrt(jnp.mean(jnp.square(_ctx_4096t)) + 1e-12) * 0.953939
        ctx_4096 = 2.81802e-05 + 1.00001 * (_ctx_4096t + 0.3 * jax.random.normal(jax.random.fold_in(_rk, 611), (32, 64, 512), jnp.float32))
        _g = jax.random.normal(jax.random.fold_in(_rk, 9001), (2, 4), jnp.float32)
        _g = jnp.sign(_g) * jnp.maximum(jnp.abs(_g), 1.0) + (_g == 0) * 1.0
        g_xattn = _g[0]
        g_ffn = _g[1]
        return (x, ctx_4096, g_xattn, g_ffn)
    x, ctx_4096, g_xattn, g_ffn = _rec_inputs()

    def _L0_xattn_setup():
        import jax, jax.numpy as jnp
        import numpy as np
        HIDDEN = 512
        N_HEADS = 32
        N_KV_HEADS = 8
        HEAD_DIM = HIDDEN // N_HEADS
        N_REP = N_HEADS // N_KV_HEADS
        EPS = 1e-05

        def _rmsnorm(x, w):
            xf = x.astype(jnp.float32)
            var = jnp.mean(xf * xf, axis=-1, keepdims=True)
            return (xf * jax.lax.rsqrt(var + EPS)).astype(x.dtype) * w
        key = jax.random.key(seed)
        ks = jax.random.split(key, 7)
        B, Q, K = (2, 128, 256)
        scale = 0.02
        return {'hidden_states': jax.random.normal(ks[0], (B, Q, HIDDEN), jnp.float32), 'encoder_hidden_states': jax.random.normal(ks[1], (B, K, HIDDEN), jnp.float32), 'wq': jax.random.normal(ks[2], (N_HEADS * HEAD_DIM, HIDDEN), jnp.float32) * scale, 'wk': jax.random.normal(ks[3], (N_KV_HEADS * HEAD_DIM, HIDDEN), jnp.float32) * scale, 'wv': jax.random.normal(ks[4], (N_KV_HEADS * HEAD_DIM, HIDDEN), jnp.float32) * scale, 'wo': jax.random.normal(ks[5], (HIDDEN, N_HEADS * HEAD_DIM), jnp.float32) * scale, 'ln_w': jnp.ones((HIDDEN,), jnp.float32)}
    _L0_xattn_all = _L0_xattn_setup()
    _L0_xattn_in = {k: v for k, v in _L0_xattn_all.items() if k in ('wq', 'wk', 'wv', 'wo', 'ln_w')}
    del _L0_xattn_all

    def _L0_ffn_setup():
        import jax, jax.numpy as jnp
        import numpy as np
        B_L, B_H = (4, 8)
        LIN_SLOPE, LIN_INTER, EST_T = (1.0, 0.0, 64.0)
        BATCH, SEQ, IN_F, OUT_F = (4, 256, 512, 512)
        MAX_BITS = 8

        def dequant_kbit(qweight, lut, bit):
            O, I32 = (qweight.shape[1], qweight.shape[2])
            shifts = jnp.arange(32, dtype=jnp.int32)
            idx = jnp.zeros((O, I32 * 32), dtype=jnp.int32)
            for p in range(bit):
                bits = (qweight[p][:, :, None] >> shifts & 1).reshape(O, I32 * 32)
                idx = idx | bits << p
            return jnp.take_along_axis(lut, idx, axis=1)
        key = jax.random.key(seed)
        k = jax.random.split(key, 5)
        x = jax.random.normal(k[0], (BATCH, SEQ, IN_F), dtype=jnp.float32)
        qweight = jax.random.randint(k[1], (MAX_BITS, OUT_F, IN_F // 32), 0, 2147483647, dtype=jnp.int32)
        lut4 = jax.random.normal(k[2], (OUT_F, 2 ** B_L), dtype=jnp.float32) * 0.02
        lut8 = jax.random.normal(k[3], (OUT_F, 2 ** B_H), dtype=jnp.float32) * 0.02
        bias = jax.random.normal(k[4], (OUT_F,), dtype=jnp.float32) * 0.01
        return {'x': x, 'qweight': qweight, 'lut4': lut4, 'lut8': lut8, 'bias': bias}
    _L0_ffn_all = _L0_ffn_setup()
    _L0_ffn_in = {k: v for k, v in _L0_ffn_all.items() if k in ('qweight', 'lut4', 'lut8', 'bias')}
    del _L0_ffn_all

    def _L1_xattn_setup():
        import jax, jax.numpy as jnp
        import numpy as np
        import math
        HIDDEN = 512
        N_HEADS = 32
        HEAD_DIM = 128
        N_KV_HEADS = 4
        N_GROUPS = N_HEADS // N_KV_HEADS
        key = jax.random.key(seed)
        ks = jax.random.split(key, 6)
        B, NL, S = (8, 64, 512)
        latents = jax.random.normal(ks[0], (B, NL, HIDDEN), dtype=jnp.float32)
        context = jax.random.normal(ks[1], (B, S, HIDDEN), dtype=jnp.float32)
        scale = 1.0 / math.sqrt(HIDDEN)
        Wq = jax.random.normal(ks[2], (HIDDEN, N_HEADS * HEAD_DIM), dtype=jnp.float32) * scale
        Wk = jax.random.normal(ks[3], (HIDDEN, N_KV_HEADS * HEAD_DIM), dtype=jnp.float32) * scale
        Wv = jax.random.normal(ks[4], (HIDDEN, N_KV_HEADS * HEAD_DIM), dtype=jnp.float32) * scale
        Wo = jax.random.normal(ks[5], (N_HEADS * HEAD_DIM, HIDDEN), dtype=jnp.float32) * scale
        return {'latents': latents, 'context': context, 'Wq': Wq, 'Wk': Wk, 'Wv': Wv, 'Wo': Wo}
    _L1_xattn_all = _L1_xattn_setup()
    _L1_xattn_in = {k: v for k, v in _L1_xattn_all.items() if k in ('Wq', 'Wk', 'Wv', 'Wo')}
    del _L1_xattn_all

    def _L1_ffn_setup():
        import math
        import jax, jax.numpy as jnp
        import numpy as np
        SCALING = 16.0 / 32.0

        def real_fourier_orthogonal_multiply(c):
            n = c.shape[-1]
            sqrt_n = math.sqrt(n)
            pair_scale = math.sqrt(n / 2.0)
            max_f = (n - 1) // 2
            work = c.astype(jnp.float32)
            dc = (work[..., 0] * sqrt_n)[..., None].astype(jnp.complex64)
            cos = work[..., 1:1 + 2 * max_f:2] * pair_scale
            sin = work[..., 2:2 + 2 * max_f:2] * pair_scale
            mid = (cos - 1j * sin).astype(jnp.complex64)
            parts = [dc, mid]
            if n % 2 == 0:
                parts.append((work[..., -1] * sqrt_n)[..., None].astype(jnp.complex64))
            spectrum = jnp.concatenate(parts, axis=-1)
            return jnp.fft.irfft(spectrum, n=n, axis=-1).astype(c.dtype)
        key = jax.random.key(seed)
        ks = jax.random.split(key, 9)
        B, S, D_in, D_out, R0, R1, E = (4, 256, 512, 512, 32, 8, 3)
        x = jax.random.normal(ks[0], (B, S, D_in), dtype=jnp.float32)
        W_base = jax.random.normal(ks[1], (D_out, D_in), dtype=jnp.float32) * 0.02
        b_base = jax.random.normal(ks[2], (D_out,), dtype=jnp.float32) * 0.02
        enc0 = jax.random.normal(ks[3], (R0, D_in), dtype=jnp.float32) * 0.02
        enc1 = jax.random.normal(ks[4], (R1, D_in), dtype=jnp.float32) * 0.02
        coefs0 = jax.random.normal(ks[5], (E, D_out, R0), dtype=jnp.float32) * 0.02
        coefs1 = jax.random.normal(ks[6], (E, D_out, R1), dtype=jnp.float32) * 0.02
        mask0 = jax.random.randint(ks[7], (E, D_out, R0), 0, 2).astype(bool)
        mask1 = jax.random.randint(ks[8], (E, D_out, R1), 0, 2).astype(bool)
        return dict(x=x, W_base=W_base, b_base=b_base, enc0=enc0, enc1=enc1, coefs0=coefs0, coefs1=coefs1, mask0=mask0, mask1=mask1)
    _L1_ffn_all = _L1_ffn_setup()
    _L1_ffn_in = {k: v for k, v in _L1_ffn_all.items() if k in ('W_base', 'b_base', 'enc0', 'enc1', 'coefs0', 'coefs1', 'mask0', 'mask1')}
    del _L1_ffn_all

    def _L2_xattn_setup():
        import jax, jax.numpy as jnp
        import numpy as np
        HEADS = 8
        WINDOW = 16

        def _pointwise(W, b, t):
            return jnp.einsum('oc,bct->bot', W, t) + b[None, :, None]
        key = jax.random.key(seed)
        ks = jax.random.split(key, 10)
        B, C, T = (4, 64, 512)
        s = 0.02
        return {'x': jax.random.normal(ks[0], (B, C, T), jnp.float32), 'cond': jax.random.normal(ks[1], (B, C, T), jnp.float32), 'Wq': jax.random.normal(ks[2], (C, C), jnp.float32) * s, 'bq': jnp.zeros((C,), jnp.float32), 'Wk': jax.random.normal(ks[3], (C, C), jnp.float32) * s, 'bk': jnp.zeros((C,), jnp.float32), 'Wv': jax.random.normal(ks[4], (C, C), jnp.float32) * s, 'bv': jnp.zeros((C,), jnp.float32), 'Wo': jax.random.normal(ks[5], (C, C), jnp.float32) * s, 'bo': jnp.zeros((C,), jnp.float32)}
    _L2_xattn_all = _L2_xattn_setup()
    _L2_xattn_in = {k: v for k, v in _L2_xattn_all.items() if k in ('Wq', 'bq', 'Wk', 'bk', 'Wv', 'bv', 'Wo', 'bo')}
    del _L2_xattn_all

    def _L2_ffn_setup():
        import jax, jax.numpy as jnp
        import numpy as np
        import math
        IN_DIM = 512
        FEATURES = 512
        BATCH, SEQ = (8, 256)
        key = jax.random.key(seed)
        kx, kk = jax.random.split(key)
        x = jax.random.normal(kx, (BATCH, SEQ, IN_DIM), dtype=jnp.float32)
        kernel = jax.random.randint(kk, (IN_DIM, FEATURES), 0, 2) > 0
        scale = jnp.asarray(1.0 / math.sqrt(IN_DIM), dtype=jnp.float32)
        return {'x': x, 'kernel': kernel, 'scale': scale}
    _L2_ffn_all = _L2_ffn_setup()
    _L2_ffn_in = {k: v for k, v in _L2_ffn_all.items() if k in ('kernel', 'scale')}
    del _L2_ffn_all

    def _L3_xattn_setup():
        import jax, jax.numpy as jnp
        import numpy as np
        EMBED = 512
        NUM_Q = 32
        NUM_KV = 8
        GROUPS = NUM_Q // NUM_KV
        HEAD_DIM = EMBED // NUM_Q
        KV_DIM = HEAD_DIM * NUM_KV
        key = jax.random.key(seed)
        ks = jax.random.split(key, 12)
        B, S = (2, 256)
        s = 0.02
        return {'query': jax.random.normal(ks[0], (B, S, EMBED), jnp.float32), 'key': jax.random.normal(ks[1], (B, S, EMBED), jnp.float32), 'value': jax.random.normal(ks[2], (B, S, EMBED), jnp.float32), 'Wq': jax.random.normal(ks[3], (EMBED, EMBED), jnp.float32) * s, 'bq': jnp.zeros((EMBED,), jnp.float32), 'Wk': jax.random.normal(ks[4], (EMBED, KV_DIM), jnp.float32) * s, 'bk': jnp.zeros((KV_DIM,), jnp.float32), 'Wv': jax.random.normal(ks[5], (EMBED, KV_DIM), jnp.float32) * s, 'bv': jnp.zeros((KV_DIM,), jnp.float32), 'Wo': jax.random.normal(ks[6], (EMBED, EMBED), jnp.float32) * s, 'bo': jnp.zeros((EMBED,), jnp.float32)}
    _L3_xattn_all = _L3_xattn_setup()
    _L3_xattn_in = {k: v for k, v in _L3_xattn_all.items() if k in ('Wq', 'bq', 'Wk', 'bk', 'Wv', 'bv', 'Wo', 'bo')}
    del _L3_xattn_all

    def _L3_ffn_setup():
        import jax, jax.numpy as jnp
        import numpy as np
        ALPHA = 32
        R = 16
        SCALING = ALPHA / R
        key = jax.random.key(seed)
        k1, k2, k3, k4 = jax.random.split(key, 4)
        B_, S, D = (4, 256, 512)
        H, r, O = (8, R, 512)
        x = jax.random.normal(k1, (B_, S, D), dtype=jnp.float32)
        A = jax.random.normal(k2, (H, r, D), dtype=jnp.float32) * 0.02
        Bm = jax.random.normal(k3, (H, O, r), dtype=jnp.float32) * 0.02
        Wr = jax.random.normal(k4, (H, D), dtype=jnp.float32) * 0.02
        br = jnp.zeros((H,), dtype=jnp.float32)
        return {'x': x, 'A': A, 'B': Bm, 'Wr': Wr, 'br': br}
    _L3_ffn_all = _L3_ffn_setup()
    _L3_ffn_in = {k: v for k, v in _L3_ffn_all.items() if k in ('A', 'B', 'Wr', 'br')}
    del _L3_ffn_all
    return {'x': x, 'ctx_4096': ctx_4096, 'g_xattn': g_xattn, 'g_ffn': g_ffn, 'L0_xattn_wq': _L0_xattn_in['wq'], 'L0_xattn_wk': _L0_xattn_in['wk'], 'L0_xattn_wv': _L0_xattn_in['wv'], 'L0_xattn_wo': _L0_xattn_in['wo'], 'L0_xattn_ln_w': _L0_xattn_in['ln_w'], 'L0_ffn_qweight': _L0_ffn_in['qweight'], 'L0_ffn_lut4': _L0_ffn_in['lut4'], 'L0_ffn_lut8': _L0_ffn_in['lut8'], 'L0_ffn_bias': _L0_ffn_in['bias'], 'L1_xattn_Wq': _L1_xattn_in['Wq'], 'L1_xattn_Wk': _L1_xattn_in['Wk'], 'L1_xattn_Wv': _L1_xattn_in['Wv'], 'L1_xattn_Wo': _L1_xattn_in['Wo'], 'L1_ffn_W_base': _L1_ffn_in['W_base'], 'L1_ffn_b_base': _L1_ffn_in['b_base'], 'L1_ffn_enc0': _L1_ffn_in['enc0'], 'L1_ffn_enc1': _L1_ffn_in['enc1'], 'L1_ffn_coefs0': _L1_ffn_in['coefs0'], 'L1_ffn_coefs1': _L1_ffn_in['coefs1'], 'L1_ffn_mask0': _L1_ffn_in['mask0'], 'L1_ffn_mask1': _L1_ffn_in['mask1'], 'L2_xattn_Wq': _L2_xattn_in['Wq'], 'L2_xattn_bq': _L2_xattn_in['bq'], 'L2_xattn_Wk': _L2_xattn_in['Wk'], 'L2_xattn_bk': _L2_xattn_in['bk'], 'L2_xattn_Wv': _L2_xattn_in['Wv'], 'L2_xattn_bv': _L2_xattn_in['bv'], 'L2_xattn_Wo': _L2_xattn_in['Wo'], 'L2_xattn_bo': _L2_xattn_in['bo'], 'L2_ffn_kernel': _L2_ffn_in['kernel'], 'L2_ffn_scale': _L2_ffn_in['scale'], 'L3_xattn_Wq': _L3_xattn_in['Wq'], 'L3_xattn_bq': _L3_xattn_in['bq'], 'L3_xattn_Wk': _L3_xattn_in['Wk'], 'L3_xattn_bk': _L3_xattn_in['bk'], 'L3_xattn_Wv': _L3_xattn_in['Wv'], 'L3_xattn_bv': _L3_xattn_in['bv'], 'L3_xattn_Wo': _L3_xattn_in['Wo'], 'L3_xattn_bo': _L3_xattn_in['bo'], 'L3_ffn_A': _L3_ffn_in['A'], 'L3_ffn_B': _L3_ffn_in['B'], 'L3_ffn_Wr': _L3_ffn_in['Wr'], 'L3_ffn_br': _L3_ffn_in['br']}

def reference(x, ctx_4096, g_xattn, g_ffn, L0_xattn_wq, L0_xattn_wk, L0_xattn_wv, L0_xattn_wo, L0_xattn_ln_w, L0_ffn_qweight, L0_ffn_lut4, L0_ffn_lut8, L0_ffn_bias, L1_xattn_Wq, L1_xattn_Wk, L1_xattn_Wv, L1_xattn_Wo, L1_ffn_W_base, L1_ffn_b_base, L1_ffn_enc0, L1_ffn_enc1, L1_ffn_coefs0, L1_ffn_coefs1, L1_ffn_mask0, L1_ffn_mask1, L2_xattn_Wq, L2_xattn_bq, L2_xattn_Wk, L2_xattn_bk, L2_xattn_Wv, L2_xattn_bv, L2_xattn_Wo, L2_xattn_bo, L2_ffn_kernel, L2_ffn_scale, L3_xattn_Wq, L3_xattn_bq, L3_xattn_Wk, L3_xattn_bk, L3_xattn_Wv, L3_xattn_bv, L3_xattn_Wo, L3_xattn_bo, L3_ffn_A, L3_ffn_B, L3_ffn_Wr, L3_ffn_br):
    import jax
    import jax.numpy as jnp

    def _L0_xattn_ref(hidden_states, encoder_hidden_states, wq, wk, wv, wo, ln_w):
        import jax, jax.numpy as jnp
        import numpy as np
        HIDDEN = 512
        N_HEADS = 32
        N_KV_HEADS = 8
        HEAD_DIM = HIDDEN // N_HEADS
        N_REP = N_HEADS // N_KV_HEADS
        EPS = 1e-05

        def _rmsnorm(x, w):
            xf = x.astype(jnp.float32)
            var = jnp.mean(xf * xf, axis=-1, keepdims=True)
            return (xf * jax.lax.rsqrt(var + EPS)).astype(x.dtype) * w
        B, Qlen, _ = hidden_states.shape
        _, Klen, _ = encoder_hidden_states.shape
        x = _rmsnorm(hidden_states, ln_w)
        q = jnp.einsum('bqd,hd->bqh', x, wq).reshape(B, Qlen, N_HEADS, HEAD_DIM)
        k = jnp.einsum('bkd,hd->bkh', encoder_hidden_states, wk).reshape(B, Klen, N_KV_HEADS, HEAD_DIM)
        v = jnp.einsum('bkd,hd->bkh', encoder_hidden_states, wv).reshape(B, Klen, N_KV_HEADS, HEAD_DIM)
        q = q.transpose(0, 2, 1, 3)
        k = k.transpose(0, 2, 1, 3)
        v = v.transpose(0, 2, 1, 3)
        k = jnp.repeat(k, N_REP, axis=1)
        v = jnp.repeat(v, N_REP, axis=1)
        scores = jnp.einsum('bhqd,bhkd->bhqk', q, k) / np.sqrt(HEAD_DIM).astype(np.float32)
        attn = jax.nn.softmax(scores.astype(jnp.float32), axis=-1).astype(q.dtype)
        out = jnp.einsum('bhqk,bhkd->bhqd', attn, v)
        out = out.transpose(0, 2, 1, 3).reshape(B, Qlen, HIDDEN)
        return jnp.einsum('bqh,dh->bqd', out, wo)

    def _L0_ffn_ref(x, qweight, lut4, lut8, bias):
        import jax, jax.numpy as jnp
        import numpy as np
        B_L, B_H = (4, 8)
        LIN_SLOPE, LIN_INTER, EST_T = (1.0, 0.0, 64.0)
        BATCH, SEQ, IN_F, OUT_F = (4, 256, 512, 512)
        MAX_BITS = 8

        def dequant_kbit(qweight, lut, bit):
            O, I32 = (qweight.shape[1], qweight.shape[2])
            shifts = jnp.arange(32, dtype=jnp.int32)
            idx = jnp.zeros((O, I32 * 32), dtype=jnp.int32)
            for p in range(bit):
                bits = (qweight[p][:, :, None] >> shifts & 1).reshape(O, I32 * 32)
                idx = idx | bits << p
            return jnp.take_along_axis(lut, idx, axis=1)
        e = jnp.linalg.norm(x, axis=-1) * LIN_SLOPE + LIN_INTER
        mask = e > EST_T
        w_l = dequant_kbit(qweight, lut4, B_L)
        w_h = dequant_kbit(qweight, lut8, B_H)
        y_l = jnp.einsum('bsi,oi->bso', x, w_l)
        y_h = jnp.einsum('bsi,oi->bso', x, w_h)
        y = jnp.where(mask[..., None], y_h, y_l) + bias
        return y

    def _L1_xattn_ref(latents, context, Wq, Wk, Wv, Wo):
        import jax, jax.numpy as jnp
        import numpy as np
        import math
        HIDDEN = 512
        N_HEADS = 32
        HEAD_DIM = 128
        N_KV_HEADS = 4
        N_GROUPS = N_HEADS // N_KV_HEADS
        b, q_len, _ = latents.shape
        kv_len = q_len + context.shape[1]
        hidden_states = jnp.concatenate([context, latents], axis=1)
        q = (latents @ Wq).reshape(b, q_len, N_KV_HEADS, N_GROUPS, HEAD_DIM)
        k = (hidden_states @ Wk).reshape(b, kv_len, N_KV_HEADS, HEAD_DIM)
        v = (hidden_states @ Wv).reshape(b, kv_len, N_KV_HEADS, HEAD_DIM)
        scale = 1.0 / math.sqrt(HEAD_DIM)
        scores = jnp.einsum('bqhgd,bkhd->bhgqk', q, k) * scale
        attn = jax.nn.softmax(scores.astype(jnp.float32), axis=-1).astype(q.dtype)
        out = jnp.einsum('bhgqk,bkhd->bqhgd', attn, v)
        out = out.reshape(b, q_len, N_HEADS * HEAD_DIM)
        return out @ Wo

    def _L1_ffn_ref(x, W_base, b_base, enc0, enc1, coefs0, coefs1, mask0, mask1):
        import math
        import jax, jax.numpy as jnp
        import numpy as np
        SCALING = 16.0 / 32.0

        def real_fourier_orthogonal_multiply(c):
            n = c.shape[-1]
            sqrt_n = math.sqrt(n)
            pair_scale = math.sqrt(n / 2.0)
            max_f = (n - 1) // 2
            work = c.astype(jnp.float32)
            dc = (work[..., 0] * sqrt_n)[..., None].astype(jnp.complex64)
            cos = work[..., 1:1 + 2 * max_f:2] * pair_scale
            sin = work[..., 2:2 + 2 * max_f:2] * pair_scale
            mid = (cos - 1j * sin).astype(jnp.complex64)
            parts = [dc, mid]
            if n % 2 == 0:
                parts.append((work[..., -1] * sqrt_n)[..., None].astype(jnp.complex64))
            spectrum = jnp.concatenate(parts, axis=-1)
            return jnp.fft.irfft(spectrum, n=n, axis=-1).astype(c.dtype)
        base = jnp.einsum('bsd,od->bso', x, W_base) + b_base
        e0 = jnp.einsum('bsd,rd->bsr', x, enc0)
        e1 = jnp.einsum('bsd,rd->bsr', x, enc1)
        w0 = coefs0 * mask0.astype(coefs0.dtype)
        w1 = coefs1 * mask1.astype(coefs1.dtype)
        decoded = jnp.einsum('bsr,eor->ebso', e0, w0) + jnp.einsum('bsr,eor->ebso', e1, w1)
        transformed = real_fourier_orthogonal_multiply(decoded)
        update = transformed.sum(axis=0)
        return base + update * SCALING

    def _L2_xattn_ref(x, cond, Wq, bq, Wk, bk, Wv, bv, Wo, bo):
        import jax, jax.numpy as jnp
        import numpy as np
        HEADS = 8
        WINDOW = 16

        def _pointwise(W, b, t):
            return jnp.einsum('oc,bct->bot', W, t) + b[None, :, None]
        B, C, T = x.shape
        H, W = (HEADS, WINDOW)
        hd = C // H
        scale = hd ** (-0.5)
        pad_left = W // 2
        pad_right = W - pad_left - 1
        q = _pointwise(Wq, bq, x)
        k = _pointwise(Wk, bk, cond)
        v = _pointwise(Wv, bv, cond)
        k = jnp.pad(k, ((0, 0), (0, 0), (pad_left, pad_right)))
        v = jnp.pad(v, ((0, 0), (0, 0), (pad_left, pad_right)))
        idx = jnp.arange(T)[:, None] + jnp.arange(W)[None, :]
        k_win = k[:, :, idx].reshape(B, H, hd, T, W)
        v_win = v[:, :, idx].reshape(B, H, hd, T, W)
        qh = q.reshape(B, H, hd, T)
        dots = jnp.einsum('bhdt,bhdtw->bhtw', qh, k_win) * scale
        attn = jax.nn.softmax(dots, axis=-1)
        out = jnp.einsum('bhtw,bhdtw->bhdt', attn, v_win)
        out = out.reshape(B, C, T)
        return _pointwise(Wo, bo, out)

    def _L2_ffn_ref(x, kernel, scale):
        import jax, jax.numpy as jnp
        import numpy as np
        import math
        IN_DIM = 512
        FEATURES = 512
        BATCH, SEQ = (8, 256)
        w = kernel.astype(x.dtype) * 2.0 - 1.0
        return scale * jnp.einsum('bsi,if->bsf', x, w)

    def _L3_xattn_ref(query, key, value, Wq, bq, Wk, bk, Wv, bv, Wo, bo):
        import jax, jax.numpy as jnp
        import numpy as np
        EMBED = 512
        NUM_Q = 32
        NUM_KV = 8
        GROUPS = NUM_Q // NUM_KV
        HEAD_DIM = EMBED // NUM_Q
        KV_DIM = HEAD_DIM * NUM_KV
        B, S, _ = query.shape
        Q = query @ Wq + bq
        K = key @ Wk + bk
        V = value @ Wv + bv
        Q = Q.reshape(B, S, NUM_KV, GROUPS, HEAD_DIM).transpose(0, 2, 3, 1, 4)
        K = K.reshape(B, S, NUM_KV, HEAD_DIM).transpose(0, 2, 1, 3)
        V = V.reshape(B, S, NUM_KV, HEAD_DIM).transpose(0, 2, 1, 3)
        scale = 1.0 / jnp.sqrt(jnp.asarray(HEAD_DIM, query.dtype))
        scores = jnp.einsum('bhgqd,bhkd->bhgqk', Q, K) * scale
        w = jax.nn.softmax(scores, axis=-1)
        y = jnp.einsum('bhgqk,bhkd->bhgqd', w, V)
        y = y.transpose(0, 3, 1, 2, 4).reshape(B, S, EMBED)
        return y @ Wo + bo

    def _L3_ffn_ref(x, A, B, Wr, br):
        import jax, jax.numpy as jnp
        import numpy as np
        ALPHA = 32
        R = 16
        SCALING = ALPHA / R
        H = A.shape[0]
        router_logits = jnp.einsum('bsd,hd->bsh', x, Wr) + br
        scores = H * jax.nn.softmax(router_logits, axis=-1)
        low = jnp.einsum('bsd,hrd->bshr', x, A)
        out = jnp.einsum('bshr,hor,bsh->bso', low, B, scores)
        return SCALING * out
    x = x + jnp.tanh(g_xattn[0]) * _L0_xattn_ref(_layernorm(x, axis=-1), ctx_4096, L0_xattn_wq, L0_xattn_wk, L0_xattn_wv, L0_xattn_wo, L0_xattn_ln_w)
    x = x + jnp.tanh(g_ffn[0]) * _L0_ffn_ref(_layernorm(x, axis=-1), L0_ffn_qweight, L0_ffn_lut4, L0_ffn_lut8, L0_ffn_bias)
    x = x + jnp.tanh(g_xattn[1]) * _L1_xattn_ref(_layernorm(x, axis=-1), ctx_4096, L1_xattn_Wq, L1_xattn_Wk, L1_xattn_Wv, L1_xattn_Wo)
    x = x + jnp.tanh(g_ffn[1]) * _L1_ffn_ref(_layernorm(x, axis=-1), L1_ffn_W_base, L1_ffn_b_base, L1_ffn_enc0, L1_ffn_enc1, L1_ffn_coefs0, L1_ffn_coefs1, L1_ffn_mask0, L1_ffn_mask1)
    x = x + jnp.tanh(g_xattn[2]) * _L2_xattn_ref(_layernorm(x, axis=-1), ctx_4096, L2_xattn_Wq, L2_xattn_bq, L2_xattn_Wk, L2_xattn_bk, L2_xattn_Wv, L2_xattn_bv, L2_xattn_Wo, L2_xattn_bo)
    x = x + jnp.tanh(g_ffn[2]) * _L2_ffn_ref(_layernorm(x, axis=-1), L2_ffn_kernel, L2_ffn_scale)
    x = x + jnp.tanh(g_xattn[3]) * _L3_xattn_ref(_layernorm(x, axis=-1), ctx_4096, ctx_4096, L3_xattn_Wq, L3_xattn_bq, L3_xattn_Wk, L3_xattn_bk, L3_xattn_Wv, L3_xattn_bv, L3_xattn_Wo, L3_xattn_bo)
    x = x + jnp.tanh(g_ffn[3]) * _L3_ffn_ref(_layernorm(x, axis=-1), L3_ffn_A, L3_ffn_B, L3_ffn_Wr, L3_ffn_br)
    return x

_drawn_inputs = setup_inputs


def setup_inputs(seed=0):
    import zlib

    import numpy as np

    out = dict(_drawn_inputs(seed))
    spreads = {'L0_xattn_ln_w': (1.0, 0.6),
     'L2_xattn_bq': (0.0, 0.8),
     'L2_xattn_bk': (0.0, 2.0),
     'L2_xattn_bv': (0.0, 0.8),
     'L2_xattn_bo': (0.0, 0.1),
     'L3_xattn_bq': (0.0, 0.8),
     'L3_xattn_bk': (0.0, 2.0),
     'L3_xattn_bv': (0.0, 0.402),
     'L3_xattn_bo': (0.0, 0.1),
     'L3_ffn_br': (0.0, 0.794)}
    factors = {'g_ffn': 33.656,
     'L0_xattn_wq': 8.0,
     'L0_xattn_wk': 8.0,
     'L0_ffn_bias': 5.528,
     'L1_ffn_b_base': 4.378,
     'L1_ffn_enc0': 2.761,
     'L1_ffn_enc1': 5.75,
     'L1_ffn_coefs0': 2.786,
     'L1_ffn_coefs1': 5.775,
     'L2_xattn_Wq': 8.0,
     'L2_xattn_Wk': 8.0,
     'L2_xattn_Wv': 8.0,
     'L2_xattn_Wo': 7.154,
     'L3_xattn_Wq': 8.0,
     'L3_xattn_Wk': 8.0}
    for name, (base, spread) in spreads.items():
        noise = np.random.default_rng([zlib.crc32(name.encode()), seed]).standard_normal(out[name].shape)
        drawn = base * np.exp(spread * noise) if base else spread * noise
        out[name] = jnp.asarray(drawn.astype(out[name].dtype))
    for name, factor in factors.items():
        out[name] = (out[name] * factor).astype(out[name].dtype)
    return out
```

```python
from contextlib import ExitStack

import concourse.bass as bass
from concourse import mybir

F32 = mybir.dt.float32
I32 = mybir.dt.int32
U8 = mybir.dt.uint8
ALU = mybir.AluOpType
ACT = mybir.ActivationFunctionType
AX_X = mybir.AxisListType.X

P = 128
D = 512
C = D // P
TOKENS = 32 * 64
SEQ = 64
EPS = 1e-5
DMA = 16

KV = 8
HD = 16
REP = 4
ENTRY = 2 * HD + 2


def heads_as_given(ap):
    return ap.rearrange("p (k r d) -> p k r d", k=KV, r=REP)


def heads_by_rep(ap):
    return ap.rearrange("p (r k d) -> p k r d", k=KV, r=REP)


class Banks:

    def __init__(self, banks, setup, loop):
        assert len(setup) % 2 == 0 and len(loop) % 2 == 0 and len(set(loop)) == len(loop)
        self.banks, self.setup, self.loop = banks, setup, loop

    def turn(self, i, label):
        if i is None:
            return self.setup.index(label)
        return len(self.setup) + i * len(self.loop) + self.loop.index(label)

    def free(self, i, label):
        return self.turn(i, label) + 1

    def full(self, i, label):
        return self.turn(i, label) + 1

    def done(self, i, label):
        return self.turn(i, label) + 3

    def bank(self, i, label):
        return self.banks[(self.setup if i is None else self.loop).index(label) % 2]


class Chip:

    def __init__(self, nc, ctx, phase):
        self.nc, self.ctx, self.phase = nc, ctx, phase

    def sb(self, name, shape, dtype=F32):
        return self.ctx.enter_context(self.nc.sbuf_tensor(f"{self.phase}_{name}", shape, dtype))

    def banks(self, name):
        return [self.ctx.enter_context(self.nc.psum_tensor(f"{self.phase}_{name}{n}", [P, D], F32))
                for n in range(2)]

    def sem(self, name):
        return self.ctx.enter_context(self.nc.semaphore(f"{self.phase}_{name}"))


def split4(ap):
    return ap.rearrange("p (c n) -> p c n", c=4)


class Region:

    def __init__(self, tensor):
        self.tensor, self.at = tensor, 0

    def carve(self, name, shape, dtype=F32):
        size = 1
        for n in shape[1:]:
            size *= n
        ap = self.tensor[0:shape[0], self.at:self.at + size]
        self.at += size
        assert self.at <= self.tensor.shape[1]
        if dtype != F32:
            ap = ap.bitcast(dtype)
        names = "abcd"[:len(shape) - 1]
        sizes = dict(zip(names[1:], shape[2:]))
        return ap if len(shape) == 2 else ap.rearrange(f"p ({' '.join(names)}) -> p {' '.join(names)}", **sizes)


def along(ap, n):
    return ap.unsqueeze(2).to_broadcast([ap.shape[0], ap.shape[1], n])


def turned(nc, out, src, ident):
    for c in range(C):
        last = nc.tensor.transpose(out[:, c * P:(c + 1) * P], src[:, c * P:(c + 1) * P], ident[:, :])
    return last


class HeadsOf16:

    def __init__(self, chip, batches, shared=None):
        sb, sem = chip.sb, chip.sem
        shared = shared or sb
        T = batches * SEQ
        self.nc, self.B, self.UNITS, self.T = chip.nc, batches, 2 * batches, T
        self.kmask = sb("kmask", [P, KV])
        self.qt, self.kbd = shared("qt", [P, batches, REP, SEQ]), shared("kbd", [P, batches, KV, SEQ])
        self.vbd = sb("vbd", [P, batches, KV // 2, ENTRY])
        self.probs, self.probs_t = shared("probs", [P, 3, KV, SEQ]), shared("probs_t", [P, 2, KV // 2 * P])
        self.neg_max, self.inv_sum = sb("neg_max", [P, 2, KV]), sb("inv_sum", [P, 2, KV // 2, 2])
        self.o_tok, self.ot = sb("o_tok", [P, 2, KV // 2, 2, HD]), shared("ot", [P, REP, T])
        self.s_filled, self.s_emptied = sem("s_filled"), sem("s_emptied")
        self.o_filled, self.o_emptied = sem("o_filled"), sem("o_emptied")
        self.max_made, self.exp_made, self.inv_made = sem("max_made"), sem("exp_made"), sem("inv_made")

    def order(self, steps):
        s_labels = [f"s{u}" for u in range(self.UNITS)]
        o_labels = []
        for s in range(steps):
            if 0 <= s - 3 < self.UNITS:
                o_labels.append(f"av{s - 3}")
            if 0 <= s - 4 < self.UNITS:
                o_labels.append(f"ot{s - 4}")
        return s_labels, o_labels

    def make_masks(self, pool, cleared, made):
        nc = self.nc
        nc.gpsimd.memset(self.kmask[:, :], 1.0).then_inc(cleared, 1)
        nc.gpsimd.memset(self.vbd[:, :, :, :], 0.0).then_inc(cleared, 1)
        pool.wait_ge(cleared, 2)
        nc.gpsimd.affine_select(out=self.kmask[:, :], in_=self.kmask[:, :], compare_op=ALU.is_ge, fill=0.0,
                                base=0, pattern=[[-HD, KV]], channel_multiplier=1).then_inc(made, 1)
        for half in range(2):
            rows = slice(half * SEQ, (half + 1) * SEQ)
            pool.wait_ge(made, 1 + half)
            nc.gpsimd.memset(self.vbd[rows, :, :, 2 * HD + half:2 * HD + half + 1], 1.0).then_inc(made, 1)
        pool.wait_ge(made, 3)
        nc.gpsimd.affine_select(out=self.kmask[:, :], in_=self.kmask[:, :], compare_op=ALU.is_ge, fill=0.0,
                                base=HD - 1, pattern=[[HD, KV]], channel_multiplier=-1).then_inc(made, 1)


    def pe_keys(self, out, wk, ctxt):
        for c in range(C):
            last = self.nc.tensor.matmul(out[:, :], wk[:, c, :], ctxt[:, c, :], start=(c == 0), stop=(c == C - 1))
        return last

    def pe_values_in(self, out, wv, ctxt):
        for t in range(self.T // P):
            for c in range(C):
                last = self.nc.tensor.matmul(out[:, t * P:(t + 1) * P], ctxt[:, c, t * P:(t + 1) * P], wv[:, c, :],
                                             start=(c == 0), stop=(c == C - 1))
        return last

    def pe_queries(self, out, wq, xnt, r):
        for c in range(C):
            last = self.nc.tensor.matmul(out[:, :], wq[:, c, r * P:(r + 1) * P], xnt[:, c, :],
                                         start=(c == 0), stop=(c == C - 1))
        return last

    def pe_scores(self, out, u):
        b, j = u // 2, u % 2
        return self.nc.tensor.matmul(out[:, :], self.qt[:, b, 2 * j:2 * j + 2, :].rearrange("p r s -> p (r s)"),
                                     self.kbd[:, b, :, :], start=True, stop=True)

    def pe_turn_probs(self, out, u, ident):
        return turned(self.nc, out, self.probs[:, u % 3].rearrange("p k s -> p (k s)"), ident)

    def pe_attend(self, out, u):
        for p in range(KV // 2):
            last = self.nc.tensor.matmul(out[:, p * ENTRY:(p + 1) * ENTRY], self.probs_t[:, u % 2, p * P:(p + 1) * P],
                                         self.vbd[:, u // 2, p, :], start=True, stop=True)
        return last

    def pe_turn_back(self, out, u, ident):
        return self.nc.tensor.transpose(out[:, 0:P], self.o_tok[:, u % 2].rearrange("p a b d -> p (a b d)"),
                                        ident[:, :])

    def pe_project(self, out, t, wo):
        for r in range(REP):
            last = self.nc.tensor.matmul(out[:, :], self.ot[:, r, t * P:(t + 1) * P], wo[:, r, :],
                                         start=(r == 0), stop=(r == REP - 1))
        return last


    def dve_spread_keys(self, bank, bk=None):
        for b in range(self.B):
            keys = bank[:, b * SEQ:(b + 1) * SEQ].unsqueeze(1).to_broadcast([P, KV, SEQ])
            mask, out = along(self.kmask[:, :], SEQ), self.kbd[:, b, :, :]
            if bk is None:
                last = self.nc.vector.tensor_tensor(out, keys, mask, ALU.mult)
            else:
                last = self.nc.vector.scalar_tensor_tensor(out=out, in0=keys, scalar=bk, in1=mask,
                                                           op0=ALU.add, op1=ALU.mult)
        return last

    def dve_spread_values(self, bank, bv=None):
        values = bank[:, :].rearrange("p (t a h d) -> p t a h d", a=KV // 2, h=2, d=HD)
        vbd = self.vbd[:, :, :, :].rearrange("p (t b) a e -> p t b a e", b=2)
        for b in range(2):
            keys = slice(b * SEQ, (b + 1) * SEQ)
            for h in range(2):
                for t in range(self.T // P):
                    out = vbd[h * SEQ:(h + 1) * SEQ, t, b, :, h * HD:(h + 1) * HD]
                    if bv is None:
                        last = self.nc.vector.tensor_copy(out, values[keys, t, :, h, :])
                    else:
                        last = self.nc.vector.tensor_tensor(out, values[keys, t, :, h, :], bv[keys, :, h, :], ALU.add)
        return last

    def dve_max(self, bank, u):
        return self.nc.vector.tensor_reduce(self.neg_max[:, u % 2, :], bank[:, :].rearrange("p (k s) -> p k s", k=KV),
                                            AX_X, ALU.max, negate=True)

    def dve_shift(self, bank, u):
        return self.nc.vector.tensor_tensor(self.probs[:, u % 3], bank[:, :].rearrange("p (k s) -> p k s", k=KV),
                                            along(self.neg_max[:, u % 2, :], SEQ), ALU.add)

    def dve_inverse(self, bank, u):
        sums = bank[:, 0:KV // 2 * ENTRY].rearrange("p (a e) -> p a e", e=ENTRY)[:, :, 2 * HD:ENTRY]
        return self.nc.vector.reciprocal(self.inv_sum[:, u % 2], sums)

    def dve_norm(self, bank, u):
        values = bank[:, 0:KV // 2 * ENTRY].rearrange("p (a e) -> p a e", e=ENTRY)
        for h in range(2):
            last = self.nc.vector.tensor_tensor(self.o_tok[:, u % 2, :, h, :], values[:, :, h * HD:(h + 1) * HD],
                                                along(self.inv_sum[:, u % 2, :, h], HD), ALU.mult)
        return last

    def dve_copy_back(self, bank, u):
        b, j = u // 2, u % 2
        return self.nc.vector.tensor_copy(self.ot[:, 2 * j:2 * j + 2, b * SEQ:(b + 1) * SEQ],
                                          bank[:, 0:P].rearrange("p (r s) -> p r s", r=2))


    def act_exp(self, u):
        return self.nc.scalar.activation(self.probs[:, u % 3], self.probs[:, u % 3], ACT.Exp, scale=HD ** -0.5)


def cross_attention_and_quantised_ffn(nc, io, x_in, ctx_in, x_out, ctx_t_out):
    TILES = 4
    GROUPS = TOKENS // (TILES * P)
    T = TILES * P
    B = T // SEQ
    OUT, FN, FFN = 7, 10, 11
    ENTRIES = 16

    def tile_at(s, first):
        return (s - first) // 4 if s >= first and (s - first) % 4 == 0 and (s - first) // 4 < TILES else None

    with ExitStack() as ctx:
        chip = Chip(nc, ctx, "l0")
        sb, sem = chip.sb, chip.sem
        heads = HeadsOf16(chip, B)
        UNITS = heads.UNITS
        STEPS = UNITS + 9
        s_loop, o_loop = heads.order(STEPS)
        a_loop = [f"ctx{t}" for t in range(TILES)] + [f"xn{t}" for t in range(TILES)] + [f"q{r}" for r in range(REP)]
        d_loop = ["k", "v"]
        for s in range(STEPS):
            if 0 <= s - 2 < UNITS:
                a_loop.append(f"pt{s - 2}")
            if tile_at(s, OUT) is not None:
                d_loop.append(f"out{tile_at(s, OUT)}")
            if tile_at(s, FN) is not None:
                a_loop.append(f"fn{tile_at(s, FN)}")
            if tile_at(s, FFN) is not None:
                d_loop.append(f"ffn{tile_at(s, FFN)}")
        a_setup = [f"wq{c}" for c in range(C)] + ["wk", "wv"] + [f"wo{r}" for r in range(REP)] + \
                  [f"lut{o}" for o in range(C)]
        A = Banks(chip.banks("bank_a"), a_setup, a_loop)
        Dr = Banks(chip.banks("bank_d"), [], d_loop)
        S = Banks(chip.banks("bank_s"), [], s_loop)
        O = Banks(chip.banks("bank_o"), [], o_loop)

        x_tiles = x_in.rearrange("(g t p) d -> g p t d", p=P, t=TILES)
        ctx_tiles = ctx_in.rearrange("(g t p) d -> g p t d", p=P, t=TILES)
        out_tiles = x_out.rearrange("(g t p) d -> g p t d", p=P, t=TILES)

        ident = sb("ident", [P, P])
        wq_raw, wo_raw = sb("wq_raw", [P, C, D]), sb("wo_raw", [P, C, D])
        wk_raw, wv_raw = sb("wk_raw", [P, D]), sb("wv_raw", [P, D])
        wq, wo = sb("wq", [P, C, D]), sb("wo", [P, REP, D])
        wk, wv = sb("wk", [P, C, P]), sb("wv", [P, C, P])
        w_low = sb("w_low", [P, C, D])
        wo_by_rep = sb("wo_by_rep", [P, C, D])
        ln_w = sb("ln_w", [P, C])
        gates, tgates = sb("gates", [P, 2]), sb("tgates", [P, 2])
        bias, gated_bias = sb("bias", [P, D]), sb("gated_bias", [P, D])
        planes = sb("planes", [P, 4, C * 16], I32)
        lut = sb("lut", [P, C, ENTRIES])
        bits = sb("bits", [P, 4, C * 16, 32], I32)
        codes = sb("codes", [P, C * D])
        picked = sb("picked", [P, 4, D])
        eps_col, half_col = sb("eps_col", [P, 1]), sb("half_col", [P, 1])
        x_new, ctx_new = sb("x_new", [P, TILES, D]), sb("ctx_new", [P, TILES, D])
        x, xn = sb("x", [P, TILES, D]), sb("xn", [P, TILES, D])
        xnt, ctxt = sb("xnt", [P, C, T]), sb("ctxt", [P, C, T])
        stats, mv = sb("stats", [P, TILES, 6]), sb("mv", [P, TILES, 2])
        small, rstd = sb("small", [P, TILES, 6]), sb("rstd", [P, TILES])

        weights_in, quant_in, small_in = sem("weights_in"), sem("quant_in"), sem("small_in")
        x_loaded, ctx_loaded = sem("x_loaded"), sem("ctx_loaded")
        x_free, ctx_free = sem("x_free"), sem("ctx_free")
        x_stored, ctx_stored = sem("x_stored"), sem("ctx_stored")
        cleared, consts_made, masks_made = sem("cleared"), sem("consts_made"), sem("masks_made")
        wo_ordered = sem("wo_ordered")
        gates_ready, gated_bias_made = sem("gates_ready"), sem("gated_bias_made")
        bits_made, codes_made = sem("bits_made"), sem("codes_made")
        picked_made, picked_used = sem("picked_made"), sem("picked_used")
        a_filled, a_emptied = sem("a_filled"), sem("a_emptied")
        d_filled, d_emptied = sem("d_filled"), sem("d_emptied")
        s_filled, s_emptied, o_filled, o_emptied = heads.s_filled, heads.s_emptied, heads.o_filled, heads.o_emptied
        stats_made, mv_made, rstd_step, rstd_made = sem("stats_made"), sem("mv_made"), sem("rstd_step"), sem("rstd_made")
        xn_made, bias_added = sem("xn_made"), sem("bias_added")
        gate = sem("gate")

        block = ctx.enter_context(nc.Block())

        @block.sync
        def _(sp):
            sp.dma_start(wq_raw[:, :, :], io["L0_xattn_wq"].rearrange("(c p) d -> p c d", p=P)).then_inc(weights_in, DMA)
            sp.dma_start(wk_raw[:, :], io["L0_xattn_wk"]).then_inc(weights_in, DMA)
            sp.dma_start(wv_raw[:, :], io["L0_xattn_wv"]).then_inc(weights_in, DMA)
            sp.dma_start(wo_raw[:, :, :], io["L0_xattn_wo"].rearrange("(c p) d -> p c d", p=P)).then_inc(weights_in, DMA)
            sp.sem_inc(ctx_free, 1)
            sp.sem_inc(x_free, 1)
            with sp.Fori(0, GROUPS) as i:
                sp.wait_ge(ctx_free, i + 1)
                sp.dma_start(ctx_new[:, :, :], ctx_tiles[i]).then_inc(ctx_loaded, DMA)
                sp.wait_ge(x_free, i + 1)
                sp.dma_start(x_new[:, :, :], x_tiles[i]).then_inc(x_loaded, DMA)
            sp.wait_ge(x_stored, 1 + DMA * TILES * GROUPS)
            sp.wait_ge(ctx_stored, 1 + 2 * DMA * GROUPS)

        @block.gpsimd
        def _(pool):
            nc.gpsimd.memset(ident[:, :], 0.0).then_inc(consts_made, 1)
            nc.gpsimd.memset(eps_col[:, :], EPS).then_inc(consts_made, 1)
            nc.gpsimd.memset(half_col[:, :], -0.5).then_inc(consts_made, 1)
            pool.wait_ge(consts_made, 3)
            nc.gpsimd.affine_select(out=ident[:, :], in_=ident[:, :], compare_op=ALU.not_equal, fill=1.0,
                                    base=0, pattern=[[-1, P]], channel_multiplier=1).then_inc(consts_made, 1)
            heads.make_masks(pool, cleared, masks_made)
            pool.wait_ge(weights_in, 4 * DMA)
            for o in range(C):
                for r in range(REP):
                    nc.gpsimd.tensor_copy(heads_by_rep(wo_by_rep[:, o, :])[:, :, r, :],
                                          heads_as_given(wo_raw[:, o, :])[:, :, r, :]).then_inc(wo_ordered, 1)
            pool.wait_ge(small_in, 4 * DMA)
            pool.wait_ge(gates_ready, 1)
            nc.gpsimd.tensor_tensor(gated_bias[:, :], bias[:, :], tgates[:, 1:2].to_broadcast([P, D]), ALU.mult)\
                .then_inc(gated_bias_made, 1)
            pool.wait_ge(gated_bias_made, 1)
            with pool.Fori(0, GROUPS) as i:
                steps = i * 7 * TILES
                for t in range(TILES):
                    s = [small[:, t, k:k + 1] for k in range(6)]
                    var = mv[:, t, 1:2]
                    chain = [(s[0], var, eps_col[:, :], ALU.add), (s[1], s[0], half_col[:, :], ALU.pow),
                             (s[2], s[1], s[1], ALU.mult), (s[3], s[2], var, ALU.mult),
                             (s[4], s[3], eps_col[:, :], ALU.add), (s[5], s[4], half_col[:, :], ALU.pow)]
                    pool.wait_ge(mv_made, i * 2 * TILES + t + 1)
                    for n, (out, in0, in1, op) in enumerate(chain):
                        if n:
                            pool.wait_ge(rstd_step, steps + 6 * t + n)
                        nc.gpsimd.tensor_tensor(out, in0, in1, op).then_inc(rstd_step, 1)
                    pool.wait_ge(rstd_step, steps + 6 * t + 6)
                    nc.gpsimd.tensor_tensor(rstd[:, t:t + 1], s[1], s[5], ALU.mult).then_inc(rstd_made, 1)
                for t in range(TILES):
                    pool.wait_ge(mv_made, i * 2 * TILES + TILES + t + 1)
                    nc.gpsimd.tensor_tensor(small[:, t, 0:1], mv[:, t, 1:2], eps_col[:, :], ALU.add).then_inc(rstd_step, 1)
                    pool.wait_ge(rstd_step, steps + 6 * TILES + t + 1)
                    nc.gpsimd.tensor_tensor(rstd[:, t:t + 1], small[:, t, 0:1], half_col[:, :], ALU.pow)\
                        .then_inc(rstd_made, 1)
                    pool.wait_ge(xn_made, i * 2 * TILES + TILES + t + 1)
                    nc.gpsimd.tensor_tensor(x[:, t, :], x[:, t, :], gated_bias[:, :], ALU.add).then_inc(bias_added, 1)

        @block.scalar
        def _(act):
            act.dma_start(gates[:, 0:1], io["g_xattn"][0:1].partition_broadcast(P)).then_inc(small_in, DMA)
            act.dma_start(gates[:, 1:2], io["g_ffn"][0:1].partition_broadcast(P)).then_inc(small_in, DMA)
            act.dma_start(bias[:, :], io["L0_ffn_bias"].partition_broadcast(P)).then_inc(small_in, DMA)
            act.dma_start(ln_w[:, :], io["L0_xattn_ln_w"].rearrange("(c p) -> p c", p=P),
                          allow_slow_non_contiguous=True).then_inc(small_in, DMA)
            act.dma_start(lut[:, :, :], io["L0_ffn_lut4"].rearrange("(o p) e -> p o e", p=P)).then_inc(quant_in, DMA)
            for n in range(4):
                act.dma_start(planes[:, n, :].rearrange("p (o w) -> p o w", o=C),
                              io["L0_ffn_qweight"][n].rearrange("(o p) w -> p o w", p=P)).then_inc(quant_in, DMA)
            act.sem_inc(a_emptied, 2)
            act.sem_inc(x_stored, 1)
            act.sem_inc(ctx_stored, 1)
            act.wait_ge(small_in, 4 * DMA)
            nc.scalar.activation(tgates[:, :], gates[:, :], ACT.Tanh).then_inc(gates_ready, 1)
            for c in range(C):
                act.wait_ge(a_filled, A.full(None, f"wq{c}"))
                nc.scalar.activation(heads_by_rep(wq[:, c, :]), heads_as_given(A.bank(None, f"wq{c}")[:, :]),
                                     ACT.Copy, scale=ln_w[:, c:c + 1])\
                    .then_inc(a_emptied, 1)
            for label, w in (("wk", wk), ("wv", wv)):
                act.wait_ge(a_filled, A.full(None, label))
                nc.scalar.activation(w[:, :, :], split4(A.bank(None, label)[:, :]), ACT.Copy).then_inc(a_emptied, 1)
            for r in range(REP):
                act.wait_ge(a_filled, A.full(None, f"wo{r}"))
                nc.scalar.activation(wo[:, r, :], A.bank(None, f"wo{r}")[:, :], ACT.Copy).then_inc(a_emptied, 1)
            for o in range(C):
                act.wait_ge(a_filled, A.full(None, f"lut{o}"))
                nc.scalar.activation(w_low[:, :, o * P:(o + 1) * P], split4(A.bank(None, f"lut{o}")[:, :]), ACT.Copy)\
                    .then_inc(a_emptied, 1)

            with act.Fori(0, GROUPS) as i:
                def empty(label, out):
                    src = A.bank(i, label)[:, :]
                    act.wait_ge(a_filled, A.full(i, label))
                    nc.scalar.activation(out, split4(src) if len(out.shape) == 3 else src, ACT.Copy)\
                        .then_inc(a_emptied, 1)

                act.wait_ge(ctx_stored, 1 + 2 * DMA * i)
                for t in range(TILES):
                    empty(f"ctx{t}", ctxt[:, :, t * P:(t + 1) * P])
                act.wait_ge(a_emptied, A.done(i, f"ctx{TILES - 1}"))
                for half in range(2):
                    act.dma_start(ctx_t_out[i * 2 + half], ctxt[:, :, half * T // 2:(half + 1) * T // 2])\
                       .then_inc(ctx_stored, DMA)
                for t in range(TILES):
                    empty(f"xn{t}", xnt[:, :, t * P:(t + 1) * P])
                for r in range(REP):
                    act.wait_ge(a_filled, A.full(i, f"q{r}"))
                    nc.scalar.activation(heads.qt[:, :, r, :], A.bank(i, f"q{r}")[:, :].rearrange("p (b s) -> p b s", b=B),
                                         ACT.Copy).then_inc(a_emptied, 1)
                for s in range(STEPS):
                    if 0 <= s - 1 < UNITS:
                        act.wait_ge(s_emptied, S.done(i, f"s{s - 1}"))
                        heads.act_exp(s - 1).then_inc(heads.exp_made, 1)
                    if 0 <= s - 2 < UNITS:
                        empty(f"pt{s - 2}", heads.probs_t[:, s % 2])
                    if tile_at(s, FN) is not None:
                        t = tile_at(s, FN)
                        empty(f"fn{t}", xnt[:, :, t * P:(t + 1) * P])
                for t in range(TILES):
                    act.wait_ge(d_emptied, Dr.done(i, f"ffn{t}"))
                    act.dma_start(out_tiles[i][:, t, :], x[:, t, :]).then_inc(x_stored, DMA)

        @block.tensor
        def _(pe):
            pe.wait_ge(consts_made, 4)
            pe.wait_ge(weights_in, 4 * DMA)
            for c in range(C):
                pe.wait_ge(a_emptied, A.free(None, f"wq{c}"))
                out = A.bank(None, f"wq{c}")
                for h in range(C):
                    last = nc.tensor.transpose(out[:, h * P:(h + 1) * P], wq_raw[:, h, c * P:(c + 1) * P], ident[:, :])
                last.then_inc(a_filled, 1)
            for label, raw in (("wk", wk_raw), ("wv", wv_raw)):
                pe.wait_ge(a_emptied, A.free(None, label))
                turned(nc, A.bank(None, label), raw, ident).then_inc(a_filled, 1)
            for r in range(REP):
                pe.wait_ge(a_emptied, A.free(None, f"wo{r}"))
                out = A.bank(None, f"wo{r}")
                pe.wait_ge(wo_ordered, C * REP)
                for o in range(C):
                    last = nc.tensor.transpose(out[:, o * P:(o + 1) * P], wo_by_rep[:, o, r * P:(r + 1) * P], ident[:, :])
                last.then_inc(a_filled, 1)
            for o in range(C):
                pe.wait_ge(a_emptied, A.free(None, f"lut{o}"))
                out = A.bank(None, f"lut{o}")
                for e in range(ENTRIES):
                    n = ENTRIES * o + e
                    pe.wait_ge(picked_made, n + 1)
                    for c in range(C):
                        last = nc.tensor.matmul(out[:, c * P:(c + 1) * P], picked[:, n % 4, c * P:(c + 1) * P],
                                                ident[:, :], start=(e == 0 and c == 0), stop=(e == ENTRIES - 1),
                                                skip_group_check=True)
                    last.then_inc(picked_used if e < ENTRIES - 1 else a_filled, 1)

            pe.wait_ge(masks_made, 4)
            with pe.Fori(0, GROUPS) as i:
                pe.wait_ge(ctx_loaded, DMA * (i + 1))
                for t in range(TILES):
                    pe.wait_ge(a_emptied, A.free(i, f"ctx{t}"))
                    turned(nc, A.bank(i, f"ctx{t}"), ctx_new[:, t, :], ident).then_inc(a_filled, 1)
                pe.wait_ge(a_emptied, A.done(i, f"ctx{TILES - 1}"))
                pe.sem_inc(ctx_free, 1)
                pe.wait_ge(d_emptied, Dr.free(i, "k"))
                heads.pe_keys(Dr.bank(i, "k"), wk, ctxt).then_inc(d_filled, 1)
                pe.wait_ge(d_emptied, Dr.free(i, "v"))
                heads.pe_values_in(Dr.bank(i, "v"), wv, ctxt).then_inc(d_filled, 1)
                for t in range(TILES):
                    pe.wait_ge(xn_made, i * 2 * TILES + t + 1)
                    pe.wait_ge(a_emptied, A.free(i, f"xn{t}"))
                    turned(nc, A.bank(i, f"xn{t}"), xn[:, t, :], ident).then_inc(a_filled, 1)
                pe.wait_ge(a_emptied, A.done(i, f"xn{TILES - 1}"))
                for r in range(REP):
                    pe.wait_ge(a_emptied, A.free(i, f"q{r}"))
                    heads.pe_queries(A.bank(i, f"q{r}"), wq, xnt, r).then_inc(a_filled, 1)
                pe.wait_ge(a_emptied, A.done(i, f"q{REP - 1}"))
                pe.wait_ge(d_emptied, Dr.done(i, "k"))
                for s in range(STEPS):
                    if s < UNITS:
                        pe.wait_ge(s_emptied, S.free(i, f"s{s}"))
                        heads.pe_scores(S.bank(i, f"s{s}"), s).then_inc(s_filled, 1)
                    if 0 <= s - 2 < UNITS:
                        u = s - 2
                        pe.wait_ge(heads.exp_made, i * UNITS + u + 1)
                        pe.wait_ge(a_emptied, A.free(i, f"pt{u}"))
                        heads.pe_turn_probs(A.bank(i, f"pt{u}"), u, ident).then_inc(a_filled, 1)
                    if 0 <= s - 3 < UNITS:
                        u = s - 3
                        if u == 0:
                            pe.wait_ge(d_emptied, Dr.done(i, "v"))
                        pe.wait_ge(a_emptied, A.done(i, f"pt{u}"))
                        pe.wait_ge(o_emptied, O.free(i, f"av{u}"))
                        heads.pe_attend(O.bank(i, f"av{u}"), u).then_inc(o_filled, 1)
                    if 0 <= s - 4 < UNITS:
                        u = s - 4
                        pe.wait_ge(o_emptied, O.done(i, f"av{u}"))
                        pe.wait_ge(o_emptied, O.free(i, f"ot{u}"))
                        heads.pe_turn_back(O.bank(i, f"ot{u}"), u, ident).then_inc(o_filled, 1)
                    if tile_at(s, OUT) is not None:
                        t = tile_at(s, OUT)
                        pe.wait_ge(o_emptied, O.done(i, f"ot{4 * t + 3}"))
                        pe.wait_ge(d_emptied, Dr.free(i, f"out{t}"))
                        heads.pe_project(Dr.bank(i, f"out{t}"), t, wo).then_inc(d_filled, 1)
                    if tile_at(s, FN) is not None:
                        t = tile_at(s, FN)
                        pe.wait_ge(xn_made, i * 2 * TILES + TILES + t + 1)
                        pe.wait_ge(a_emptied, A.free(i, f"fn{t}"))
                        turned(nc, A.bank(i, f"fn{t}"), xn[:, t, :], ident).then_inc(a_filled, 1)
                    if tile_at(s, FFN) is not None:
                        t = tile_at(s, FFN)
                        pe.wait_ge(a_emptied, A.done(i, f"fn{t}"))
                        pe.wait_ge(d_emptied, Dr.free(i, f"ffn{t}"))
                        for c in range(C):
                            last = nc.tensor.matmul(Dr.bank(i, f"ffn{t}")[:, :], xnt[:, c, t * P:(t + 1) * P],
                                                    w_low[:, c, :], start=(c == 0), stop=(c == C - 1))
                        last.then_inc(d_filled, 1)

        @block.vector
        def _(dve):
            for emptied in (d_emptied, s_emptied, o_emptied):
                dve.sem_inc(emptied, 2)
            dve.wait_ge(quant_in, 5 * DMA)
            for s in range(32):
                nc.vector.tensor_scalar(bits[:, :, :, s], planes[:, :, :], s, 1,
                                        ALU.logical_shift_right, ALU.bitwise_and).then_inc(bits_made, 1)
            dve.wait_ge(bits_made, 32)
            plane = [bits[:, n].rearrange("p w s -> p (w s)") for n in range(4)]
            nc.vector.scalar_tensor_tensor(out=codes[:, :], in0=plane[3], scalar=2.0, in1=plane[2],
                                           op0=ALU.mult, op1=ALU.add).then_inc(codes_made, 1)
            for n in (1, 0):
                dve.wait_ge(codes_made, 2 - n)
                nc.vector.scalar_tensor_tensor(out=codes[:, :], in0=codes[:, :], scalar=2.0, in1=plane[n],
                                               op0=ALU.mult, op1=ALU.add).then_inc(codes_made, 1)
            dve.wait_ge(codes_made, 3)
            for o in range(C):
                for e in range(ENTRIES):
                    n = ENTRIES * o + e
                    if n >= 4:
                        used = n - 4
                        if used % ENTRIES == ENTRIES - 1:
                            dve.wait_ge(a_filled, A.full(None, f"lut{used // ENTRIES}"))
                        else:
                            dve.wait_ge(picked_used, used - used // ENTRIES + 1)
                    nc.vector.tensor_scalar(picked[:, n % 4, :], codes[:, o * D:(o + 1) * D], float(e),
                                            lut[:, o, e:e + 1], ALU.is_equal, ALU.mult).then_inc(picked_made, 1)
            dve.wait_ge(masks_made, 4)
            dve.wait_ge(gates_ready, 1)

            with dve.Fori(0, GROUPS) as i:
                def statistics(n, t, src):
                    nc.vector.bn_stats(stats[:, t, :], src[:, t, :]).then_inc(stats_made, 1)
                    dve.wait_ge(stats_made, i * 2 * TILES + n * TILES + t + 1)
                    dve.sem_inc(gate, 1)
                    nc.vector.bn_aggr(mv[:, t, :], stats[:, t, :]).then_inc(mv_made, 1)

                def normalise(n, t, src):
                    dve.wait_ge(rstd_made, i * 2 * TILES + n * TILES + t + 1)
                    nc.vector.tensor_scalar(xn[:, t, :], src[:, t, :], mv[:, t, 0:1], rstd[:, t:t + 1],
                                            ALU.subtract, ALU.mult).then_inc(xn_made, 1)

                dve.wait_ge(x_loaded, DMA * (i + 1))
                for t in range(TILES):
                    statistics(0, t, x_new)
                    if t:
                        normalise(0, t - 1, x_new)
                normalise(0, TILES - 1, x_new)
                dve.wait_ge(d_filled, Dr.full(i, "k"))
                heads.dve_spread_keys(Dr.bank(i, "k")).then_inc(d_emptied, 1)
                dve.wait_ge(d_filled, Dr.full(i, "v"))
                heads.dve_spread_values(Dr.bank(i, "v")).then_inc(d_emptied, 1)
                dve.wait_ge(x_stored, 1 + DMA * TILES * i)
                for s in range(STEPS):
                    if s < UNITS:
                        dve.wait_ge(s_filled, S.full(i, f"s{s}"))
                        heads.dve_max(S.bank(i, f"s{s}"), s).then_inc(heads.max_made, 1)
                    if 0 <= s - 3 < UNITS:
                        u = s - 3
                        dve.wait_ge(o_filled, O.full(i, f"av{u}"))
                        heads.dve_inverse(O.bank(i, f"av{u}"), u).then_inc(heads.inv_made, 1)
                    if s < UNITS:
                        dve.wait_ge(heads.max_made, i * UNITS + s + 1)
                        heads.dve_shift(S.bank(i, f"s{s}"), s).then_inc(s_emptied, 1)
                    if 0 <= s - 3 < UNITS:
                        dve.wait_ge(heads.inv_made, i * UNITS + u + 1)
                        heads.dve_norm(O.bank(i, f"av{u}"), u).then_inc(o_emptied, 1)
                    if 0 <= s - 4 < UNITS:
                        dve.wait_ge(o_filled, O.full(i, f"ot{s - 4}"))
                        heads.dve_copy_back(O.bank(i, f"ot{s - 4}"), s - 4).then_inc(o_emptied, 1)
                    if tile_at(s, OUT + 1) is not None:
                        t = tile_at(s, OUT + 1)
                        dve.wait_ge(d_filled, Dr.full(i, f"out{t}"))
                        nc.vector.scalar_tensor_tensor(out=x[:, t, :], in0=Dr.bank(i, f"out{t}")[:, :],
                                                       scalar=tgates[:, 0:1], in1=x_new[:, t, :],
                                                       op0=ALU.mult, op1=ALU.add).then_inc(d_emptied, 1)
                        dve.wait_ge(d_emptied, Dr.done(i, f"out{t}"))
                        if t == TILES - 1:
                            dve.sem_inc(x_free, 1)
                        statistics(1, t, x)
                    if tile_at(s, OUT + 2) is not None:
                        normalise(1, tile_at(s, OUT + 2), x)
                    if tile_at(s, FFN + 1) is not None:
                        t = tile_at(s, FFN + 1)
                        dve.wait_ge(bias_added, i * TILES + t + 1)
                        dve.wait_ge(d_filled, Dr.full(i, f"ffn{t}"))
                        nc.vector.scalar_tensor_tensor(out=x[:, t, :], in0=Dr.bank(i, f"ffn{t}")[:, :],
                                                       scalar=tgates[:, 1:2], in1=x[:, t, :],
                                                       op0=ALU.mult, op1=ALU.add).then_inc(d_emptied, 1)


def latent_attention(nc, io, x_in, ctx_t, x_out):
    B = 4
    T = B * SEQ
    TILES = T // P
    GROUPS = TOKENS // T
    G, PAIRS = 4, 4
    UNITS = G * PAIRS
    KEYS = 2 * SEQ
    SCALE = 128 ** -0.5

    with ExitStack() as ctx:
        chip = Chip(nc, ctx, "l1")
        sb, sem = chip.sb, chip.sem
        a_loop = [f"x{t}" for t in range(TILES)] + ["k0", "v0", "q0"]
        for s in range(UNITS):
            if s + 1 < UNITS:
                a_loop.append(f"q{s + 1}")
                if s % PAIRS == 2 and s // PAIRS + 1 < G:
                    a_loop.append(f"k{s // PAIRS + 1}")
                if s % PAIRS == 3:
                    a_loop.append(f"v{s // PAIRS + 1}")
            a_loop.append(f"pt{s}")
        A = Banks(chip.banks("bank_a"), [], a_loop)
        S = Banks(chip.banks("bank_s"), [], [f"s{u}" for u in range(UNITS)])
        V = Banks(chip.banks("bank_v"), [], [f"av{u}" for u in range(UNITS)])
        y = chip.banks("bank_y")

        x_tiles = x_in.rearrange("(g t p) d -> g p t d", p=P, t=TILES)
        out_tiles = x_out.rearrange("(g t p) d -> g p t d", p=P, t=TILES)

        ident = sb("ident", [P, P])
        wk, wv = sb("wk", [P, C, G * P]), sb("wv", [P, C, G * P])
        wq = [sb(f"wq{g}", [P, C, 8 * P]) for g in range(G)]
        wo = [sb(f"wo{g}", [P, 8, D]) for g in range(G)]
        tgate = sb("tgate", [P, 1])
        eps_col, half_col = sb("eps_col", [P, 1]), sb("half_col", [P, 1])
        xn, x = sb("xn", [P, TILES, D]), sb("x", [P, TILES, D])
        both = sb("both", [P, C, B, 2, SEQ])
        kt, v = sb("kt", [P, 2, B, KEYS]), sb("v", [P, 2, B, P])
        qt = sb("qt", [P, 2, B, 2, SEQ])
        probs, probs_t = sb("probs", [P, 2, B, KEYS]), sb("probs_t", [P, 2, B, P])
        ot = sb("ot", [P, 2, 2, B, SEQ])
        gated = sb("gated", [P, TILES, D])
        neg_max, sums, inv_sum = sb("neg_max", [P, 2, B]), sb("sums", [P, 2, B]), sb("inv_sum", [P, 2, B])
        stats, mv = sb("stats", [P, TILES, 6]), sb("mv", [P, TILES, 2])
        small, rstd = sb("small", [P, TILES]), sb("rstd", [P, TILES])

        kv_in, gate_in = sem("kv_in"), sem("gate_in")
        wq_in, wo_in = [sem(f"wq_in{g}") for g in range(G)], [sem(f"wo_in{g}") for g in range(G)]
        xn_loaded, ctx_loaded, x_loaded, x_stored = sem("xn_loaded"), sem("ctx_loaded"), sem("x_loaded"), sem("x_stored")
        xn_free, ctx_free = sem("xn_free"), sem("ctx_free")
        consts_made, tgate_ready = sem("consts_made"), sem("tgate_ready")
        a_filled, a_emptied = sem("a_filled"), sem("a_emptied")
        s_filled, s_emptied = sem("s_filled"), sem("s_emptied")
        v_filled, v_emptied = sem("v_filled"), sem("v_emptied")
        y_filled, y_emptied = sem("y_filled"), sem("y_emptied")
        stats_made, mv_made, rstd_step, rstd_made = sem("stats_made"), sem("mv_made"), sem("rstd_step"), sem("rstd_made")
        xn_made, x_made = sem("xn_made"), sem("x_made")
        max_made, exp_made, sum_made, inv_made, probs_made = \
            sem("max_made"), sem("exp_made"), sem("sum_made"), sem("inv_made"), sem("probs_made")
        gate = sem("gate")

        block = ctx.enter_context(nc.Block())

        @block.sync
        def _(sp):
            sp.dma_start(wk[:, :, :], io["L1_xattn_Wk"].rearrange("(c p) n -> p c n", p=P)).then_inc(kv_in, DMA)
            sp.dma_start(wv[:, :, :], io["L1_xattn_Wv"].rearrange("(c p) n -> p c n", p=P)).then_inc(kv_in, DMA)
            sp.sem_inc(xn_free, 1)
            sp.sem_inc(ctx_free, 1)
            sp.sem_inc(x_stored, 1)
            with sp.Fori(0, GROUPS) as i:
                sp.wait_ge(xn_free, i + 1)
                sp.dma_start(xn[:, :, :], x_tiles[i]).then_inc(xn_loaded, DMA)
                sp.wait_ge(ctx_free, i + 1)
                for c in range(C):
                    sp.dma_start(both[:, c, :, 0, :], ctx_t[i][:, c, :].rearrange("p (b s) -> p b s", b=B))\
                      .then_inc(ctx_loaded, DMA)
                sp.wait_ge(x_stored, 1 + DMA * TILES * i)
                sp.dma_start(x[:, :, :], x_tiles[i]).then_inc(x_loaded, DMA)
            sp.wait_ge(x_stored, 1 + DMA * TILES * GROUPS)

        @block.gpsimd
        def _(pool):
            nc.gpsimd.memset(ident[:, :], 0.0).then_inc(consts_made, 1)
            nc.gpsimd.memset(eps_col[:, :], EPS).then_inc(consts_made, 1)
            nc.gpsimd.memset(half_col[:, :], -0.5).then_inc(consts_made, 1)
            pool.wait_ge(consts_made, 3)
            nc.gpsimd.affine_select(out=ident[:, :], in_=ident[:, :], compare_op=ALU.not_equal, fill=1.0,
                                    base=0, pattern=[[-1, P]], channel_multiplier=1).then_inc(consts_made, 1)
            with pool.Fori(0, GROUPS) as i:
                for t in range(TILES):
                    pool.wait_ge(mv_made, i * TILES + t + 1)
                    nc.gpsimd.tensor_tensor(small[:, t:t + 1], mv[:, t, 1:2], eps_col[:, :], ALU.add).then_inc(rstd_step, 1)
                    pool.wait_ge(rstd_step, i * TILES + t + 1)
                    nc.gpsimd.tensor_tensor(rstd[:, t:t + 1], small[:, t:t + 1], half_col[:, :], ALU.pow)\
                        .then_inc(rstd_made, 1)
                pool.wait_ge(x_loaded, DMA * (i + 1))
                pool.sem_inc(gate, 1)
                for t in range(TILES):
                    pool.wait_ge(y_emptied, 1 + i * TILES + t + 1)
                    nc.gpsimd.tensor_tensor(x[:, t, :], x[:, t, :], gated[:, t, :], ALU.add).then_inc(x_made, 1)

        @block.scalar
        def _(act):
            act.dma_start(tgate[:, :], io["g_xattn"][1:2].partition_broadcast(P)).then_inc(gate_in, DMA)
            for g in range(G):
                act.dma_start(wq[g][:, :, :], io["L1_xattn_Wq"].rearrange("(c p) n -> p c n", p=P)
                              [:, :, g * 8 * P:(g + 1) * 8 * P]).then_inc(wq_in[g], DMA)
                act.dma_start(wo[g][:, :, :], io["L1_xattn_Wo"].rearrange("(h p) n -> p h n", p=P)
                              [:, 8 * g:8 * g + 8, :]).then_inc(wo_in[g], DMA)
            act.sem_inc(a_emptied, 2)
            act.sem_inc(y_emptied, 1)
            act.wait_ge(gate_in, DMA)
            nc.scalar.activation(tgate[:, :], tgate[:, :], ACT.Tanh).then_inc(tgate_ready, 1)
            act.wait_ge(tgate_ready, 1)
            with act.Fori(0, GROUPS) as i:
                def empty(label, out):
                    src = A.bank(i, label)[:, :]
                    if len(out.shape) == 3:
                        src = src.rearrange("p (b n) -> p b n", b=out.shape[1])
                    act.wait_ge(a_filled, A.full(i, label))
                    nc.scalar.activation(out, src, ACT.Copy).then_inc(a_emptied, 1)

                def empty_queries(u):
                    src = A.bank(i, f"q{u}")[:, :].rearrange("p (h b s) -> p b h s", h=2, b=B)
                    act.wait_ge(a_filled, A.full(i, f"q{u}"))
                    nc.scalar.activation(qt[:, u % 2], src, ACT.Copy).then_inc(a_emptied, 1)

                for t in range(TILES):
                    act.wait_ge(a_filled, A.full(i, f"x{t}"))
                    for b in range(2):
                        last = nc.scalar.activation(both[:, :, 2 * t + b, 1, :],
                                                    split4(A.bank(i, f"x{t}")[:, :])[:, :, b * SEQ:(b + 1) * SEQ], ACT.Copy)
                    last.then_inc(a_emptied, 1)
                empty("k0", kt[:, 0].rearrange("p b k -> p (b k)"))
                empty("v0", v[:, 0].rearrange("p b k -> p (b k)"))
                empty_queries(0)
                for s in range(UNITS):
                    act.wait_ge(s_emptied, S.done(i, f"s{s}"))
                    nc.scalar.activation(probs[:, s % 2], probs[:, s % 2], ACT.Exp, scale=SCALE).then_inc(exp_made, 1)
                    if s + 1 < UNITS:
                        empty_queries(s + 1)
                        g = s // PAIRS + 1
                        if s % PAIRS == 2 and g < G:
                            empty(f"k{g}", kt[:, g % 2].rearrange("p b k -> p (b k)"))
                        if s % PAIRS == 3:
                            empty(f"v{g}", v[:, g % 2].rearrange("p b k -> p (b k)"))
                    empty(f"pt{s}", probs_t[:, s % 2].rearrange("p b k -> p (b k)"))
                for t in range(TILES):
                    act.wait_ge(y_filled, i * TILES + t + 1)
                    nc.scalar.activation(gated[:, t, :], y[t][:, :], ACT.Copy, scale=tgate[:, 0:1]).then_inc(y_emptied, 1)
                for t in range(TILES):
                    act.wait_ge(x_made, i * TILES + t + 1)
                    act.dma_start(out_tiles[i][:, t, :], x[:, t, :]).then_inc(x_stored, DMA)

        @block.tensor
        def _(pe):
            pe.wait_ge(consts_made, 4)
            pe.wait_ge(kv_in, 2 * DMA)
            with pe.Fori(0, GROUPS) as i:
                def keys(g):
                    pe.wait_ge(a_emptied, A.free(i, f"k{g}"))
                    for c in range(C):
                        last = nc.tensor.matmul(A.bank(i, f"k{g}")[:, :], wk[:, c, g * P:(g + 1) * P],
                                                both[:, c].rearrange("p b h s -> p (b h s)"), start=(c == 0), stop=(c == C - 1))
                    last.then_inc(a_filled, 1)

                def values(g):
                    pe.wait_ge(a_emptied, A.free(i, f"v{g}"))
                    for b in range(B):
                        for c in range(C):
                            last = nc.tensor.matmul(A.bank(i, f"v{g}")[:, b * P:(b + 1) * P],
                                                    both[:, c, b].rearrange("p h s -> p (h s)"), wv[:, c, g * P:(g + 1) * P],
                                                    start=(c == 0), stop=(c == C - 1))
                    last.then_inc(a_filled, 1)

                def queries(u):
                    g = u // PAIRS
                    if u % PAIRS == 0:
                        pe.wait_ge(wq_in[g], DMA)
                    pe.wait_ge(a_emptied, A.free(i, f"q{u}"))
                    for h in range(2):
                        col = (2 * (u % PAIRS) + h) * P
                        for c in range(C):
                            last = nc.tensor.matmul(A.bank(i, f"q{u}")[:, h * T:(h + 1) * T], wq[g][:, c, col:col + P],
                                                    both[:, c, :, 1, :], start=(c == 0), stop=(c == C - 1))
                    last.then_inc(a_filled, 1)

                def scores(u):
                    pe.wait_ge(a_emptied, A.done(i, f"q{u}"))
                    pe.wait_ge(s_emptied, S.free(i, f"s{u}"))
                    for b in range(B):
                        last = nc.tensor.matmul(S.bank(i, f"s{u}")[:, b * KEYS:(b + 1) * KEYS],
                                                qt[:, u % 2, b].rearrange("p h s -> p (h s)"), kt[:, u // PAIRS % 2, b, :],
                                                start=True, stop=True)
                    last.then_inc(s_filled, 1)

                def turn_probs(u):
                    pe.wait_ge(probs_made, i * UNITS + u + 1)
                    pe.wait_ge(a_emptied, A.free(i, f"pt{u}"))
                    turned(nc, A.bank(i, f"pt{u}"), probs[:, u % 2].rearrange("p b k -> p (b k)"), ident)\
                        .then_inc(a_filled, 1)

                def attend(u):
                    pe.wait_ge(a_emptied, A.done(i, f"pt{u}"))
                    pe.wait_ge(v_emptied, V.free(i, f"av{u}"))
                    for b in range(B):
                        last = nc.tensor.matmul(V.bank(i, f"av{u}")[:, b * P:(b + 1) * P], v[:, u // PAIRS % 2, b, :],
                                                probs_t[:, u % 2, b, :], start=True, stop=True)
                    last.then_inc(v_filled, 1)

                def project(u):
                    g = u // PAIRS
                    if u % PAIRS == 0:
                        pe.wait_ge(wo_in[g], DMA)
                    if u == 0:
                        pe.wait_ge(y_emptied, 1 + i * TILES)
                    pe.wait_ge(v_emptied, V.done(i, f"av{u}"))
                    for t in range(TILES):
                        for h in range(2):
                            tokens = ot[:, u % 2, h, 2 * t:2 * t + 2, :].rearrange("p b s -> p (b s)")
                            last = nc.tensor.matmul(y[t][:, :], tokens, wo[g][:, 2 * (u % PAIRS) + h, :],
                                                    start=(u == 0 and h == 0), stop=(u == UNITS - 1 and h == 1))
                        if u == UNITS - 1:
                            last.then_inc(y_filled, 1)

                for t in range(TILES):
                    pe.wait_ge(xn_made, i * TILES + t + 1)
                    pe.wait_ge(a_emptied, A.free(i, f"x{t}"))
                    turned(nc, A.bank(i, f"x{t}"), xn[:, t, :], ident).then_inc(a_filled, 1)
                pe.wait_ge(a_emptied, A.done(i, f"x{TILES - 1}"))
                pe.sem_inc(xn_free, 1)
                pe.wait_ge(ctx_loaded, DMA * C * (i + 1))
                keys(0)
                values(0)
                queries(0)
                for s in range(UNITS + 1):
                    if s < UNITS:
                        if s % PAIRS == 0:
                            pe.wait_ge(a_emptied, A.done(i, f"v{s // PAIRS}"))
                            if s // PAIRS == G - 1:
                                pe.sem_inc(ctx_free, 1)
                        scores(s)
                    if s >= 1:
                        attend(s - 1)
                    if s + 1 < UNITS:
                        queries(s + 1)
                        if s % PAIRS == 2 and s // PAIRS + 1 < G:
                            keys(s // PAIRS + 1)
                        if s % PAIRS == 3:
                            values(s // PAIRS + 1)
                    if s < UNITS:
                        turn_probs(s)
                    if s >= 1:
                        project(s - 1)

        @block.vector
        def _(dve):
            dve.sem_inc(s_emptied, 2)
            dve.sem_inc(v_emptied, 2)
            with dve.Fori(0, GROUPS) as i:
                dve.wait_ge(xn_loaded, DMA * (i + 1))
                for t in range(TILES):
                    nc.vector.bn_stats(stats[:, t, :], xn[:, t, :]).then_inc(stats_made, 1)
                for t in range(TILES):
                    dve.wait_ge(stats_made, i * TILES + t + 1)
                    dve.sem_inc(gate, 1)
                    nc.vector.bn_aggr(mv[:, t, :], stats[:, t, :]).then_inc(mv_made, 1)
                for t in range(TILES):
                    dve.wait_ge(rstd_made, i * TILES + t + 1)
                    nc.vector.tensor_scalar(xn[:, t, :], xn[:, t, :], mv[:, t, 0:1], rstd[:, t:t + 1],
                                            ALU.subtract, ALU.mult).then_inc(xn_made, 1)
                for s in range(UNITS + 1):
                    n = s % 2
                    if s < UNITS:
                        scores = S.bank(i, f"s{s}")[:, :].rearrange("p (b k) -> p b k", b=B)
                        dve.wait_ge(s_filled, S.full(i, f"s{s}"))
                        nc.vector.tensor_reduce(neg_max[:, n, :], scores, AX_X, ALU.max, negate=True).then_inc(max_made, 1)
                        dve.wait_ge(max_made, i * UNITS + s + 1)
                        nc.vector.tensor_tensor(probs[:, n], scores, along(neg_max[:, n, :], KEYS), ALU.add)\
                            .then_inc(s_emptied, 1)
                    if s >= 1:
                        dve.wait_ge(v_filled, V.full(i, f"av{s - 1}"))
                        nc.vector.tensor_copy(ot[:, (s - 1) % 2].rearrange("p h b s -> p b h s"),
                                              V.bank(i, f"av{s - 1}")[:, :].rearrange("p (b h s) -> p b h s", b=B, h=2))\
                            .then_inc(v_emptied, 1)
                    if s < UNITS:
                        dve.wait_ge(exp_made, i * UNITS + s + 1)
                        nc.vector.tensor_reduce(sums[:, n, :], probs[:, n], AX_X, ALU.add).then_inc(sum_made, 1)
                        dve.wait_ge(sum_made, i * UNITS + s + 1)
                        nc.vector.reciprocal(inv_sum[:, n, :], sums[:, n, :]).then_inc(inv_made, 1)
                        dve.wait_ge(inv_made, i * UNITS + s + 1)
                        nc.vector.tensor_tensor(probs[:, n], probs[:, n], along(inv_sum[:, n, :], KEYS), ALU.mult)\
                            .then_inc(probs_made, 1)


def window_and_last_layers(nc, io, x_in, ctx_in, ctx_t, x_out):
    TILES = 4
    GROUPS = TOKENS // (TILES * P)
    T = TILES * P
    B = T // SEQ
    W = 16
    LEFT = W // 2
    HEADS2, HD2 = 8, 8
    BH = 2 * HEADS2
    SCALE2 = HD2 ** -0.5
    R0, R1, E = 32, 8, 3
    H3, R3 = 8, 16
    LOW = H3 * R3
    OUT, FN, ROUTE, LOWT, FFN = 7, 10, 11, 14, 16
    POOL_W = (2, 5, 8, 11, 14)
    DVE_W = tuple(w for w in range(W) if w not in POOL_W)
    MACROS = TILES + 3

    def tile_at(s, first):
        return (s - first) // 4 if s >= first and (s - first) % 4 == 0 and (s - first) // 4 < TILES else None

    def is_tile(t):
        return 0 <= t < TILES

    with ExitStack() as ctx:
        chip = Chip(nc, ctx, "l3")
        sb, sem = chip.sb, chip.sem
        region = sb("region", [P, 2 * 4 * W * P])
        at_setup, at_layer3 = Region(region), Region(region)
        heads = HeadsOf16(chip, B, at_layer3.carve)
        UNITS = heads.UNITS
        STEPS = FFN + 2 + 4 * (TILES - 1) + 1

        a_setup = ["gt"] + [f"fold{c}" for c in range(C)] + ["w2", "low_a", "low_r", "low_b", "none"]
        a_loop = ["xa0", "xa1", "q2_0", "k2_0", "v2_0"]
        d_loop = ["f1_0", "f1_1"]
        s_loop, o_loop = [], []
        ln_order = [f"a{t}" for t in range(TILES)] + ["b0", "b1"]
        bias_order = [f"a{t}" for t in range(TILES)] + ["b0", "b1"]
        for m in range(MACROS):
            if is_tile(m):
                s_loop += [f"dots{m}_0", f"dots{m}_1"]
            if is_tile(m - 2):
                o_loop += [f"b{m - 2}_{w}" for w in range(W)]
                d_loop.append(f"y{m - 2}")
                ln_order.append(f"c{m - 2}")
            if is_tile(m + 2):
                a_loop.append(f"xa{m + 2}")
                d_loop.append(f"f1_{m + 2}")
                ln_order.append(f"b{m + 2}")
                bias_order.append(f"b{m + 2}")
            if is_tile(m - 3):
                a_loop.append(f"xc{m - 3}")
                d_loop.append(f"f2_{m - 3}")
                ln_order.append(f"d{m - 3}")
                bias_order.append(f"d{m - 3}")
            if is_tile(m + 1):
                a_loop += [f"q2_{m + 1}", f"k2_{m + 1}", f"v2_{m + 1}"]
        a_loop += [f"xd{t}" for t in range(TILES)] + [f"q{r}" for r in range(REP)]
        d_loop += ["k", "v"]
        ln_order += [f"e{t}" for t in range(TILES)]
        s3, o3 = heads.order(STEPS)
        s_loop += s3
        o_loop += o3
        for s in range(STEPS):
            if 0 <= s - 2 < UNITS:
                a_loop.append(f"pt{s - 2}")
            if tile_at(s, OUT) is not None:
                d_loop.append(f"out{tile_at(s, OUT)}")
            if tile_at(s, FN) is not None:
                a_loop.append(f"xe{tile_at(s, FN)}")
            if tile_at(s, ROUTE) is not None:
                d_loop.append(f"route{tile_at(s, ROUTE)}")
            if tile_at(s, LOWT) is not None:
                a_loop.append(f"lowt{tile_at(s, LOWT)}")
            if tile_at(s, FFN) is not None:
                d_loop.append(f"f3_{tile_at(s, FFN)}")
        if len(a_loop) % 2:
            a_loop.append("none")
        A = Banks(chip.banks("bank_a"), a_setup, a_loop)
        Dr = Banks(chip.banks("bank_d"), [], d_loop)
        S = Banks(chip.banks("bank_s"), [], s_loop)
        O = Banks(chip.banks("bank_o"), [], o_loop)

        def ln(i, label):
            return i * len(ln_order) + ln_order.index(label) + 1

        def biased(i, label):
            return i * len(bias_order) + bias_order.index(label) + 1

        x_tiles = x_in.rearrange("(g t p) d -> g p t d", p=P, t=TILES)
        ctx_tiles = ctx_in.rearrange("(g t p) d -> g p t d", p=P, t=TILES)
        out_tiles = x_out.rearrange("(g t p) d -> g p t d", p=P, t=TILES)

        ident, head_sum = sb("ident", [P, P]), sb("head_sum", [P, BH])
        eps_col, half_col = sb("eps_col", [P, 1]), sb("half_col", [P, 1])
        w_f1, w_f2 = sb("w_f1", [P, C, D]), sb("w_f2", [P, C, D])
        w2, b2 = sb("w2", [P, 4, P]), sb("b2", [P, 4])
        wq, wo = sb("wq", [P, C, D]), sb("wo", [P, REP, D])
        wk, wv = sb("wk", [P, C, P]), sb("wv", [P, C, P])
        bq, bk, bv = sb("bq", [P, REP]), sb("bk", [P, 1]), sb("bv", [P, KV // 2, 2, HD])
        w_low, w_up = sb("w_low", [P, C, LOW + H3]), sb("w_up", [P, D])
        router_bias = sb("router_bias", [P, H3])
        gates, tgates = sb("gates", [P, 6]), sb("tgates", [P, 5])
        f2_gate = sb("f2_gate", [P, 1])
        gated_b1, gated_b2, gated_b3 = sb("gated_b1", [P, D]), sb("gated_b2", [P, 1]), sb("gated_b3", [P, D])

        carve = at_setup.carve
        base_raw, fourier = carve("base_raw", [P, C, D]), carve("fourier", [P, C, D])
        coefs = [carve("coefs0", [P, C, E, R0]), carve("coefs1", [P, C, E, R1])]
        flags = [carve("flags0", [P, C, E, R0 // 4], I32), carve("flags1", [P, C, E, R1 // 4], I32)]
        masked = [carve("masked0", [P, C, E, R0]), carve("masked1", [P, C, E, R1])]
        pair_sum, expert_sum = carve("pair_sum", [P, C, R0 + R1]), carve("expert_sum", [P, C, R0 + R1])
        enc, gt = carve("enc", [P, D]), carve("gt", [P, D])
        w2_raw = carve("w2_raw", [P, 4, P])
        signs_raw = carve("signs_raw", [P, C, D // 4], I32)
        wq_raw = carve("wq_raw", [P, C, D])
        low_raw, router_raw, up_raw = carve("low_raw", [P, D]), carve("router_raw", [P, D]), carve("up_raw", [P, C, P])
        b1_raw, b3_raw = carve("b1_raw", [P, D]), carve("b3_raw", [P, D])

        x, xn, ctx_new = sb("x", [P, TILES, D]), sb("xn", [P, TILES, D]), sb("ctx_new", [P, TILES, D])
        xnt, ctxt = sb("xnt", [P, C, T]), sb("ctxt", [P, C, T])
        stats, mv = sb("stats", [P, TILES, 6]), sb("mv", [P, TILES, 2])
        small, rstd = sb("small", [P, TILES]), sb("rstd", [P, TILES])
        q2 = sb("q2", [P, 2, D])
        k2, v2 = sb("k2", [P, 2, D + W]), sb("v2", [P, 3, D + W])
        prods, prods_pool, values = sb("prods", [P, 4, D]), sb("prods_pool", [P, 2, D]), sb("values", [P, 4, D])
        probs2 = sb("probs2", [P, 2, 2 * BH, W])
        wide = region[:, :].rearrange("p (n t w c) -> p n t w c", n=2, t=4, w=W)
        neg_max2, sums2, inv2 = sb("neg_max2", [P, 2, 2 * BH]), sb("sums2", [P, 2, 2 * BH]), sb("inv2", [P, 2, 2 * BH])
        logits, router_max = sb("logits", [P, 2, H3]), sb("router_max", [P, 2])
        router_sum, router_inv, mix = sb("router_sum", [P, 2]), sb("router_inv", [P, 2]), sb("mix", [P, 2, H3])
        low, low_t = sb("low", [P, 2, H3, R3]), sb("low_t", [P, 2, P])

        w_in, small_in = sem("w_in"), sem("small_in")
        cleared, consts_made, masks_made, raw_cleared = sem("cleared"), sem("consts_made"), sem("masks_made"), sem("raw_cleared")
        gates_ready, gated_made = sem("gates_ready"), sem("gated_made")
        masked_made, pair_made, experts_made, wq_ordered, signs_made = \
            sem("masked_made"), sem("pair_made"), sem("experts_made"), sem("wq_ordered"), sem("signs_made")
        x_loaded = [sem(f"x_loaded{t}") for t in range(TILES)]
        x_stored = [sem(f"x_stored{t}") for t in range(TILES)]
        ctx_loaded, ctx_free = sem("ctx_loaded"), sem("ctx_free")
        a_filled, a_emptied = sem("a_filled"), sem("a_emptied")
        d_filled, d_emptied = sem("d_filled"), sem("d_emptied")
        s_filled, s_emptied, o_filled, o_emptied = heads.s_filled, heads.s_emptied, heads.o_filled, heads.o_emptied
        stats_made, mv_made, rstd_step, rstd_made = sem("stats_made"), sem("mv_made"), sem("rstd_step"), sem("rstd_made")
        xn_made, bias_added = sem("xn_made"), sem("bias_added")
        prods_made, pool_prods_made, prods_used = sem("prods_made"), sem("pool_prods_made"), sem("prods_used")
        max2_made, exp2_made, sum2_made, inv2_made, probs2_made, wide_made = \
            sem("max2_made"), sem("exp2_made"), sem("sum2_made"), sem("inv2_made"), sem("probs2_made"), sem("wide_made")
        logits_made, router_max_made, router_exp_made, router_inv_made, mix_made = \
            sem("logits_made"), sem("router_max_made"), sem("router_exp_made"), sem("router_inv_made"), sem("mix_made")
        gate = sem("gate")

        block = ctx.enter_context(nc.Block())

        @block.sync
        def _(sp):
            def load(out, src):
                sp.dma_start(out, src).then_inc(w_in, DMA)

            load(base_raw, io["L1_ffn_W_base"].rearrange("(c p) d -> p c d", p=P))
            load(fourier, io["fourier"].rearrange("(c p) d -> p c d", p=P))
            for n in range(2):
                for c in range(C):
                    rows = slice(c * P, (c + 1) * P)
                    load(coefs[n][:, c], io[f"L1_ffn_coefs{n}"][:, rows, :].rearrange("e p r -> p e r"))
                    load(flags[n][:, c], io[f"L1_ffn_mask{n}"][:, rows, :].rearrange("e p r -> p e r"))
            load(enc[0:R0, :], io["L1_ffn_enc0"])
            load(enc[R0:R0 + R1, :], io["L1_ffn_enc1"])
            load(wq_raw, io["L3_xattn_Wq"].rearrange("(c p) n -> p c n", p=P))
            load(low_raw, io["L3_ffn_A"].rearrange("h r d -> (h r) d"))
            load(router_raw[0:H3, :], io["L3_ffn_Wr"])
            for c in range(C):
                load(up_raw[:, c].rearrange("p (h r) -> p h r", h=H3),
                     io["L3_ffn_B"][:, c * P:(c + 1) * P, :].rearrange("h p r -> p h r"))
            load(signs_raw, io["L2_ffn_kernel"].rearrange("(c p) f -> p c f", p=P))
            load(wk[:, :, :], io["L3_xattn_Wk"].rearrange("(c p) n -> p c n", p=P))
            load(wv[:, :, :], io["L3_xattn_Wv"].rearrange("(c p) n -> p c n", p=P))
            for k in range(KV):
                load(wo[k * HD:(k + 1) * HD, :, :],
                     io["L3_xattn_Wo"][k * REP * HD:(k + 1) * REP * HD, :].rearrange("(r d) n -> d r n", r=REP))
            sp.wait_ge(raw_cleared, 1)
            for n, name in enumerate("qkvo"):
                for b in range(2):
                    load(w2_raw[b * SEQ:(b + 1) * SEQ, n, b * SEQ:(b + 1) * SEQ], io[f"L2_xattn_W{name}"])
            for t in range(TILES):
                sp.sem_inc(x_stored[t], 1)
            sp.sem_inc(ctx_free, 1)
            with sp.Fori(0, GROUPS) as i:
                for t in range(TILES):
                    sp.wait_ge(x_stored[t], 1 + DMA * i)
                    sp.dma_start(x[:, t, :], x_tiles[i][:, t, :]).then_inc(x_loaded[t], DMA)
                sp.wait_ge(ctx_free, i + 1)
                sp.dma_start(ctx_new[:, :, :], ctx_tiles[i]).then_inc(ctx_loaded, DMA)
                for half in range(2):
                    sp.dma_start(ctxt[:, :, half * T // 2:(half + 1) * T // 2], ctx_t[i * 2 + half])\
                      .then_inc(ctx_loaded, DMA)
            for t in range(TILES):
                sp.wait_ge(x_stored[t], 1 + DMA * GROUPS)

        LOADS = 2 + 4 * C + 2 + 3 + C + 1 + 2 + KV + 8
        SMALL = 6 + 8 + 2 * KV + 4

        @block.gpsimd
        def _(pool):
            nc.gpsimd.memset(w2_raw, 0.0).then_inc(raw_cleared, 1)
            nc.gpsimd.memset(ident[:, :], 0.0).then_inc(consts_made, 1)
            nc.gpsimd.memset(eps_col[:, :], EPS).then_inc(consts_made, 1)
            nc.gpsimd.memset(half_col[:, :], -0.5).then_inc(consts_made, 1)
            nc.gpsimd.memset(k2[:, :, :], 0.0).then_inc(consts_made, 1)
            nc.gpsimd.memset(v2[:, :, :], 0.0).then_inc(consts_made, 1)
            nc.gpsimd.memset(head_sum[:, :], 1.0).then_inc(consts_made, 1)
            pool.wait_ge(consts_made, 6)
            nc.gpsimd.affine_select(out=ident[:, :], in_=ident[:, :], compare_op=ALU.not_equal, fill=1.0,
                                    base=0, pattern=[[-1, P]], channel_multiplier=1).then_inc(consts_made, 1)
            nc.gpsimd.affine_select(out=head_sum[:, :], in_=head_sum[:, :], compare_op=ALU.is_ge, fill=0.0,
                                    base=0, pattern=[[-HD2, BH]], channel_multiplier=1).then_inc(consts_made, 1)
            pool.wait_ge(consts_made, 8)
            nc.gpsimd.affine_select(out=head_sum[:, :], in_=head_sum[:, :], compare_op=ALU.is_ge, fill=0.0,
                                    base=HD2 - 1, pattern=[[HD2, BH]], channel_multiplier=-1).then_inc(consts_made, 1)
            heads.make_masks(pool, cleared, masks_made)
            pool.wait_ge(small_in, SMALL * DMA)
            pool.wait_ge(gates_ready, 1)
            nc.gpsimd.tensor_tensor(gated_b1[:, :], b1_raw, tgates[:, 0:1].to_broadcast([P, D]), ALU.mult)\
                .then_inc(gated_made, 1)
            nc.gpsimd.tensor_tensor(gated_b2[:, :], b2[:, 3:4], tgates[:, 1:2], ALU.mult).then_inc(gated_made, 1)
            nc.gpsimd.tensor_tensor(f2_gate[:, :], gates[:, 5:6], tgates[:, 2:3], ALU.mult).then_inc(gated_made, 1)
            nc.gpsimd.tensor_tensor(gated_b3[:, :], b3_raw, tgates[:, 3:4].to_broadcast([P, D]), ALU.mult)\
                .then_inc(gated_made, 1)
            pool.wait_ge(w_in, LOADS * DMA)
            for c in range(C):
                for r in range(REP):
                    nc.gpsimd.tensor_copy(heads_by_rep(wq[:, c, :])[:, :, r, :], heads_as_given(wq_raw[:, c, :])[:, :, r, :])\
                        .then_inc(wq_ordered, 1)
            pool.wait_ge(gated_made, 4)

            with pool.Fori(0, GROUPS) as i:
                def inverse_deviation(label):
                    t = int(label[-1])
                    pool.wait_ge(mv_made, ln(i, label))
                    nc.gpsimd.tensor_tensor(small[:, t:t + 1], mv[:, t, 1:2], eps_col[:, :], ALU.add).then_inc(rstd_step, 1)
                    pool.wait_ge(rstd_step, ln(i, label))
                    nc.gpsimd.tensor_tensor(rstd[:, t:t + 1], small[:, t:t + 1], half_col[:, :], ALU.pow)\
                        .then_inc(rstd_made, 1)

                def add_bias(label):
                    t = int(label[-1])
                    row = {"a": gated_b1[:, :], "b": gated_b2[:, 0:1].to_broadcast([P, D]), "d": gated_b3[:, :]}[label[0]]
                    pool.wait_ge(xn_made, ln(i, label))
                    nc.gpsimd.tensor_tensor(x[:, t, :], x[:, t, :], row, ALU.add).then_inc(bias_added, 1)

                for t in range(TILES):
                    inverse_deviation(f"a{t}")
                for t in range(TILES):
                    add_bias(f"a{t}")
                for t in range(2):
                    inverse_deviation(f"b{t}")
                for t in range(2):
                    add_bias(f"b{t}")
                for m in range(MACROS):
                    if is_tile(m):
                        for k, w in enumerate(POOL_W):
                            n = m * len(POOL_W) + k
                            if k == 0:
                                pool.wait_ge(a_emptied, A.done(i, f"k2_{m}"))
                            if n >= 2:
                                used, used_w = (n - 2) // len(POOL_W), POOL_W[(n - 2) % len(POOL_W)]
                                pool.wait_ge(prods_used, (i * TILES + used) * (W - 1) + used_w + 1)
                            nc.gpsimd.tensor_tensor(prods_pool[:, n % 2, :], q2[:, m % 2, :], k2[:, m % 2, w:w + D], ALU.mult)\
                                .then_inc(pool_prods_made, 1)
                    for label, t in (("c", m - 2), ("b", m + 2), ("d", m - 3)):
                        if is_tile(t):
                            inverse_deviation(f"{label}{t}")
                    for label, t in (("b", m + 2), ("d", m - 3)):
                        if is_tile(t):
                            add_bias(f"{label}{t}")
                for t in range(TILES):
                    inverse_deviation(f"e{t}")

        @block.scalar
        def _(act):
            def load(out, src, **more):
                act.dma_start(out, src, **more).then_inc(small_in, DMA)

            for n, (name, k) in enumerate((("g_ffn", 1), ("g_xattn", 2), ("g_ffn", 2), ("g_xattn", 3), ("g_ffn", 3),
                                           ("L2_ffn_scale", 0))):
                load(gates[:, n:n + 1], io[name][k:k + 1].partition_broadcast(P))
            for n, name in enumerate("qkvo"):
                for b in range(2):
                    load(b2[b * SEQ:(b + 1) * SEQ, n:n + 1], io[f"L2_xattn_b{name}"].rearrange("(p a) -> p a", a=1))
            for k in range(KV):
                for half in range(2):
                    reps = slice(2 * half, 2 * half + 2)
                    load(bq[k * HD:(k + 1) * HD, reps],
                         io["L3_xattn_bq"][k * REP * HD:(k + 1) * REP * HD].rearrange("(r d) -> d r", r=REP)[:, reps],
                         allow_slow_non_contiguous=True)
            load(bk[:, :], io["L3_xattn_bk"].rearrange("(p a) -> p a", a=1))
            load(bv[:, :, :, :].rearrange("p a h d -> p (a h d)"), io["L3_xattn_bv"].partition_broadcast(P))
            load(b3_raw, io["L3_xattn_bo"].partition_broadcast(P))
            load(b1_raw, io["L1_ffn_b_base"].partition_broadcast(P))
            act.dma_start(router_bias[:, :], io["L3_ffn_br"].partition_broadcast(P)).then_inc(small_in, DMA)
            act.sem_inc(a_emptied, 2)
            act.wait_ge(small_in, (SMALL + 1) * DMA)
            nc.scalar.activation(tgates[:, :], gates[:, 0:5], ACT.Tanh).then_inc(gates_ready, 1)

            def setup_bank(label):
                act.wait_ge(a_filled, A.full(None, label))
                return A.bank(None, label)[:, :]

            nc_act = nc.scalar.activation
            src = setup_bank("gt")
            nc_act(gt[0:R0 + R1, :], src[0:R0 + R1, :], ACT.Copy, scale=0.5).then_inc(a_emptied, 1)
            for c in range(C):
                nc_act(w_f1[:, c, :], setup_bank(f"fold{c}"), ACT.Copy).then_inc(a_emptied, 1)
            nc_act(w2[:, :, :], split4(setup_bank("w2")), ACT.Copy).then_inc(a_emptied, 1)
            nc_act(w_low[:, :, 0:LOW], split4(setup_bank("low_a")), ACT.Copy).then_inc(a_emptied, 1)
            nc_act(w_low[:, :, LOW:LOW + H3], setup_bank("low_r")[:, 0:C * H3].rearrange("p (c h) -> p c h", c=C),
                   ACT.Copy).then_inc(a_emptied, 1)
            nc_act(w_up[:, :], setup_bank("low_b"), ACT.Copy).then_inc(a_emptied, 1)
            act.wait_ge(a_filled, A.full(None, "none"))
            act.sem_inc(a_emptied, 1)

            with act.Fori(0, GROUPS) as i:
                def empty(label, out, bias=None):
                    src = A.bank(i, label)[:, :]
                    act.wait_ge(a_filled, A.full(i, label))
                    if len(out.shape) == 3:
                        src = src.rearrange("p (b n) -> p b n", b=out.shape[1])
                    if bias is None:
                        nc.scalar.activation(out, src, ACT.Copy).then_inc(a_emptied, 1)
                    else:
                        nc.scalar.activation(out, src, ACT.Identity, bias=bias).then_inc(a_emptied, 1)

                def empty_layer2(t):
                    empty(f"q2_{t}", q2[:, t % 2, :], b2[:, 0:1])
                    empty(f"k2_{t}", k2[:, t % 2, LEFT:LEFT + D], b2[:, 1:2])
                    empty(f"v2_{t}", v2[:, t % 3, LEFT:LEFT + D], b2[:, 2:3])

                def chunk(t):
                    return xnt[:, :, t * P:(t + 1) * P]

                empty("xa0", chunk(0))
                empty("xa1", chunk(1))
                empty_layer2(0)
                for m in range(MACROS):
                    if is_tile(m - 1):
                        t = m - 1
                        for half in range(2):
                            act.wait_ge(probs2_made, (i * TILES + t) * 2 + half + 1)
                            for n in range(2):
                                src = probs2[:, half, n * BH:(n + 1) * BH, :].rearrange("p b w -> p w b")\
                                    .unsqueeze(3).to_broadcast([P, W, BH, HD2])
                                out = wide[:, t % 2, 2 * half + n].rearrange("p w (b c) -> p w b c", b=BH)
                                nc.scalar.activation(out, src, ACT.Copy).then_inc(wide_made, 1)
                    if is_tile(m):
                        for half in range(2):
                            act.wait_ge(s_emptied, S.done(i, f"dots{m}_{half}"))
                            nc.scalar.activation(probs2[:, half], probs2[:, half], ACT.Exp, scale=SCALE2).then_inc(exp2_made, 1)
                    if is_tile(m + 2):
                        empty(f"xa{m + 2}", chunk(m + 2))
                    if is_tile(m - 3):
                        empty(f"xc{m - 3}", chunk(m - 3))
                    if is_tile(m + 1):
                        empty_layer2(m + 1)
                for t in range(TILES):
                    empty(f"xd{t}", chunk(t))
                for r in range(REP):
                    empty(f"q{r}", heads.qt[:, :, r, :], bq[:, r:r + 1])
                for s in range(STEPS):
                    if 0 <= s - 1 < UNITS:
                        act.wait_ge(s_emptied, S.done(i, f"s{s - 1}"))
                        heads.act_exp(s - 1).then_inc(heads.exp_made, 1)
                    if 0 <= s - 2 < UNITS:
                        empty(f"pt{s - 2}", heads.probs_t[:, s % 2])
                    if tile_at(s, FN) is not None:
                        empty(f"xe{tile_at(s, FN)}", chunk(tile_at(s, FN)))
                    if tile_at(s, ROUTE + 1) is not None:
                        t = tile_at(s, ROUTE + 1)
                        n = t % 2
                        act.wait_ge(router_max_made, i * TILES + t + 1)
                        nc.scalar.activation(logits[:, n], logits[:, n], ACT.Exp, bias=router_max[:, n:n + 1],
                                             accum_out=router_sum[:, n:n + 1]).then_inc(router_exp_made, 1)
                    if tile_at(s, LOWT) is not None:
                        t = tile_at(s, LOWT)
                        act.wait_ge(a_filled, A.full(i, f"lowt{t}"))
                        nc.scalar.activation(low_t[:, t % 2, :], A.bank(i, f"lowt{t}")[:, 0:P], ACT.Copy).then_inc(a_emptied, 1)
                    if tile_at(s, FFN + 2) is not None:
                        t = tile_at(s, FFN + 2)
                        act.wait_ge(d_emptied, Dr.done(i, f"f3_{t}"))
                        act.dma_start(out_tiles[i][:, t, :], x[:, t, :]).then_inc(x_stored[t], DMA)
                if "none" in a_loop:
                    act.wait_ge(a_filled, A.full(i, "none"))
                    act.sem_inc(a_emptied, 1)

        @block.tensor
        def _(pe):
            pe.wait_ge(consts_made, 9)
            pe.wait_ge(w_in, LOADS * DMA)
            pe.wait_ge(experts_made, 2)
            pe.wait_ge(a_emptied, A.free(None, "gt"))
            for c in range(C):
                last = nc.tensor.matmul(A.bank(None, "gt")[0:R0 + R1, :], expert_sum[:, c, :], fourier[:, c, :],
                                        start=(c == 0), stop=(c == C - 1))
            last.then_inc(a_filled, 1)
            for c in range(C):
                pe.wait_ge(a_emptied, A.free(None, f"fold{c}"))
                if c == 0:
                    pe.wait_ge(a_emptied, A.done(None, "gt"))
                out = A.bank(None, f"fold{c}")
                for o in range(C):
                    nc.tensor.matmul(out[:, o * P:(o + 1) * P], base_raw[:, o, c * P:(c + 1) * P], ident[:, :],
                                     start=(o == 0), stop=False, skip_group_check=True)
                nc.tensor.matmul(out[:, :], enc[0:R0 + R1, c * P:(c + 1) * P], gt[0:R0 + R1, :],
                                 start=False, stop=True, skip_group_check=True).then_inc(a_filled, 1)
            for label, raw, n in (("w2", w2_raw, 4), ("low_a", low_raw, 4), ("low_r", router_raw, 4), ("low_b", up_raw, 4)):
                pe.wait_ge(a_emptied, A.free(None, label))
                out = A.bank(None, label)
                for c in range(n):
                    if label == "low_r":
                        last = nc.tensor.transpose(out[:, c * H3:(c + 1) * H3], raw[0:H3, c * P:(c + 1) * P], ident[0:H3, 0:H3])
                    else:
                        src = raw[:, c * P:(c + 1) * P] if label == "low_a" else raw[:, c, :]
                        last = nc.tensor.transpose(out[:, c * P:(c + 1) * P], src, ident[:, :])
                last.then_inc(a_filled, 1)
            pe.wait_ge(a_emptied, A.done(None, "low_b"))
            pe.sem_inc(a_filled, 1)
            pe.wait_ge(wq_ordered, C * REP)
            pe.wait_ge(signs_made, 1)
            pe.wait_ge(masks_made, 4)

            with pe.Fori(0, GROUPS) as i:
                def turn_x(kind, t):
                    pe.wait_ge(xn_made, ln(i, f"{kind}{t}"))
                    pe.wait_ge(a_emptied, A.free(i, f"x{kind}{t}"))
                    turned(nc, A.bank(i, f"x{kind}{t}"), xn[:, t, :], ident).then_inc(a_filled, 1)

                def feed_forward(label, kind, t, w):
                    pe.wait_ge(a_emptied, A.done(i, f"x{kind}{t}"))
                    pe.wait_ge(d_emptied, Dr.free(i, label))
                    for c in range(C):
                        last = nc.tensor.matmul(Dr.bank(i, label)[:, :], xnt[:, c, t * P:(t + 1) * P], w[:, c, :],
                                                start=(c == 0), stop=(c == C - 1))
                    last.then_inc(d_filled, 1)

                def project_layer2(t):
                    for n, (label, src) in enumerate((("q2", xn), ("k2", ctx_new), ("v2", ctx_new))):
                        if n == 0:
                            pe.wait_ge(xn_made, ln(i, f"b{t}"))
                        pe.wait_ge(a_emptied, A.free(i, f"{label}_{t}"))
                        nc.tensor.matmul(A.bank(i, f"{label}_{t}")[:, :], w2[:, n, :], src[:, t, :],
                                         start=True, stop=True).then_inc(a_filled, 1)

                for t in range(2):
                    turn_x("a", t)
                for t in range(2):
                    feed_forward(f"f1_{t}", "a", t, w_f1)
                pe.wait_ge(ctx_loaded, 3 * DMA * (i + 1))
                project_layer2(0)
                for m in range(MACROS):
                    if is_tile(m):
                        for half in range(2):
                            pe.wait_ge(s_emptied, S.free(i, f"dots{m}_{half}"))
                    if is_tile(m - 2):
                        pe.wait_ge(wide_made, (i * TILES + m - 1) * 4)
                        pe.wait_ge(d_emptied, Dr.free(i, f"y{m - 2}"))
                    for w in range(W + 1):
                        if is_tile(m - 2) and w < W:
                            label = f"b{m - 2}_{w}"
                            pe.wait_ge(o_emptied, O.free(i, label))
                            for c in range(C):
                                last = nc.tensor.transpose(O.bank(i, label)[:, c * P:(c + 1) * P], wide[:, m % 2, c, w, :],
                                                           ident[:, :])
                            last.then_inc(o_filled, 1)
                        if is_tile(m) and w < W:
                            if w in POOL_W:
                                n = m * len(POOL_W) + POOL_W.index(w)
                                pe.wait_ge(pool_prods_made, i * TILES * len(POOL_W) + n + 1)
                                src = prods_pool[:, n % 2, :]
                            else:
                                n = m * len(DVE_W) + DVE_W.index(w)
                                pe.wait_ge(prods_made, i * TILES * len(DVE_W) + n + 1)
                                src = prods[:, n % 4, :]
                            for c in range(C):
                                out = S.bank(i, f"dots{m}_{c // 2}")[:, :].rearrange("p (t b w) -> p t b w", t=2, w=W)
                                last = nc.tensor.matmul(out[:, c % 2, :, w], src[:, c * P:(c + 1) * P], head_sum[:, :],
                                                        start=True, stop=True)
                            if w < W - 1:
                                last.then_inc(prods_used, 1)
                            else:
                                last.then_inc(s_filled, 2)
                        if is_tile(m - 2) and w >= 1:
                            pe.wait_ge(o_emptied, O.done(i, f"b{m - 2}_{w - 1}"))
                            last = nc.tensor.matmul(Dr.bank(i, f"y{m - 2}")[:, :], w2[:, 3, :], values[:, (w - 1) % 4, :],
                                                    start=(w == 1), stop=(w == W))
                            if w == W:
                                last.then_inc(d_filled, 1)
                    if is_tile(m + 2):
                        turn_x("a", m + 2)
                        feed_forward(f"f1_{m + 2}", "a", m + 2, w_f1)
                    if is_tile(m - 3):
                        turn_x("c", m - 3)
                        feed_forward(f"f2_{m - 3}", "c", m - 3, w_f2)
                    if is_tile(m + 1):
                        project_layer2(m + 1)
                pe.wait_ge(d_emptied, Dr.free(i, "k"))
                heads.pe_keys(Dr.bank(i, "k"), wk, ctxt).then_inc(d_filled, 1)
                pe.wait_ge(d_emptied, Dr.free(i, "v"))
                heads.pe_values_in(Dr.bank(i, "v"), wv, ctxt).then_inc(d_filled, 1)
                for t in range(TILES):
                    turn_x("d", t)
                pe.wait_ge(a_emptied, A.done(i, f"xd{TILES - 1}"))
                for r in range(REP):
                    pe.wait_ge(a_emptied, A.free(i, f"q{r}"))
                    heads.pe_queries(A.bank(i, f"q{r}"), wq, xnt, r).then_inc(a_filled, 1)
                pe.wait_ge(a_emptied, A.done(i, f"q{REP - 1}"))
                pe.wait_ge(d_emptied, Dr.done(i, "v"))
                pe.sem_inc(ctx_free, 1)
                for s in range(STEPS):
                    if s < UNITS:
                        pe.wait_ge(s_emptied, S.free(i, f"s{s}"))
                        heads.pe_scores(S.bank(i, f"s{s}"), s).then_inc(s_filled, 1)
                    if 0 <= s - 2 < UNITS:
                        u = s - 2
                        pe.wait_ge(heads.exp_made, i * UNITS + u + 1)
                        pe.wait_ge(a_emptied, A.free(i, f"pt{u}"))
                        heads.pe_turn_probs(A.bank(i, f"pt{u}"), u, ident).then_inc(a_filled, 1)
                    if 0 <= s - 3 < UNITS:
                        u = s - 3
                        pe.wait_ge(a_emptied, A.done(i, f"pt{u}"))
                        pe.wait_ge(o_emptied, O.free(i, f"av{u}"))
                        heads.pe_attend(O.bank(i, f"av{u}"), u).then_inc(o_filled, 1)
                    if 0 <= s - 4 < UNITS:
                        u = s - 4
                        pe.wait_ge(o_emptied, O.done(i, f"av{u}"))
                        pe.wait_ge(o_emptied, O.free(i, f"ot{u}"))
                        heads.pe_turn_back(O.bank(i, f"ot{u}"), u, ident).then_inc(o_filled, 1)
                    if tile_at(s, OUT) is not None:
                        t = tile_at(s, OUT)
                        pe.wait_ge(o_emptied, O.done(i, f"ot{4 * t + 3}"))
                        pe.wait_ge(d_emptied, Dr.free(i, f"out{t}"))
                        heads.pe_project(Dr.bank(i, f"out{t}"), t, wo).then_inc(d_filled, 1)
                    if tile_at(s, FN) is not None:
                        turn_x("e", tile_at(s, FN))
                    if tile_at(s, ROUTE) is not None:
                        t = tile_at(s, ROUTE)
                        pe.wait_ge(a_emptied, A.done(i, f"xe{t}"))
                        pe.wait_ge(d_emptied, Dr.free(i, f"route{t}"))
                        for c in range(C):
                            last = nc.tensor.matmul(Dr.bank(i, f"route{t}")[:, 0:LOW + H3], xnt[:, c, t * P:(t + 1) * P],
                                                    w_low[:, c, :], start=(c == 0), stop=(c == C - 1))
                        last.then_inc(d_filled, 1)
                    if tile_at(s, LOWT) is not None:
                        t = tile_at(s, LOWT)
                        pe.wait_ge(d_emptied, Dr.done(i, f"route{t}"))
                        pe.wait_ge(a_emptied, A.free(i, f"lowt{t}"))
                        nc.tensor.transpose(A.bank(i, f"lowt{t}")[:, 0:P], low[:, t % 2].rearrange("p h r -> p (h r)"),
                                            ident[:, :]).then_inc(a_filled, 1)
                    if tile_at(s, FFN) is not None:
                        t = tile_at(s, FFN)
                        pe.wait_ge(a_emptied, A.done(i, f"lowt{t}"))
                        pe.wait_ge(d_emptied, Dr.free(i, f"f3_{t}"))
                        nc.tensor.matmul(Dr.bank(i, f"f3_{t}")[:, :], low_t[:, t % 2, :], w_up[:, :],
                                         start=True, stop=True).then_inc(d_filled, 1)
                if "none" in a_loop:
                    pe.wait_ge(a_emptied, A.free(i, "none"))
                    pe.sem_inc(a_filled, 1)

        @block.vector
        def _(dve):
            for emptied in (d_emptied, s_emptied, o_emptied):
                dve.sem_inc(emptied, 2)
            dve.wait_ge(w_in, LOADS * DMA)
            for n, r in enumerate((R0, R1)):
                mask = flags[n].bitcast(U8)
                for c in range(C):
                    nc.vector.tensor_tensor(masked[n][:, c], coefs[n][:, c], mask[:, c], ALU.mult).then_inc(masked_made, 1)
            dve.wait_ge(masked_made, 2 * C)
            for n, (lo, r) in enumerate(((0, R0), (R0, R1))):
                nc.vector.tensor_tensor(pair_sum[:, :, lo:lo + r], masked[n][:, :, 0], masked[n][:, :, 1], ALU.add)\
                    .then_inc(pair_made, 1)
            dve.wait_ge(pair_made, 2)
            for n, (lo, r) in enumerate(((0, R0), (R0, R1))):
                nc.vector.tensor_tensor(expert_sum[:, :, lo:lo + r], pair_sum[:, :, lo:lo + r], masked[n][:, :, 2], ALU.add)\
                    .then_inc(experts_made, 1)
            nc.vector.tensor_scalar(w_f2[:, :, :], signs_raw.bitcast(U8), 2.0, -1.0, ALU.mult, ALU.add).then_inc(signs_made, 1)
            dve.wait_ge(masks_made, 4)
            dve.wait_ge(gated_made, 4)

            with dve.Fori(0, GROUPS) as i:
                def statistics(label):
                    t = int(label[-1])
                    nc.vector.bn_stats(stats[:, t, :], x[:, t, :]).then_inc(stats_made, 1)
                    dve.wait_ge(stats_made, ln(i, label))
                    dve.sem_inc(gate, 1)
                    nc.vector.bn_aggr(mv[:, t, :], stats[:, t, :]).then_inc(mv_made, 1)

                def normalise(label):
                    t = int(label[-1])
                    dve.wait_ge(rstd_made, ln(i, label))
                    nc.vector.tensor_scalar(xn[:, t, :], x[:, t, :], mv[:, t, 0:1], rstd[:, t:t + 1],
                                            ALU.subtract, ALU.mult).then_inc(xn_made, 1)

                def residual(label, t, scale, bias=None):
                    if bias is not None:
                        dve.wait_ge(bias_added, biased(i, bias))
                    dve.wait_ge(d_filled, Dr.full(i, label))
                    nc.vector.scalar_tensor_tensor(out=x[:, t, :], in0=Dr.bank(i, label)[:, :], scalar=scale,
                                                   in1=x[:, t, :], op0=ALU.mult, op1=ALU.add).then_inc(d_emptied, 1)
                    dve.wait_ge(d_emptied, Dr.done(i, label))

                def product(m, w):
                    n = m * len(DVE_W) + DVE_W.index(w)
                    if w == 0:
                        dve.wait_ge(a_emptied, A.done(i, f"k2_{m}"))
                    if n >= 4:
                        used, used_w = (n - 4) // len(DVE_W), DVE_W[(n - 4) % len(DVE_W)]
                        if used_w < W - 1:
                            dve.wait_ge(prods_used, (i * TILES + used) * (W - 1) + used_w + 1)
                        else:
                            dve.wait_ge(s_filled, S.full(i, f"dots{used}_1"))
                    nc.vector.tensor_tensor(prods[:, n % 4, :], q2[:, m % 2, :], k2[:, m % 2, w:w + D], ALU.mult)\
                        .then_inc(prods_made, 1)

                for t in range(TILES):
                    dve.wait_ge(x_loaded[t], DMA * (i + 1))
                    statistics(f"a{t}")
                for t in range(TILES):
                    normalise(f"a{t}")
                for t in range(2):
                    residual(f"f1_{t}", t, tgates[:, 0:1], f"a{t}")
                    statistics(f"b{t}")
                for t in range(2):
                    normalise(f"b{t}")
                for m in range(MACROS):
                    if is_tile(m):
                        product(m, 0)
                        product(m, 1)
                    for w in range(W):
                        if is_tile(m) and w + 2 in DVE_W:
                            product(m, w + 2)
                        if is_tile(m - 2):
                            label = f"b{m - 2}_{w}"
                            if w == 0:
                                dve.wait_ge(a_emptied, A.done(i, f"v2_{m - 2}"))
                            dve.wait_ge(o_filled, O.full(i, label))
                            nc.vector.tensor_tensor(values[:, w % 4, :], O.bank(i, label)[:, :],
                                                    v2[:, (m - 2) % 3, w:w + D], ALU.mult).then_inc(o_emptied, 1)
                        if is_tile(m - 1):
                            half, part = w % 2, w // 2
                            count = (i * TILES + m - 1) * 2 + half + 1
                            if part == 0:
                                dve.wait_ge(exp2_made, count)
                                nc.vector.tensor_reduce(sums2[:, half], probs2[:, half], AX_X, ALU.add).then_inc(sum2_made, 1)
                            if part == 1:
                                dve.wait_ge(sum2_made, count)
                                nc.vector.reciprocal(inv2[:, half], sums2[:, half]).then_inc(inv2_made, 1)
                            if part == 2:
                                dve.wait_ge(inv2_made, count)
                                nc.vector.tensor_tensor(probs2[:, half], probs2[:, half], along(inv2[:, half], W), ALU.mult)\
                                    .then_inc(probs2_made, 1)
                    if is_tile(m):
                        for half in range(2):
                            scores = S.bank(i, f"dots{m}_{half}")[:, :].rearrange("p (b w) -> p b w", w=W)
                            if half == 0:
                                dve.wait_ge(s_filled, S.full(i, f"dots{m}_1"))
                            nc.vector.tensor_reduce(neg_max2[:, half], scores, AX_X, ALU.max, negate=True).then_inc(max2_made, 1)
                        if m >= 1:
                            dve.wait_ge(wide_made, (i * TILES + m) * 4)
                        for half in range(2):
                            scores = S.bank(i, f"dots{m}_{half}")[:, :].rearrange("p (b w) -> p b w", w=W)
                            dve.wait_ge(max2_made, (i * TILES + m) * 2 + half + 1)
                            nc.vector.tensor_tensor(probs2[:, half], scores, along(neg_max2[:, half], W), ALU.add)\
                                .then_inc(s_emptied, 1)
                    if is_tile(m - 2):
                        residual(f"y{m - 2}", m - 2, tgates[:, 1:2], f"b{m - 2}")
                        statistics(f"c{m - 2}")
                    if is_tile(m + 2):
                        residual(f"f1_{m + 2}", m + 2, tgates[:, 0:1], f"a{m + 2}")
                        statistics(f"b{m + 2}")
                    if is_tile(m - 3):
                        residual(f"f2_{m - 3}", m - 3, f2_gate[:, 0:1])
                        statistics(f"d{m - 3}")
                    for label, t in (("c", m - 2), ("b", m + 2), ("d", m - 3)):
                        if is_tile(t):
                            normalise(f"{label}{t}")
                dve.wait_ge(d_filled, Dr.full(i, "k"))
                heads.dve_spread_keys(Dr.bank(i, "k"), bk[:, 0:1]).then_inc(d_emptied, 1)
                dve.wait_ge(d_filled, Dr.full(i, "v"))
                heads.dve_spread_values(Dr.bank(i, "v"), bv[:, :, :, :]).then_inc(d_emptied, 1)
                for s in range(STEPS):
                    if s < UNITS:
                        dve.wait_ge(s_filled, S.full(i, f"s{s}"))
                        heads.dve_max(S.bank(i, f"s{s}"), s).then_inc(heads.max_made, 1)
                    if 0 <= s - 3 < UNITS:
                        u = s - 3
                        dve.wait_ge(o_filled, O.full(i, f"av{u}"))
                        heads.dve_inverse(O.bank(i, f"av{u}"), u).then_inc(heads.inv_made, 1)
                    if s < UNITS:
                        dve.wait_ge(heads.max_made, i * UNITS + s + 1)
                        heads.dve_shift(S.bank(i, f"s{s}"), s).then_inc(s_emptied, 1)
                    if 0 <= s - 3 < UNITS:
                        dve.wait_ge(heads.inv_made, i * UNITS + u + 1)
                        heads.dve_norm(O.bank(i, f"av{u}"), u).then_inc(o_emptied, 1)
                    if 0 <= s - 4 < UNITS:
                        dve.wait_ge(o_filled, O.full(i, f"ot{s - 4}"))
                        heads.dve_copy_back(O.bank(i, f"ot{s - 4}"), s - 4).then_inc(o_emptied, 1)
                    if tile_at(s, OUT + 1) is not None:
                        t = tile_at(s, OUT + 1)
                        residual(f"out{t}", t, tgates[:, 3:4], f"d{t}")
                        statistics(f"e{t}")
                    if tile_at(s, OUT + 2) is not None:
                        normalise(f"e{tile_at(s, OUT + 2)}")
                    if tile_at(s, ROUTE + 1) is not None:
                        t = tile_at(s, ROUTE + 1)
                        n = t % 2
                        dve.wait_ge(d_filled, Dr.full(i, f"route{t}"))
                        nc.vector.tensor_tensor(logits[:, n], Dr.bank(i, f"route{t}")[:, LOW:LOW + H3], router_bias[:, :],
                                                ALU.add).then_inc(logits_made, 1)
                        dve.wait_ge(logits_made, i * TILES + t + 1)
                        nc.vector.tensor_reduce(router_max[:, n:n + 1], logits[:, n], AX_X, ALU.max, negate=True)\
                            .then_inc(router_max_made, 1)
                    if tile_at(s, ROUTE + 2) is not None:
                        t = tile_at(s, ROUTE + 2)
                        n = t % 2
                        dve.wait_ge(router_exp_made, i * TILES + t + 1)
                        nc.vector.reciprocal(router_inv[:, n:n + 1], router_sum[:, n:n + 1]).then_inc(router_inv_made, 1)
                        dve.wait_ge(router_inv_made, i * TILES + t + 1)
                        nc.vector.tensor_scalar(mix[:, n], logits[:, n], router_inv[:, n:n + 1], 2.0 * H3,
                                                ALU.mult, ALU.mult).then_inc(mix_made, 1)
                        dve.wait_ge(mix_made, i * TILES + t + 1)
                        nc.vector.tensor_tensor(low[:, n], Dr.bank(i, f"route{t}")[:, 0:LOW].rearrange("p (h r) -> p h r", h=H3),
                                                along(mix[:, n], R3), ALU.mult).then_inc(d_emptied, 1)
                    if tile_at(s, FFN + 2) is not None:
                        residual(f"f3_{tile_at(s, FFN + 2)}", tile_at(s, FFN + 2), tgates[:, 4:5])


UNUSED = ("L0_ffn_lut8",)


def flamingo_layers(nc, io, out):
    ctx_t = nc.dram_tensor("ctx_transposed", (TOKENS // 256, P, C, 256), F32, kind="Internal").ap()
    x_1 = nc.dram_tensor("x_after_layer_0", (TOKENS, D), F32, kind="Internal").ap()
    x_2 = nc.dram_tensor("x_after_latents", (TOKENS, D), F32, kind="Internal").ap()
    cross_attention_and_quantised_ffn(nc, io, io["x"], io["ctx_4096"], x_1, ctx_t)
    latent_attention(nc, io, x_1, ctx_t, x_2)
    window_and_last_layers(nc, io, x_2, io["ctx_4096"], ctx_t, out)


def fourier_rows(n):
    import numpy as np
    j = np.arange(n)
    rows = np.empty((n, n))
    rows[0] = 1 / np.sqrt(n)
    for m in range(1, (n - 1) // 2 + 1):
        rows[2 * m - 1] = np.sqrt(2 / n) * np.cos(2 * np.pi * ((m * j) % n) / n)
        rows[2 * m] = np.sqrt(2 / n) * np.sin(2 * np.pi * ((m * j) % n) / n)
    if n % 2 == 0:
        rows[n - 1] = (-1.0) ** j / np.sqrt(n)
    return rows.astype(np.float32)


def kernel(**inputs):
    import numpy as np
    import concourse.bacc as bacc
    from concourse import mybir as mb
    from concourse.bass_utils import run_bass_kernel_spmd

    nc = bacc.Bacc("TRN2", target_bir_lowering=False, num_devices=1)
    arrays, io = {}, {}
    for name, value in inputs.items():
        if name in UNUSED:
            continue
        a = np.ascontiguousarray(value)
        if a.dtype == np.bool_:
            a = a.view(np.int32)
        if name in ("x", "ctx_4096"):
            a = a.reshape(TOKENS, D)
        if a.ndim == 0:
            a = a.reshape(1)
        arrays[f"in_{name}"] = a
        io[name] = nc.dram_tensor(f"in_{name}", a.shape, mb.dt.from_np(a.dtype), kind="ExternalInput").ap()
    arrays["in_fourier"] = fourier_rows(D)
    io["fourier"] = nc.dram_tensor("in_fourier", (D, D), mb.dt.float32, kind="ExternalInput").ap()
    out = nc.dram_tensor("out_x", (TOKENS, D), mb.dt.float32, kind="ExternalOutput").ap()
    flamingo_layers(nc, io, out)
    result = run_bass_kernel_spmd(nc, [arrays], core_ids=[0])
    return result.results[0]["out_x"].reshape(32, SEQ, D)
```

```python
from contextlib import ExitStack

import concourse.bass as bass
from concourse import mybir

F32 = mybir.dt.float32
I32 = mybir.dt.int32
U8 = mybir.dt.uint8
ALU = mybir.AluOpType
ACT = mybir.ActivationFunctionType
AX_X = mybir.AxisListType.X

P = 128
D = 512
C = D // P
TOKENS = 32 * 64
SEQ = 64
EPS = 1e-5
DMA = 16

KV = 8
HD = 16
REP = 4
ENTRY = 64


def heads_as_given(ap):
    return ap.rearrange("p (k r d) -> p k r d", k=KV, r=REP)


def heads_by_rep(ap):
    return ap.rearrange("p (r k d) -> p k r d", k=KV, r=REP)


class Banks:

    def __init__(self, banks, setup, loop):
        assert len(setup) % 2 == 0 and len(loop) % 2 == 0 and len(set(loop)) == len(loop)
        self.banks, self.setup, self.loop = banks, setup, loop

    def turn(self, i, label):
        if i is None:
            return self.setup.index(label)
        return len(self.setup) + i * len(self.loop) + self.loop.index(label)

    def free(self, i, label):
        return self.turn(i, label) + 1

    def full(self, i, label):
        return self.turn(i, label) + 1

    def done(self, i, label):
        return self.turn(i, label) + 3

    def bank(self, i, label):
        return self.banks[(self.setup if i is None else self.loop).index(label) % 2]


class Chip:

    def __init__(self, nc, ctx, phase):
        self.nc, self.ctx, self.phase = nc, ctx, phase
        self.sems = []
        ctx.callback(self.clear_semaphores)

    def clear_semaphores(self):
        self.nc.clear_and_free_semaphores(self.sems)
        self.nc.all_engine_barrier()

    def sb(self, name, shape, dtype=F32):
        return self.ctx.enter_context(self.nc.sbuf_tensor(f"{self.phase}_{name}", shape, dtype))

    def banks(self, name):
        return [self.ctx.enter_context(self.nc.psum_tensor(f"{self.phase}_{name}{n}", [P, D], F32))
                for n in range(2)]

    def sem(self, name):
        self.sems.append(self.nc.alloc_semaphore(f"{self.phase}_{name}"))
        return self.sems[-1]


def split4(ap):
    return ap.rearrange("p (c n) -> p c n", c=4)


class Region:

    def __init__(self, tensor):
        self.tensor, self.at = tensor, 0

    def carve(self, name, shape, dtype=F32):
        size = 1
        for n in shape[1:]:
            size *= n
        ap = self.tensor[0:shape[0], self.at:self.at + size]
        self.at += size
        assert self.at <= self.tensor.shape[1]
        if dtype != F32:
            ap = ap.bitcast(dtype)
        names = "abcd"[:len(shape) - 1]
        sizes = dict(zip(names[1:], shape[2:]))
        return ap if len(shape) == 2 else ap.rearrange(f"p ({' '.join(names)}) -> p {' '.join(names)}", **sizes)


def along(ap, n):
    return ap.unsqueeze(2).to_broadcast([ap.shape[0], ap.shape[1], n])


def turned(nc, out, src, ident):
    for c in range(C):
        last = nc.tensor.transpose(out[:, c * P:(c + 1) * P], src[:, c * P:(c + 1) * P], ident[:, :])
    return last


class HeadsOf16:

    def __init__(self, chip, batches, shared=None):
        sb, sem = chip.sb, chip.sem
        shared = shared or sb
        T = batches * SEQ
        self.nc, self.B, self.UNITS, self.T = chip.nc, batches, 2 * batches, T
        self.kmask = sb("kmask", [P, KV])
        self.qt, self.kbd = shared("qt", [P, batches, REP, SEQ]), shared("kbd", [P, batches, KV, SEQ])
        self.vbd = sb("vbd", [P, batches, KV // 2, ENTRY])
        self.probs, self.probs_t = shared("probs", [P, 3, KV, SEQ]), shared("probs_t", [P, 2, KV // 2 * P])
        self.neg_max, self.inv_sum = sb("neg_max", [P, 2, KV]), sb("inv_sum", [P, 2, KV // 2, 2])
        self.o_tok, self.ot = sb("o_tok", [P, 2, KV // 2, 2, HD]), shared("ot", [P, REP, T])
        self.s_filled, self.s_emptied = sem("s_filled"), sem("s_emptied")
        self.o_filled, self.o_emptied = sem("o_filled"), sem("o_emptied")
        self.max_made, self.exp_made, self.inv_made = sem("max_made"), sem("exp_made"), sem("inv_made")

    def order(self, steps):
        s_labels = [f"s{u}" for u in range(self.UNITS)]
        o_labels = []
        for s in range(steps):
            if 0 <= s - 3 < self.UNITS:
                o_labels.append(f"av{s - 3}")
            if 0 <= s - 4 < self.UNITS:
                o_labels.append(f"ot{s - 4}")
        return s_labels, o_labels

    def make_masks(self, pool, cleared, made):
        nc = self.nc
        nc.gpsimd.memset(self.kmask[:, :], 1.0).then_inc(cleared, 1)
        nc.gpsimd.memset(self.vbd[:, :, :, :], 0.0).then_inc(cleared, 1)
        pool.wait_ge(cleared, 2)
        nc.gpsimd.affine_select(out=self.kmask[:, :], in_=self.kmask[:, :], compare_op=ALU.is_ge, fill=0.0,
                                base=0, pattern=[[-HD, KV]], channel_multiplier=1).then_inc(made, 1)
        for half in range(2):
            rows = slice(half * SEQ, (half + 1) * SEQ)
            pool.wait_ge(made, 1 + half)
            nc.gpsimd.memset(self.vbd[rows, :, :, 2 * HD + half:2 * HD + half + 1], 1.0).then_inc(made, 1)
        pool.wait_ge(made, 3)
        nc.gpsimd.affine_select(out=self.kmask[:, :], in_=self.kmask[:, :], compare_op=ALU.is_ge, fill=0.0,
                                base=HD - 1, pattern=[[HD, KV]], channel_multiplier=-1).then_inc(made, 1)


    def pe_keys(self, out, wk, ctxt):
        for c in range(C):
            last = self.nc.tensor.matmul(out[:, :], wk[:, c, :], ctxt[:, c, :], start=(c == 0), stop=(c == C - 1))
        return last

    def pe_values_in(self, out, wv, ctxt):
        for t in range(self.T // P):
            for c in range(C):
                last = self.nc.tensor.matmul(out[:, t * P:(t + 1) * P], ctxt[:, c, t * P:(t + 1) * P], wv[:, c, :],
                                             start=(c == 0), stop=(c == C - 1))
        return last

    def pe_queries(self, out, wq, xnt, r):
        for c in range(C):
            last = self.nc.tensor.matmul(out[:, :], wq[:, c, r * P:(r + 1) * P], xnt[:, c, :],
                                         start=(c == 0), stop=(c == C - 1))
        return last

    def pe_scores(self, out, u):
        b, j = u // 2, u % 2
        return self.nc.tensor.matmul(out[:, :], self.qt[:, b, 2 * j:2 * j + 2, :].rearrange("p r s -> p (r s)"),
                                     self.kbd[:, b, :, :], start=True, stop=True)

    def pe_turn_probs(self, out, u, ident):
        return turned(self.nc, out, self.probs[:, u % 3].rearrange("p k s -> p (k s)"), ident)

    def pe_attend(self, out, u):
        for p in range(KV // 2):
            last = self.nc.tensor.matmul(out[:, p * ENTRY:(p + 1) * ENTRY], self.probs_t[:, u % 2, p * P:(p + 1) * P],
                                         self.vbd[:, u // 2, p, :], start=True, stop=True)
        return last

    def pe_turn_back(self, out, u, ident):
        return self.nc.tensor.transpose(out[:, 0:P], self.o_tok[:, u % 2].rearrange("p a b d -> p (a b d)"),
                                        ident[:, :])

    def pe_project(self, out, t, wo):
        for r in range(REP):
            last = self.nc.tensor.matmul(out[:, :], self.ot[:, r, t * P:(t + 1) * P], wo[:, r, :],
                                         start=(r == 0), stop=(r == REP - 1))
        return last


    def dve_spread_keys(self, bank, bk=None):
        for b in range(self.B):
            keys = bank[:, b * SEQ:(b + 1) * SEQ].unsqueeze(1).to_broadcast([P, KV, SEQ])
            mask, out = along(self.kmask[:, :], SEQ), self.kbd[:, b, :, :]
            if bk is None:
                last = self.nc.vector.tensor_tensor(out, keys, mask, ALU.mult)
            else:
                last = self.nc.vector.scalar_tensor_tensor(out=out, in0=keys, scalar=bk, in1=mask,
                                                           op0=ALU.add, op1=ALU.mult)
        return last

    def dve_spread_values(self, bank, bv=None):
        values = bank[:, :].rearrange("p (t a h d) -> p t a h d", a=KV // 2, h=2, d=HD)
        vbd = self.vbd[:, :, :, :].rearrange("p (t b) a e -> p t b a e", b=2)
        for b in range(2):
            keys = slice(b * SEQ, (b + 1) * SEQ)
            for h in range(2):
                for t in range(self.T // P):
                    out = vbd[h * SEQ:(h + 1) * SEQ, t, b, :, h * HD:(h + 1) * HD]
                    if bv is None:
                        last = self.nc.vector.tensor_copy(out, values[keys, t, :, h, :])
                    else:
                        last = self.nc.vector.tensor_tensor(out, values[keys, t, :, h, :], bv[keys, :, h, :], ALU.add)
        return last

    def dve_max(self, bank, u):
        return self.nc.vector.tensor_reduce(self.neg_max[:, u % 2, :], bank[:, :].rearrange("p (k s) -> p k s", k=KV),
                                            AX_X, ALU.max, negate=True)

    def dve_shift(self, bank, u):
        return self.nc.vector.tensor_tensor(self.probs[:, u % 3], bank[:, :].rearrange("p (k s) -> p k s", k=KV),
                                            along(self.neg_max[:, u % 2, :], SEQ), ALU.add)

    def dve_inverse(self, bank, u):
        sums = bank[:, 0:KV // 2 * ENTRY].rearrange("p (a e) -> p a e", e=ENTRY)[:, :, 2 * HD:2 * HD + 2]
        return self.nc.vector.reciprocal(self.inv_sum[:, u % 2], sums)

    def dve_norm(self, bank, u):
        values = bank[:, 0:KV // 2 * ENTRY].rearrange("p (a e) -> p a e", e=ENTRY)
        for h in range(2):
            last = self.nc.vector.tensor_tensor(self.o_tok[:, u % 2, :, h, :], values[:, :, h * HD:(h + 1) * HD],
                                                along(self.inv_sum[:, u % 2, :, h], HD), ALU.mult)
        return last

    def dve_copy_back(self, bank, u):
        b, j = u // 2, u % 2
        return self.nc.vector.tensor_copy(self.ot[:, 2 * j:2 * j + 2, b * SEQ:(b + 1) * SEQ],
                                          bank[:, 0:P].rearrange("p (r s) -> p r s", r=2))


    def act_exp(self, u):
        return self.nc.scalar.activation(self.probs[:, u % 3], self.probs[:, u % 3], ACT.Exp, scale=HD ** -0.5)


def early_latent_memory(early):
    carve = Region(early).carve
    return carve("wk", [P, C, D]), carve("wv", [P, C, D]), carve("wq0", [P, C, 2 * D])


def early_latent_weights(io, early):
    wk, wv, wq0 = early_latent_memory(early)
    return [(wk, io["L1_xattn_Wk"].rearrange("(c p) n -> p c n", p=P)),
            (wv, io["L1_xattn_Wv"].rearrange("(c p) n -> p c n", p=P)),
            (wq0, io["L1_xattn_Wq"].rearrange("(c p) n -> p c n", p=P)[:, :, 0:2 * D])]


def latent_attention(nc, io, x_in, ctx_t, x_out, early):
    B = 4
    T = B * SEQ
    TILES = T // P
    GROUPS = TOKENS // T
    G, PAIRS = 4, 4
    UNITS = G * PAIRS
    KEYS = 2 * SEQ
    SCALE = 128 ** -0.5

    with ExitStack() as ctx:
        chip = Chip(nc, ctx, "l1")
        sb, sem = chip.sb, chip.sem
        a_loop = [f"x{t}" for t in range(TILES)] + ["k0", "v0", "q0"]
        for s in range(UNITS):
            if s + 1 < UNITS:
                a_loop.append(f"q{s + 1}")
                if s % PAIRS == 2 and s // PAIRS + 1 < G:
                    a_loop.append(f"k{s // PAIRS + 1}")
                if s % PAIRS == 3:
                    a_loop.append(f"v{s // PAIRS + 1}")
            a_loop.append(f"pt{s}")
        A = Banks(chip.banks("bank_a"), [], a_loop)
        S = Banks(chip.banks("bank_s"), [], [f"s{u}" for u in range(UNITS)])
        V = Banks(chip.banks("bank_v"), [], [f"av{u}" for u in range(UNITS)])
        y = chip.banks("bank_y")

        x_tiles = x_in.rearrange("(g t p) d -> g p t d", p=P, t=TILES)
        out_tiles = x_out.rearrange("(g t p) d -> g p t d", p=P, t=TILES)

        ident = sb("ident", [P, P])
        wk, wv, wq0 = early_latent_memory(early)
        wq = [wq0] + [sb(f"wq{g}", [P, C, 8 * P]) for g in range(1, G)]
        wo = [sb(f"wo{g}", [P, 8, D]) for g in range(G)]
        tgate = sb("tgate", [P, 1])
        eps_col, half_col = sb("eps_col", [P, 1]), sb("half_col", [P, 1])
        xn, x = sb("xn", [P, TILES, D]), sb("x", [P, TILES, D])
        both = sb("both", [P, C, B, 2, SEQ])
        kt, v = sb("kt", [P, 2, B, KEYS]), sb("v", [P, 2, B, P])
        qt = sb("qt", [P, 2, B, 2, SEQ])
        probs, probs_t = sb("probs", [P, 2, B, KEYS]), sb("probs_t", [P, 2, B, P])
        ot = sb("ot", [P, 2, 2, B, SEQ])
        gated = sb("gated", [P, TILES, D])
        neg_max, sums, inv_sum = sb("neg_max", [P, 2, B]), sb("sums", [P, 2, B]), sb("inv_sum", [P, 2, B])
        stats, mv = sb("stats", [P, TILES, 6]), sb("mv", [P, TILES, 2])
        small, rstd = sb("small", [P, TILES]), sb("rstd", [P, TILES])

        gate_in = sem("gate_in")
        wq_in, wo_in = [sem(f"wq_in{g}") for g in range(G)], [sem(f"wo_in{g}") for g in range(G)]
        xn_loaded, ctx_loaded, x_loaded, x_stored = sem("xn_loaded"), sem("ctx_loaded"), sem("x_loaded"), sem("x_stored")
        xn_free, ctx_free = sem("xn_free"), sem("ctx_free")
        consts_made, tgate_ready = sem("consts_made"), sem("tgate_ready")
        a_filled, a_emptied = sem("a_filled"), sem("a_emptied")
        s_filled, s_emptied = sem("s_filled"), sem("s_emptied")
        v_filled, v_emptied = sem("v_filled"), sem("v_emptied")
        y_filled, y_emptied = sem("y_filled"), sem("y_emptied")
        stats_made, mv_made, rstd_step, rstd_made = sem("stats_made"), sem("mv_made"), sem("rstd_step"), sem("rstd_made")
        xn_made, x_made = sem("xn_made"), sem("x_made")
        max_made, exp_made, sum_made, inv_made, probs_made = \
            sem("max_made"), sem("exp_made"), sem("sum_made"), sem("inv_made"), sem("probs_made")
        gate = sem("gate")

        block = ctx.enter_context(nc.Block())

        @block.sync
        def _(sp):
            sp.sem_inc(xn_free, 1)
            sp.sem_inc(ctx_free, 1)
            sp.sem_inc(x_stored, 1)
            with sp.Fori(0, GROUPS) as i:
                sp.wait_ge(xn_free, i + 1)
                sp.dma_start(xn[:, :, :], x_tiles[i]).then_inc(xn_loaded, DMA)
                sp.wait_ge(ctx_free, i + 1)
                for c in range(C):
                    sp.dma_start(both[:, c, :, 0, :], ctx_t[i][:, c, :].rearrange("p (b s) -> p b s", b=B))\
                      .then_inc(ctx_loaded, DMA)
                sp.wait_ge(x_stored, 1 + DMA * TILES * i)
                sp.dma_start(x[:, :, :], x_tiles[i]).then_inc(x_loaded, DMA)
            sp.wait_ge(x_stored, 1 + DMA * TILES * GROUPS)

        @block.gpsimd
        def _(pool):
            nc.gpsimd.memset(ident[:, :], 0.0).then_inc(consts_made, 1)
            nc.gpsimd.memset(eps_col[:, :], EPS).then_inc(consts_made, 1)
            nc.gpsimd.memset(half_col[:, :], -0.5).then_inc(consts_made, 1)
            pool.wait_ge(consts_made, 3)
            nc.gpsimd.affine_select(out=ident[:, :], in_=ident[:, :], compare_op=ALU.not_equal, fill=1.0,
                                    base=0, pattern=[[-1, P]], channel_multiplier=1).then_inc(consts_made, 1)
            with pool.Fori(0, GROUPS) as i:
                for t in range(TILES):
                    pool.wait_ge(mv_made, i * TILES + t + 1)
                    nc.gpsimd.tensor_tensor(small[:, t:t + 1], mv[:, t, 1:2], eps_col[:, :], ALU.add).then_inc(rstd_step, 1)
                    pool.wait_ge(rstd_step, i * TILES + t + 1)
                    nc.gpsimd.tensor_tensor(rstd[:, t:t + 1], small[:, t:t + 1], half_col[:, :], ALU.pow)\
                        .then_inc(rstd_made, 1)
                pool.wait_ge(x_loaded, DMA * (i + 1))
                pool.sem_inc(gate, 1)
                for t in range(TILES):
                    pool.wait_ge(y_emptied, 1 + i * TILES + t + 1)
                    nc.gpsimd.tensor_tensor(x[:, t, :], x[:, t, :], gated[:, t, :], ALU.add).then_inc(x_made, 1)

        @block.scalar
        def _(act):
            act.dma_start(tgate[:, :], io["g_xattn"][1:2].partition_broadcast(P)).then_inc(gate_in, DMA)
            act.wait_ge(ctx_loaded, DMA * C)
            for g in range(G):
                if g:
                    act.dma_start(wq[g][:, :, :], io["L1_xattn_Wq"].rearrange("(c p) n -> p c n", p=P)
                                  [:, :, g * 8 * P:(g + 1) * 8 * P]).then_inc(wq_in[g], DMA)
                act.dma_start(wo[g][:, :, :], io["L1_xattn_Wo"].rearrange("(h p) n -> p h n", p=P)
                              [:, 8 * g:8 * g + 8, :]).then_inc(wo_in[g], DMA)
            act.sem_inc(a_emptied, 2)
            act.sem_inc(y_emptied, 1)
            act.wait_ge(gate_in, DMA)
            nc.scalar.activation(tgate[:, :], tgate[:, :], ACT.Tanh).then_inc(tgate_ready, 1)
            act.wait_ge(tgate_ready, 1)
            with act.Fori(0, GROUPS) as i:
                def empty(label, out):
                    src = A.bank(i, label)[:, :]
                    if len(out.shape) == 3:
                        src = src.rearrange("p (b n) -> p b n", b=out.shape[1])
                    act.wait_ge(a_filled, A.full(i, label))
                    nc.scalar.activation(out, src, ACT.Copy).then_inc(a_emptied, 1)

                def empty_queries(u):
                    src = A.bank(i, f"q{u}")[:, :].rearrange("p (h b s) -> p b h s", h=2, b=B)
                    act.wait_ge(a_filled, A.full(i, f"q{u}"))
                    nc.scalar.activation(qt[:, u % 2], src, ACT.Copy).then_inc(a_emptied, 1)

                for t in range(TILES):
                    act.wait_ge(a_filled, A.full(i, f"x{t}"))
                    for b in range(2):
                        last = nc.scalar.activation(both[:, :, 2 * t + b, 1, :],
                                                    split4(A.bank(i, f"x{t}")[:, :])[:, :, b * SEQ:(b + 1) * SEQ], ACT.Copy)
                    last.then_inc(a_emptied, 1)
                empty("k0", kt[:, 0].rearrange("p b k -> p (b k)"))
                empty("v0", v[:, 0].rearrange("p b k -> p (b k)"))
                empty_queries(0)
                for s in range(UNITS):
                    act.wait_ge(s_emptied, S.done(i, f"s{s}"))
                    nc.scalar.activation(probs[:, s % 2], probs[:, s % 2], ACT.Exp, scale=SCALE).then_inc(exp_made, 1)
                    if s + 1 < UNITS:
                        empty_queries(s + 1)
                        g = s // PAIRS + 1
                        if s % PAIRS == 2 and g < G:
                            empty(f"k{g}", kt[:, g % 2].rearrange("p b k -> p (b k)"))
                        if s % PAIRS == 3:
                            empty(f"v{g}", v[:, g % 2].rearrange("p b k -> p (b k)"))
                    empty(f"pt{s}", probs_t[:, s % 2].rearrange("p b k -> p (b k)"))
                for t in range(TILES):
                    act.wait_ge(y_filled, i * TILES + t + 1)
                    nc.scalar.activation(gated[:, t, :], y[t][:, :], ACT.Copy, scale=tgate[:, 0:1]).then_inc(y_emptied, 1)
                for t in range(TILES):
                    act.wait_ge(x_made, i * TILES + t + 1)
                    act.dma_start(out_tiles[i][:, t, :], x[:, t, :]).then_inc(x_stored, DMA)

        @block.tensor
        def _(pe):
            pe.wait_ge(consts_made, 4)
            with pe.Fori(0, GROUPS) as i:
                def keys(g):
                    pe.wait_ge(a_emptied, A.free(i, f"k{g}"))
                    for c in range(C):
                        last = nc.tensor.matmul(A.bank(i, f"k{g}")[:, :], wk[:, c, g * P:(g + 1) * P],
                                                both[:, c].rearrange("p b h s -> p (b h s)"), start=(c == 0), stop=(c == C - 1))
                    last.then_inc(a_filled, 1)

                def values(g):
                    pe.wait_ge(a_emptied, A.free(i, f"v{g}"))
                    for b in range(B):
                        for c in range(C):
                            last = nc.tensor.matmul(A.bank(i, f"v{g}")[:, b * P:(b + 1) * P],
                                                    both[:, c, b].rearrange("p h s -> p (h s)"), wv[:, c, g * P:(g + 1) * P],
                                                    start=(c == 0), stop=(c == C - 1))
                    last.then_inc(a_filled, 1)

                def queries(u):
                    g = u // PAIRS
                    if u % PAIRS == 0 and g:
                        pe.wait_ge(wq_in[g], DMA)
                    pe.wait_ge(a_emptied, A.free(i, f"q{u}"))
                    for h in range(2):
                        col = (2 * (u % PAIRS) + h) * P
                        for c in range(C):
                            last = nc.tensor.matmul(A.bank(i, f"q{u}")[:, h * T:(h + 1) * T], wq[g][:, c, col:col + P],
                                                    both[:, c, :, 1, :], start=(c == 0), stop=(c == C - 1))
                    last.then_inc(a_filled, 1)

                def scores(u):
                    pe.wait_ge(a_emptied, A.done(i, f"q{u}"))
                    pe.wait_ge(s_emptied, S.free(i, f"s{u}"))
                    for b in range(B):
                        last = nc.tensor.matmul(S.bank(i, f"s{u}")[:, b * KEYS:(b + 1) * KEYS],
                                                qt[:, u % 2, b].rearrange("p h s -> p (h s)"), kt[:, u // PAIRS % 2, b, :],
                                                start=True, stop=True)
                    last.then_inc(s_filled, 1)

                def turn_probs(u):
                    pe.wait_ge(probs_made, i * UNITS + u + 1)
                    pe.wait_ge(a_emptied, A.free(i, f"pt{u}"))
                    turned(nc, A.bank(i, f"pt{u}"), probs[:, u % 2].rearrange("p b k -> p (b k)"), ident)\
                        .then_inc(a_filled, 1)

                def attend(u):
                    pe.wait_ge(a_emptied, A.done(i, f"pt{u}"))
                    pe.wait_ge(v_emptied, V.free(i, f"av{u}"))
                    for b in range(B):
                        last = nc.tensor.matmul(V.bank(i, f"av{u}")[:, b * P:(b + 1) * P], v[:, u // PAIRS % 2, b, :],
                                                probs_t[:, u % 2, b, :], start=True, stop=True)
                    last.then_inc(v_filled, 1)

                def project(u):
                    g = u // PAIRS
                    if u % PAIRS == 0:
                        pe.wait_ge(wo_in[g], DMA)
                    if u == 0:
                        pe.wait_ge(y_emptied, 1 + i * TILES)
                    pe.wait_ge(v_emptied, V.done(i, f"av{u}"))
                    for t in range(TILES):
                        for h in range(2):
                            tokens = ot[:, u % 2, h, 2 * t:2 * t + 2, :].rearrange("p b s -> p (b s)")
                            last = nc.tensor.matmul(y[t][:, :], tokens, wo[g][:, 2 * (u % PAIRS) + h, :],
                                                    start=(u == 0 and h == 0), stop=(u == UNITS - 1 and h == 1))
                        if u == UNITS - 1:
                            last.then_inc(y_filled, 1)

                for t in range(TILES):
                    pe.wait_ge(xn_made, i * TILES + t + 1)
                    pe.wait_ge(a_emptied, A.free(i, f"x{t}"))
                    turned(nc, A.bank(i, f"x{t}"), xn[:, t, :], ident).then_inc(a_filled, 1)
                pe.wait_ge(a_emptied, A.done(i, f"x{TILES - 1}"))
                pe.sem_inc(xn_free, 1)
                pe.wait_ge(ctx_loaded, DMA * C * (i + 1))
                keys(0)
                values(0)
                queries(0)
                for s in range(UNITS + 1):
                    if s < UNITS:
                        if s % PAIRS == 0:
                            pe.wait_ge(a_emptied, A.done(i, f"v{s // PAIRS}"))
                            if s // PAIRS == G - 1:
                                pe.sem_inc(ctx_free, 1)
                        scores(s)
                    if s >= 1:
                        attend(s - 1)
                    if s + 1 < UNITS:
                        queries(s + 1)
                        if s % PAIRS == 2 and s // PAIRS + 1 < G:
                            keys(s // PAIRS + 1)
                        if s % PAIRS == 3:
                            values(s // PAIRS + 1)
                    if s < UNITS:
                        turn_probs(s)
                    if s >= 1:
                        project(s - 1)

        @block.vector
        def _(dve):
            dve.sem_inc(s_emptied, 2)
            dve.sem_inc(v_emptied, 2)
            with dve.Fori(0, GROUPS) as i:
                dve.wait_ge(xn_loaded, DMA * (i + 1))
                for t in range(TILES):
                    nc.vector.bn_stats(stats[:, t, :], xn[:, t, :]).then_inc(stats_made, 1)
                for t in range(TILES):
                    dve.wait_ge(stats_made, i * TILES + t + 1)
                    dve.sem_inc(gate, 1)
                    nc.vector.bn_aggr(mv[:, t, :], stats[:, t, :]).then_inc(mv_made, 1)
                for t in range(TILES):
                    dve.wait_ge(rstd_made, i * TILES + t + 1)
                    nc.vector.tensor_scalar(xn[:, t, :], xn[:, t, :], mv[:, t, 0:1], rstd[:, t:t + 1],
                                            ALU.subtract, ALU.mult).then_inc(xn_made, 1)
                for s in range(UNITS + 1):
                    n = s % 2
                    if s < UNITS:
                        scores = S.bank(i, f"s{s}")[:, :].rearrange("p (b k) -> p b k", b=B)
                        dve.wait_ge(s_filled, S.full(i, f"s{s}"))
                        nc.vector.tensor_reduce(neg_max[:, n, :], scores, AX_X, ALU.max, negate=True).then_inc(max_made, 1)
                        dve.wait_ge(max_made, i * UNITS + s + 1)
                        nc.vector.tensor_tensor(probs[:, n], scores, along(neg_max[:, n, :], KEYS), ALU.add)\
                            .then_inc(s_emptied, 1)
                    if s >= 1:
                        dve.wait_ge(v_filled, V.full(i, f"av{s - 1}"))
                        nc.vector.tensor_copy(ot[:, (s - 1) % 2].rearrange("p h b s -> p b h s"),
                                              V.bank(i, f"av{s - 1}")[:, :].rearrange("p (b h s) -> p b h s", b=B, h=2))\
                            .then_inc(v_emptied, 1)
                    if s < UNITS:
                        dve.wait_ge(exp_made, i * UNITS + s + 1)
                        nc.vector.tensor_reduce(sums[:, n, :], probs[:, n], AX_X, ALU.add).then_inc(sum_made, 1)
                        dve.wait_ge(sum_made, i * UNITS + s + 1)
                        nc.vector.reciprocal(inv_sum[:, n, :], sums[:, n, :]).then_inc(inv_made, 1)
                        dve.wait_ge(inv_made, i * UNITS + s + 1)
                        nc.vector.tensor_tensor(probs[:, n], probs[:, n], along(inv_sum[:, n, :], KEYS), ALU.mult)\
                            .then_inc(probs_made, 1)


def cross_attention_and_quantised_ffn(nc, io, x_in, ctx_in, x_out, ctx_t_out, early):
    TILES = 4
    GROUPS = TOKENS // (TILES * P)
    T = TILES * P
    B = T // SEQ
    OUT, FN, FFN = 7, 10, 11
    ENTRIES = 16

    def tile_at(s, first):
        return (s - first) // 4 if s >= first and (s - first) % 4 == 0 and (s - first) // 4 < TILES else None

    with ExitStack() as ctx:
        chip = Chip(nc, ctx, "l0")
        sb, sem = chip.sb, chip.sem
        heads = HeadsOf16(chip, B)
        UNITS = heads.UNITS
        STEPS = UNITS + 9
        s_loop, o_loop = heads.order(STEPS)
        a_loop = [f"ctx{t}" for t in range(TILES)] + [f"xn{t}" for t in range(TILES)] + [f"q{r}" for r in range(REP)]
        d_loop = ["k", "v"]
        for s in range(STEPS):
            if 0 <= s - 2 < UNITS:
                a_loop.append(f"pt{s - 2}")
            if tile_at(s, OUT) is not None:
                d_loop.append(f"out{tile_at(s, OUT)}")
            if tile_at(s, FN) is not None:
                a_loop.append(f"fn{tile_at(s, FN)}")
            if tile_at(s, FFN) is not None:
                d_loop.append(f"ffn{tile_at(s, FFN)}")
        a_setup = [f"wq{c}" for c in range(C)] + ["wk", "wv"] + [f"wo{r}" for r in range(REP)] + \
                  [f"lut{o}" for o in range(C)]
        A = Banks(chip.banks("bank_a"), a_setup, a_loop)
        Dr = Banks(chip.banks("bank_d"), [], d_loop)
        S = Banks(chip.banks("bank_s"), [], s_loop)
        O = Banks(chip.banks("bank_o"), [], o_loop)

        x_tiles = x_in.rearrange("(g t p) d -> g p t d", p=P, t=TILES)
        ctx_tiles = ctx_in.rearrange("(g t p) d -> g p t d", p=P, t=TILES)
        out_tiles = x_out.rearrange("(g t p) d -> g p t d", p=P, t=TILES)

        ident = sb("ident", [P, P])
        xn, wo_raw = sb("xn", [P, TILES, D]), sb("wo_raw", [P, C, D])
        wq_raw = xn
        wk_raw, wv_raw = sb("wk_raw", [P, D]), sb("wv_raw", [P, D])
        wq, wo = sb("wq", [P, C, D]), sb("wo", [P, REP, D])
        wk, wv = sb("wk", [P, C, P]), sb("wv", [P, C, P])
        w_low = sb("w_low", [P, C, D])
        wo_by_rep = sb("wo_by_rep", [P, C, D])
        ln_w = sb("ln_w", [P, C])
        gates, tgates = sb("gates", [P, 2]), sb("tgates", [P, 2])
        bias, gated_bias = sb("bias", [P, D]), sb("gated_bias", [P, D])
        planes = sb("planes", [P, 4, C * 16], I32)
        lut = sb("lut", [P, C, ENTRIES])
        bits = Region(early).carve("bits", [P, 4, C * 16, 32], I32)
        codes = sb("codes", [P, C * D])
        picked = sb("picked", [P, 4, D])
        eps_col, half_col = sb("eps_col", [P, 1]), sb("half_col", [P, 1])
        x_new, ctx_new = sb("x_new", [P, TILES, D]), sb("ctx_new", [P, TILES, D])
        x = sb("x", [P, TILES, D])
        xnt, ctxt = sb("xnt", [P, C, T]), sb("ctxt", [P, C, T])
        stats, mv = sb("stats", [P, TILES, 6]), sb("mv", [P, TILES, 2])
        small, rstd = sb("small", [P, TILES, 6]), sb("rstd", [P, TILES])

        weights_in, quant_in, small_in = sem("weights_in"), sem("quant_in"), sem("small_in")
        x_loaded, ctx_loaded = sem("x_loaded"), sem("ctx_loaded")
        x_free, ctx_free = sem("x_free"), sem("ctx_free")
        x_stored, ctx_stored = sem("x_stored"), sem("ctx_stored")
        cleared, consts_made, masks_made = sem("cleared"), sem("consts_made"), sem("masks_made")
        wo_ordered = sem("wo_ordered")
        gates_ready, gated_bias_made = sem("gates_ready"), sem("gated_bias_made")
        bits_made, codes_made, early_in = sem("bits_made"), sem("codes_made"), sem("early_in")
        picked_made, picked_used = sem("picked_made"), sem("picked_used")
        a_filled, a_emptied = sem("a_filled"), sem("a_emptied")
        d_filled, d_emptied = sem("d_filled"), sem("d_emptied")
        s_filled, s_emptied, o_filled, o_emptied = heads.s_filled, heads.s_emptied, heads.o_filled, heads.o_emptied
        stats_made, mv_made, rstd_step, rstd_made = sem("stats_made"), sem("mv_made"), sem("rstd_step"), sem("rstd_made")
        xn_made, bias_added = sem("xn_made"), sem("bias_added")
        gate = sem("gate")

        block = ctx.enter_context(nc.Block())

        @block.sync
        def _(sp):
            sp.dma_start(wq_raw[:, :, :], io["L0_xattn_wq"].rearrange("(c p) d -> p c d", p=P)).then_inc(weights_in, DMA)
            sp.dma_start(wk_raw[:, :], io["L0_xattn_wk"]).then_inc(weights_in, DMA)
            sp.dma_start(wv_raw[:, :], io["L0_xattn_wv"]).then_inc(weights_in, DMA)
            sp.dma_start(wo_raw[:, :, :], io["L0_xattn_wo"].rearrange("(c p) d -> p c d", p=P)).then_inc(weights_in, DMA)
            sp.sem_inc(ctx_free, 1)
            sp.sem_inc(x_free, 1)
            with sp.Fori(0, GROUPS) as i:
                sp.wait_ge(ctx_free, i + 1)
                sp.dma_start(ctx_new[:, :, :], ctx_tiles[i]).then_inc(ctx_loaded, DMA)
                sp.wait_ge(x_free, i + 1)
                sp.dma_start(x_new[:, :, :], x_tiles[i]).then_inc(x_loaded, DMA)
            sp.wait_ge(codes_made, 3)
            loads = early_latent_weights(io, early)
            for out, src in loads:
                sp.dma_start(out, src).then_inc(early_in, DMA)
            sp.wait_ge(early_in, DMA * len(loads))
            sp.wait_ge(x_stored, 1 + DMA * TILES * GROUPS)
            sp.wait_ge(ctx_stored, 1 + 2 * DMA * GROUPS)

        @block.gpsimd
        def _(pool):
            nc.gpsimd.memset(ident[:, :], 0.0).then_inc(consts_made, 1)
            nc.gpsimd.memset(eps_col[:, :], EPS).then_inc(consts_made, 1)
            nc.gpsimd.memset(half_col[:, :], -0.5).then_inc(consts_made, 1)
            pool.wait_ge(consts_made, 3)
            nc.gpsimd.affine_select(out=ident[:, :], in_=ident[:, :], compare_op=ALU.not_equal, fill=1.0,
                                    base=0, pattern=[[-1, P]], channel_multiplier=1).then_inc(consts_made, 1)
            heads.make_masks(pool, cleared, masks_made)
            pool.wait_ge(weights_in, 4 * DMA)
            for o in range(C):
                for r in range(REP):
                    nc.gpsimd.tensor_copy(heads_by_rep(wo_by_rep[:, o, :])[:, :, r, :],
                                          heads_as_given(wo_raw[:, o, :])[:, :, r, :]).then_inc(wo_ordered, 1)
            pool.wait_ge(small_in, 4 * DMA)
            pool.wait_ge(gates_ready, 1)
            nc.gpsimd.tensor_tensor(gated_bias[:, :], bias[:, :], tgates[:, 1:2].to_broadcast([P, D]), ALU.mult)\
                .then_inc(gated_bias_made, 1)
            pool.wait_ge(gated_bias_made, 1)
            with pool.Fori(0, GROUPS) as i:
                steps = i * 7 * TILES
                for t in range(TILES):
                    s = [small[:, t, k:k + 1] for k in range(6)]
                    var = mv[:, t, 1:2]
                    chain = [(s[0], var, eps_col[:, :], ALU.add), (s[1], s[0], half_col[:, :], ALU.pow),
                             (s[2], s[1], s[1], ALU.mult), (s[3], s[2], var, ALU.mult),
                             (s[4], s[3], eps_col[:, :], ALU.add), (s[5], s[4], half_col[:, :], ALU.pow)]
                    pool.wait_ge(mv_made, i * 2 * TILES + t + 1)
                    for n, (out, in0, in1, op) in enumerate(chain):
                        if n:
                            pool.wait_ge(rstd_step, steps + 6 * t + n)
                        nc.gpsimd.tensor_tensor(out, in0, in1, op).then_inc(rstd_step, 1)
                    pool.wait_ge(rstd_step, steps + 6 * t + 6)
                    nc.gpsimd.tensor_tensor(rstd[:, t:t + 1], s[1], s[5], ALU.mult).then_inc(rstd_made, 1)
                for t in range(TILES):
                    pool.wait_ge(mv_made, i * 2 * TILES + TILES + t + 1)
                    nc.gpsimd.tensor_tensor(small[:, t, 0:1], mv[:, t, 1:2], eps_col[:, :], ALU.add).then_inc(rstd_step, 1)
                    pool.wait_ge(rstd_step, steps + 6 * TILES + t + 1)
                    nc.gpsimd.tensor_tensor(rstd[:, t:t + 1], small[:, t, 0:1], half_col[:, :], ALU.pow)\
                        .then_inc(rstd_made, 1)
                    pool.wait_ge(xn_made, i * 2 * TILES + TILES + t + 1)
                    nc.gpsimd.tensor_tensor(x[:, t, :], x[:, t, :], gated_bias[:, :], ALU.add).then_inc(bias_added, 1)

        @block.scalar
        def _(act):
            act.dma_start(gates[:, 0:1], io["g_xattn"][0:1].partition_broadcast(P)).then_inc(small_in, DMA)
            act.dma_start(gates[:, 1:2], io["g_ffn"][0:1].partition_broadcast(P)).then_inc(small_in, DMA)
            act.dma_start(bias[:, :], io["L0_ffn_bias"].partition_broadcast(P)).then_inc(small_in, DMA)
            act.dma_start(ln_w[:, :], io["L0_xattn_ln_w"].rearrange("(c p) -> p c", p=P),
                          allow_slow_non_contiguous=True).then_inc(small_in, DMA)
            act.dma_start(lut[:, :, :], io["L0_ffn_lut4"].rearrange("(o p) e -> p o e", p=P)).then_inc(quant_in, DMA)
            for n in range(4):
                act.dma_start(planes[:, n, :].rearrange("p (o w) -> p o w", o=C),
                              io["L0_ffn_qweight"][n].rearrange("(o p) w -> p o w", p=P)).then_inc(quant_in, DMA)
            act.sem_inc(a_emptied, 2)
            act.sem_inc(x_stored, 1)
            act.sem_inc(ctx_stored, 1)
            act.wait_ge(small_in, 4 * DMA)
            nc.scalar.activation(tgates[:, :], gates[:, :], ACT.Tanh).then_inc(gates_ready, 1)
            for c in range(C):
                act.wait_ge(a_filled, A.full(None, f"wq{c}"))
                nc.scalar.activation(heads_by_rep(wq[:, c, :]), heads_as_given(A.bank(None, f"wq{c}")[:, :]),
                                     ACT.Copy, scale=ln_w[:, c:c + 1])\
                    .then_inc(a_emptied, 1)
            for label, w in (("wk", wk), ("wv", wv)):
                act.wait_ge(a_filled, A.full(None, label))
                nc.scalar.activation(w[:, :, :], split4(A.bank(None, label)[:, :]), ACT.Copy).then_inc(a_emptied, 1)
            for r in range(REP):
                act.wait_ge(a_filled, A.full(None, f"wo{r}"))
                nc.scalar.activation(wo[:, r, :], A.bank(None, f"wo{r}")[:, :], ACT.Copy).then_inc(a_emptied, 1)
            for o in range(C):
                act.wait_ge(a_filled, A.full(None, f"lut{o}"))
                nc.scalar.activation(w_low[:, :, o * P:(o + 1) * P], split4(A.bank(None, f"lut{o}")[:, :]), ACT.Copy)\
                    .then_inc(a_emptied, 1)

            with act.Fori(0, GROUPS) as i:
                def empty(label, out):
                    src = A.bank(i, label)[:, :]
                    act.wait_ge(a_filled, A.full(i, label))
                    nc.scalar.activation(out, split4(src) if len(out.shape) == 3 else src, ACT.Copy)\
                        .then_inc(a_emptied, 1)

                act.wait_ge(ctx_stored, 1 + 2 * DMA * i)
                for t in range(TILES):
                    empty(f"ctx{t}", ctxt[:, :, t * P:(t + 1) * P])
                act.wait_ge(a_emptied, A.done(i, f"ctx{TILES - 1}"))
                for half in range(2):
                    act.dma_start(ctx_t_out[i * 2 + half], ctxt[:, :, half * T // 2:(half + 1) * T // 2])\
                       .then_inc(ctx_stored, DMA)
                for t in range(TILES):
                    empty(f"xn{t}", xnt[:, :, t * P:(t + 1) * P])
                for r in range(REP):
                    act.wait_ge(a_filled, A.full(i, f"q{r}"))
                    nc.scalar.activation(heads.qt[:, :, r, :], A.bank(i, f"q{r}")[:, :].rearrange("p (b s) -> p b s", b=B),
                                         ACT.Copy).then_inc(a_emptied, 1)
                for s in range(STEPS):
                    if 0 <= s - 1 < UNITS:
                        act.wait_ge(s_emptied, S.done(i, f"s{s - 1}"))
                        heads.act_exp(s - 1).then_inc(heads.exp_made, 1)
                    if 0 <= s - 2 < UNITS:
                        empty(f"pt{s - 2}", heads.probs_t[:, s % 2])
                    if tile_at(s, FN) is not None:
                        t = tile_at(s, FN)
                        empty(f"fn{t}", xnt[:, :, t * P:(t + 1) * P])
                for t in range(TILES):
                    act.wait_ge(d_emptied, Dr.done(i, f"ffn{t}"))
                    act.dma_start(out_tiles[i][:, t, :], x[:, t, :]).then_inc(x_stored, DMA)

        @block.tensor
        def _(pe):
            pe.wait_ge(consts_made, 4)
            pe.wait_ge(weights_in, 4 * DMA)
            for c in range(C):
                pe.wait_ge(a_emptied, A.free(None, f"wq{c}"))
                out = A.bank(None, f"wq{c}")
                for h in range(C):
                    last = nc.tensor.transpose(out[:, h * P:(h + 1) * P], wq_raw[:, h, c * P:(c + 1) * P], ident[:, :])
                last.then_inc(a_filled, 1)
            for label, raw in (("wk", wk_raw), ("wv", wv_raw)):
                pe.wait_ge(a_emptied, A.free(None, label))
                turned(nc, A.bank(None, label), raw, ident).then_inc(a_filled, 1)
            for r in range(REP):
                pe.wait_ge(a_emptied, A.free(None, f"wo{r}"))
                out = A.bank(None, f"wo{r}")
                pe.wait_ge(wo_ordered, C * REP)
                for o in range(C):
                    last = nc.tensor.transpose(out[:, o * P:(o + 1) * P], wo_by_rep[:, o, r * P:(r + 1) * P], ident[:, :])
                last.then_inc(a_filled, 1)
            for o in range(C):
                pe.wait_ge(a_emptied, A.free(None, f"lut{o}"))
                out = A.bank(None, f"lut{o}")
                for e in range(ENTRIES):
                    n = ENTRIES * o + e
                    pe.wait_ge(picked_made, n + 1)
                    for c in range(C):
                        last = nc.tensor.matmul(out[:, c * P:(c + 1) * P], picked[:, n % 4, c * P:(c + 1) * P],
                                                ident[:, :], start=(e == 0 and c == 0), stop=(e == ENTRIES - 1),
                                                skip_group_check=True)
                    last.then_inc(picked_used if e < ENTRIES - 1 else a_filled, 1)

            pe.wait_ge(masks_made, 4)
            with pe.Fori(0, GROUPS) as i:
                pe.wait_ge(ctx_loaded, DMA * (i + 1))
                for t in range(TILES):
                    pe.wait_ge(a_emptied, A.free(i, f"ctx{t}"))
                    turned(nc, A.bank(i, f"ctx{t}"), ctx_new[:, t, :], ident).then_inc(a_filled, 1)
                pe.wait_ge(a_emptied, A.done(i, f"ctx{TILES - 1}"))
                pe.sem_inc(ctx_free, 1)
                pe.wait_ge(d_emptied, Dr.free(i, "k"))
                heads.pe_keys(Dr.bank(i, "k"), wk, ctxt).then_inc(d_filled, 1)
                pe.wait_ge(d_emptied, Dr.free(i, "v"))
                heads.pe_values_in(Dr.bank(i, "v"), wv, ctxt).then_inc(d_filled, 1)
                for t in range(TILES):
                    pe.wait_ge(xn_made, i * 2 * TILES + t + 1)
                    pe.wait_ge(a_emptied, A.free(i, f"xn{t}"))
                    turned(nc, A.bank(i, f"xn{t}"), xn[:, t, :], ident).then_inc(a_filled, 1)
                pe.wait_ge(a_emptied, A.done(i, f"xn{TILES - 1}"))
                for r in range(REP):
                    pe.wait_ge(a_emptied, A.free(i, f"q{r}"))
                    heads.pe_queries(A.bank(i, f"q{r}"), wq, xnt, r).then_inc(a_filled, 1)
                pe.wait_ge(a_emptied, A.done(i, f"q{REP - 1}"))
                pe.wait_ge(d_emptied, Dr.done(i, "k"))
                for s in range(STEPS):
                    if s < UNITS:
                        pe.wait_ge(s_emptied, S.free(i, f"s{s}"))
                        heads.pe_scores(S.bank(i, f"s{s}"), s).then_inc(s_filled, 1)
                    if 0 <= s - 2 < UNITS:
                        u = s - 2
                        pe.wait_ge(heads.exp_made, i * UNITS + u + 1)
                        pe.wait_ge(a_emptied, A.free(i, f"pt{u}"))
                        heads.pe_turn_probs(A.bank(i, f"pt{u}"), u, ident).then_inc(a_filled, 1)
                    if 0 <= s - 3 < UNITS:
                        u = s - 3
                        if u == 0:
                            pe.wait_ge(d_emptied, Dr.done(i, "v"))
                        pe.wait_ge(a_emptied, A.done(i, f"pt{u}"))
                        pe.wait_ge(o_emptied, O.free(i, f"av{u}"))
                        heads.pe_attend(O.bank(i, f"av{u}"), u).then_inc(o_filled, 1)
                    if 0 <= s - 4 < UNITS:
                        u = s - 4
                        pe.wait_ge(o_emptied, O.done(i, f"av{u}"))
                        pe.wait_ge(o_emptied, O.free(i, f"ot{u}"))
                        heads.pe_turn_back(O.bank(i, f"ot{u}"), u, ident).then_inc(o_filled, 1)
                    if tile_at(s, OUT) is not None:
                        t = tile_at(s, OUT)
                        pe.wait_ge(o_emptied, O.done(i, f"ot{4 * t + 3}"))
                        pe.wait_ge(d_emptied, Dr.free(i, f"out{t}"))
                        heads.pe_project(Dr.bank(i, f"out{t}"), t, wo).then_inc(d_filled, 1)
                    if tile_at(s, FN) is not None:
                        t = tile_at(s, FN)
                        pe.wait_ge(xn_made, i * 2 * TILES + TILES + t + 1)
                        pe.wait_ge(a_emptied, A.free(i, f"fn{t}"))
                        turned(nc, A.bank(i, f"fn{t}"), xn[:, t, :], ident).then_inc(a_filled, 1)
                    if tile_at(s, FFN) is not None:
                        t = tile_at(s, FFN)
                        pe.wait_ge(a_emptied, A.done(i, f"fn{t}"))
                        pe.wait_ge(d_emptied, Dr.free(i, f"ffn{t}"))
                        for c in range(C):
                            last = nc.tensor.matmul(Dr.bank(i, f"ffn{t}")[:, :], xnt[:, c, t * P:(t + 1) * P],
                                                    w_low[:, c, :], start=(c == 0), stop=(c == C - 1))
                        last.then_inc(d_filled, 1)

        @block.vector
        def _(dve):
            for emptied in (d_emptied, s_emptied, o_emptied):
                dve.sem_inc(emptied, 2)
            dve.wait_ge(quant_in, 5 * DMA)
            for s in range(32):
                nc.vector.tensor_scalar(bits[:, :, :, s], planes[:, :, :], s, 1,
                                        ALU.logical_shift_right, ALU.bitwise_and).then_inc(bits_made, 1)
            dve.wait_ge(bits_made, 32)
            plane = [bits[:, n].rearrange("p w s -> p (w s)") for n in range(4)]
            nc.vector.scalar_tensor_tensor(out=codes[:, :], in0=plane[3], scalar=2.0, in1=plane[2],
                                           op0=ALU.mult, op1=ALU.add).then_inc(codes_made, 1)
            for n in (1, 0):
                dve.wait_ge(codes_made, 2 - n)
                nc.vector.scalar_tensor_tensor(out=codes[:, :], in0=codes[:, :], scalar=2.0, in1=plane[n],
                                               op0=ALU.mult, op1=ALU.add).then_inc(codes_made, 1)
            dve.wait_ge(codes_made, 3)
            for o in range(C):
                for e in range(ENTRIES):
                    n = ENTRIES * o + e
                    if n >= 4:
                        used = n - 4
                        if used % ENTRIES == ENTRIES - 1:
                            dve.wait_ge(a_filled, A.full(None, f"lut{used // ENTRIES}"))
                        else:
                            dve.wait_ge(picked_used, used - used // ENTRIES + 1)
                    nc.vector.tensor_scalar(picked[:, n % 4, :], codes[:, o * D:(o + 1) * D], float(e),
                                            lut[:, o, e:e + 1], ALU.is_equal, ALU.mult).then_inc(picked_made, 1)
            dve.wait_ge(masks_made, 4)
            dve.wait_ge(gates_ready, 1)

            with dve.Fori(0, GROUPS) as i:
                def statistics(n, t, src):
                    nc.vector.bn_stats(stats[:, t, :], src[:, t, :]).then_inc(stats_made, 1)
                    dve.wait_ge(stats_made, i * 2 * TILES + n * TILES + t + 1)
                    dve.sem_inc(gate, 1)
                    nc.vector.bn_aggr(mv[:, t, :], stats[:, t, :]).then_inc(mv_made, 1)

                def normalise(n, t, src):
                    dve.wait_ge(rstd_made, i * 2 * TILES + n * TILES + t + 1)
                    nc.vector.tensor_scalar(xn[:, t, :], src[:, t, :], mv[:, t, 0:1], rstd[:, t:t + 1],
                                            ALU.subtract, ALU.mult).then_inc(xn_made, 1)

                dve.wait_ge(x_loaded, DMA * (i + 1))
                for t in range(TILES):
                    statistics(0, t, x_new)
                    if t:
                        normalise(0, t - 1, x_new)
                normalise(0, TILES - 1, x_new)
                dve.wait_ge(d_filled, Dr.full(i, "k"))
                heads.dve_spread_keys(Dr.bank(i, "k")).then_inc(d_emptied, 1)
                dve.wait_ge(d_filled, Dr.full(i, "v"))
                heads.dve_spread_values(Dr.bank(i, "v")).then_inc(d_emptied, 1)
                dve.wait_ge(x_stored, 1 + DMA * TILES * i)
                for s in range(STEPS):
                    if s < UNITS:
                        dve.wait_ge(s_filled, S.full(i, f"s{s}"))
                        heads.dve_max(S.bank(i, f"s{s}"), s).then_inc(heads.max_made, 1)
                    if 0 <= s - 3 < UNITS:
                        u = s - 3
                        dve.wait_ge(o_filled, O.full(i, f"av{u}"))
                        heads.dve_inverse(O.bank(i, f"av{u}"), u).then_inc(heads.inv_made, 1)
                    if s < UNITS:
                        dve.wait_ge(heads.max_made, i * UNITS + s + 1)
                        heads.dve_shift(S.bank(i, f"s{s}"), s).then_inc(s_emptied, 1)
                    if 0 <= s - 3 < UNITS:
                        dve.wait_ge(heads.inv_made, i * UNITS + u + 1)
                        heads.dve_norm(O.bank(i, f"av{u}"), u).then_inc(o_emptied, 1)
                    if 0 <= s - 4 < UNITS:
                        dve.wait_ge(o_filled, O.full(i, f"ot{s - 4}"))
                        heads.dve_copy_back(O.bank(i, f"ot{s - 4}"), s - 4).then_inc(o_emptied, 1)
                    if tile_at(s, OUT + 1) is not None:
                        t = tile_at(s, OUT + 1)
                        dve.wait_ge(d_filled, Dr.full(i, f"out{t}"))
                        nc.vector.scalar_tensor_tensor(out=x[:, t, :], in0=Dr.bank(i, f"out{t}")[:, :],
                                                       scalar=tgates[:, 0:1], in1=x_new[:, t, :],
                                                       op0=ALU.mult, op1=ALU.add).then_inc(d_emptied, 1)
                        dve.wait_ge(d_emptied, Dr.done(i, f"out{t}"))
                        if t == TILES - 1:
                            dve.sem_inc(x_free, 1)
                        statistics(1, t, x)
                    if tile_at(s, OUT + 2) is not None:
                        normalise(1, tile_at(s, OUT + 2), x)
                    if tile_at(s, FFN + 1) is not None:
                        t = tile_at(s, FFN + 1)
                        dve.wait_ge(bias_added, i * TILES + t + 1)
                        dve.wait_ge(d_filled, Dr.full(i, f"ffn{t}"))
                        nc.vector.scalar_tensor_tensor(out=x[:, t, :], in0=Dr.bank(i, f"ffn{t}")[:, :],
                                                       scalar=tgates[:, 1:2], in1=x[:, t, :],
                                                       op0=ALU.mult, op1=ALU.add).then_inc(d_emptied, 1)


class LastWeights:

    def __init__(self, nc, ctx):
        def sb(name, shape):
            return ctx.enter_context(nc.sbuf_tensor(f"last_{name}", shape, F32))

        self.wk, self.wv, self.wo = sb("wk", [P, C, P]), sb("wv", [P, C, P]), sb("wo", [P, REP, D])
        self.wq_raw, self.up_raw = sb("wq_raw", [P, C, D])[:, :, :], sb("up_raw", [P, C, P])[:, :, :]
        self.low_raw = sb("low_raw", [P, D])[:, :]

    def loads(self, io):
        experts = io["L3_ffn_Wr"].shape[0]
        pairs = [(self.wq_raw, io["L3_xattn_Wq"].rearrange("(c p) n -> p c n", p=P)),
                 (self.low_raw, io["L3_ffn_A"].rearrange("h r d -> (h r) d")),
                 (self.wk[:, :, :], io["L3_xattn_Wk"].rearrange("(c p) n -> p c n", p=P)),
                 (self.wv[:, :, :], io["L3_xattn_Wv"].rearrange("(c p) n -> p c n", p=P))]
        pairs += [(self.up_raw[:, c].rearrange("p (h r) -> p h r", h=experts),
                   io["L3_ffn_B"][:, c * P:(c + 1) * P, :].rearrange("h p r -> p h r")) for c in range(C)]
        pairs += [(self.wo[k * HD:(k + 1) * HD, :, :],
                   io["L3_xattn_Wo"][k * REP * HD:(k + 1) * REP * HD, :].rearrange("(r d) n -> d r n", r=REP))
                  for k in range(KV)]
        return pairs


def last_layer(nc, io, x_in, ctx_t, x_out, last):
    TILES = 4
    GROUPS = TOKENS // (TILES * P)
    T = TILES * P
    B = T // SEQ
    H3, R3 = 8, 16
    LOW = H3 * R3
    OUT, FN, ROUTE, LOWT, FFN = 7, 10, 11, 14, 16
    def tile_at(s, first):
        return (s - first) // 4 if s >= first and (s - first) % 4 == 0 and (s - first) // 4 < TILES else None

    with ExitStack() as ctx:
        chip = Chip(nc, ctx, "l3")
        sb, sem = chip.sb, chip.sem
        heads = HeadsOf16(chip, B)
        UNITS = heads.UNITS
        STEPS = FFN + 2 + 4 * (TILES - 1) + 1

        a_setup = ["low_a", "low_r", "low_b", "none"]
        a_loop = [f"xd{t}" for t in range(TILES)] + [f"q{r}" for r in range(REP)]
        d_loop = ["k", "v"]
        ln_order = [f"d{t}" for t in range(TILES)] + [f"e{t}" for t in range(TILES)]
        s_loop, o_loop = heads.order(STEPS)
        for s in range(STEPS):
            if 0 <= s - 2 < UNITS:
                a_loop.append(f"pt{s - 2}")
            if tile_at(s, OUT) is not None:
                d_loop.append(f"out{tile_at(s, OUT)}")
            if tile_at(s, FN) is not None:
                a_loop.append(f"xe{tile_at(s, FN)}")
            if tile_at(s, ROUTE) is not None:
                d_loop.append(f"route{tile_at(s, ROUTE)}")
            if tile_at(s, LOWT) is not None:
                a_loop.append(f"lowt{tile_at(s, LOWT)}")
            if tile_at(s, FFN) is not None:
                d_loop.append(f"f3_{tile_at(s, FFN)}")
        if len(a_loop) % 2:
            a_loop.append("none")
        A = Banks(chip.banks("bank_a"), a_setup, a_loop)
        Dr = Banks(chip.banks("bank_d"), [], d_loop)
        S = Banks(chip.banks("bank_s"), [], s_loop)
        O = Banks(chip.banks("bank_o"), [], o_loop)

        def ln(i, label):
            return i * len(ln_order) + ln_order.index(label) + 1

        def biased(i, label):
            return i * TILES + int(label[-1]) + 1

        x_tiles = x_in.rearrange("(g t p) d -> g p t d", p=P, t=TILES)
        out_tiles = x_out.rearrange("(g t p) d -> g p t d", p=P, t=TILES)

        ident = sb("ident", [P, P])
        eps_col, half_col = sb("eps_col", [P, 1]), sb("half_col", [P, 1])
        wq = sb("wq", [P, C, D])
        wk, wv, wo = last.wk, last.wv, last.wo
        bq, bk, bv = sb("bq", [P, REP]), sb("bk", [P, 1]), sb("bv", [P, KV // 2, 2, HD])
        w_low, w_up = sb("w_low", [P, C, LOW + H3]), sb("w_up", [P, D])
        router_bias = sb("router_bias", [P, H3])
        gates, tgates = sb("gates", [P, 2]), sb("tgates", [P, 2])
        gated_b3 = sb("gated_b3", [P, D])

        wq_raw, low_raw, up_raw = last.wq_raw, last.low_raw, last.up_raw
        router_raw = sb("router_raw", [P, D])
        b3_raw = sb("b3_raw", [P, D])

        x, xn = sb("x", [P, TILES, D]), sb("xn", [P, TILES, D])
        xnt, ctxt = sb("xnt", [P, C, T]), sb("ctxt", [P, C, T])
        stats, mv = sb("stats", [P, TILES, 6]), sb("mv", [P, TILES, 2])
        small, rstd = sb("small", [P, TILES]), sb("rstd", [P, TILES])
        logits, router_max = sb("logits", [P, 2, H3]), sb("router_max", [P, 2])
        router_sum, router_inv, mix = sb("router_sum", [P, 2]), sb("router_inv", [P, 2]), sb("mix", [P, 2, H3])
        low, low_t = sb("low", [P, 2, H3, R3]), sb("low_t", [P, 2, P])

        small_in, router_in = sem("small_in"), sem("router_in")
        cleared, consts_made, masks_made = sem("cleared"), sem("consts_made"), sem("masks_made")
        gates_ready, gated_made, wq_ordered = sem("gates_ready"), sem("gated_made"), sem("wq_ordered")
        x_loaded = [sem(f"x_loaded{t}") for t in range(TILES)]
        x_stored = [sem(f"x_stored{t}") for t in range(TILES)]
        ctx_loaded, ctx_free = sem("ctx_loaded"), sem("ctx_free")
        a_filled, a_emptied = sem("a_filled"), sem("a_emptied")
        d_filled, d_emptied = sem("d_filled"), sem("d_emptied")
        s_filled, s_emptied, o_filled, o_emptied = heads.s_filled, heads.s_emptied, heads.o_filled, heads.o_emptied
        stats_made, mv_made, rstd_step, rstd_made = sem("stats_made"), sem("mv_made"), sem("rstd_step"), sem("rstd_made")
        xn_made, bias_added = sem("xn_made"), sem("bias_added")
        logits_made, router_max_made, router_exp_made, router_inv_made, mix_made = \
            sem("logits_made"), sem("router_max_made"), sem("router_exp_made"), sem("router_inv_made"), sem("mix_made")
        gate = sem("gate")

        block = ctx.enter_context(nc.Block())

        @block.sync
        def _(sp):
            sp.dma_start(router_raw[0:H3, :], io["L3_ffn_Wr"]).then_inc(router_in, DMA)
            for t in range(TILES):
                sp.sem_inc(x_stored[t], 1)
            sp.sem_inc(ctx_free, 1)
            with sp.Fori(0, GROUPS) as i:
                for t in range(TILES):
                    sp.wait_ge(x_stored[t], 1 + DMA * i)
                    sp.dma_start(x[:, t, :], x_tiles[i][:, t, :]).then_inc(x_loaded[t], DMA)
                sp.wait_ge(ctx_free, i + 1)
                for half in range(2):
                    sp.dma_start(ctxt[:, :, half * T // 2:(half + 1) * T // 2], ctx_t[i * 2 + half])\
                      .then_inc(ctx_loaded, DMA)
            for t in range(TILES):
                sp.wait_ge(x_stored[t], 1 + DMA * GROUPS)

        SMALL = 2 + 2 * KV + 4

        @block.gpsimd
        def _(pool):
            nc.gpsimd.memset(ident[:, :], 0.0).then_inc(consts_made, 1)
            nc.gpsimd.memset(eps_col[:, :], EPS).then_inc(consts_made, 1)
            nc.gpsimd.memset(half_col[:, :], -0.5).then_inc(consts_made, 1)
            pool.wait_ge(consts_made, 3)
            nc.gpsimd.affine_select(out=ident[:, :], in_=ident[:, :], compare_op=ALU.not_equal, fill=1.0,
                                    base=0, pattern=[[-1, P]], channel_multiplier=1).then_inc(consts_made, 1)
            heads.make_masks(pool, cleared, masks_made)
            pool.wait_ge(small_in, SMALL * DMA)
            pool.wait_ge(gates_ready, 1)
            nc.gpsimd.tensor_tensor(gated_b3[:, :], b3_raw[:, :], tgates[:, 0:1].to_broadcast([P, D]), ALU.mult)\
                .then_inc(gated_made, 1)
            for c in range(C):
                for r in range(REP):
                    nc.gpsimd.tensor_copy(heads_by_rep(wq[:, c, :])[:, :, r, :], heads_as_given(wq_raw[:, c, :])[:, :, r, :])\
                        .then_inc(wq_ordered, 1)
            pool.wait_ge(gated_made, 1)

            with pool.Fori(0, GROUPS) as i:
                def inverse_deviation(label):
                    t = int(label[-1])
                    pool.wait_ge(mv_made, ln(i, label))
                    nc.gpsimd.tensor_tensor(small[:, t:t + 1], mv[:, t, 1:2], eps_col[:, :], ALU.add).then_inc(rstd_step, 1)
                    pool.wait_ge(rstd_step, ln(i, label))
                    nc.gpsimd.tensor_tensor(rstd[:, t:t + 1], small[:, t:t + 1], half_col[:, :], ALU.pow)\
                        .then_inc(rstd_made, 1)

                def add_bias(label):
                    t = int(label[-1])
                    pool.wait_ge(xn_made, ln(i, label))
                    nc.gpsimd.tensor_tensor(x[:, t, :], x[:, t, :], gated_b3[:, :], ALU.add).then_inc(bias_added, 1)

                for t in range(TILES):
                    inverse_deviation(f"d{t}")
                for t in range(TILES):
                    add_bias(f"d{t}")
                for t in range(TILES):
                    inverse_deviation(f"e{t}")

        @block.scalar
        def _(act):
            def load(out, src, **more):
                act.dma_start(out, src, **more).then_inc(small_in, DMA)

            for n, name in enumerate(("g_xattn", "g_ffn")):
                load(gates[:, n:n + 1], io[name][3:4].partition_broadcast(P))
            for k in range(KV):
                for half in range(2):
                    reps = slice(2 * half, 2 * half + 2)
                    load(bq[k * HD:(k + 1) * HD, reps],
                         io["L3_xattn_bq"][k * REP * HD:(k + 1) * REP * HD].rearrange("(r d) -> d r", r=REP)[:, reps],
                         allow_slow_non_contiguous=True)
            load(bk[:, :], io["L3_xattn_bk"].rearrange("(p a) -> p a", a=1))
            load(bv[:, :, :, :].rearrange("p a h d -> p (a h d)"), io["L3_xattn_bv"].partition_broadcast(P))
            load(b3_raw[:, :], io["L3_xattn_bo"].partition_broadcast(P))
            load(router_bias[:, :], io["L3_ffn_br"].partition_broadcast(P))
            act.sem_inc(a_emptied, 2)
            act.wait_ge(small_in, SMALL * DMA)
            nc.scalar.activation(tgates[:, :], gates[:, :], ACT.Tanh).then_inc(gates_ready, 1)

            def setup_bank(label):
                act.wait_ge(a_filled, A.full(None, label))
                return A.bank(None, label)[:, :]

            nc.scalar.activation(w_low[:, :, 0:LOW], split4(setup_bank("low_a")), ACT.Copy).then_inc(a_emptied, 1)
            nc.scalar.activation(w_low[:, :, LOW:LOW + H3], setup_bank("low_r")[:, 0:C * H3].rearrange("p (c h) -> p c h", c=C),
                   ACT.Copy).then_inc(a_emptied, 1)
            nc.scalar.activation(w_up[:, :], setup_bank("low_b"), ACT.Copy).then_inc(a_emptied, 1)
            act.wait_ge(a_filled, A.full(None, "none"))
            act.sem_inc(a_emptied, 1)

            with act.Fori(0, GROUPS) as i:
                def empty(label, out, bias=None):
                    src = A.bank(i, label)[:, :]
                    act.wait_ge(a_filled, A.full(i, label))
                    if len(out.shape) == 3:
                        src = src.rearrange("p (b n) -> p b n", b=out.shape[1])
                    if bias is None:
                        nc.scalar.activation(out, src, ACT.Copy).then_inc(a_emptied, 1)
                    else:
                        nc.scalar.activation(out, src, ACT.Identity, bias=bias).then_inc(a_emptied, 1)

                def chunk(t):
                    return xnt[:, :, t * P:(t + 1) * P]

                for t in range(TILES):
                    empty(f"xd{t}", chunk(t))
                for r in range(REP):
                    empty(f"q{r}", heads.qt[:, :, r, :], bq[:, r:r + 1])
                for s in range(STEPS):
                    if 0 <= s - 1 < UNITS:
                        act.wait_ge(s_emptied, S.done(i, f"s{s - 1}"))
                        heads.act_exp(s - 1).then_inc(heads.exp_made, 1)
                    if 0 <= s - 2 < UNITS:
                        empty(f"pt{s - 2}", heads.probs_t[:, s % 2])
                    if tile_at(s, FN) is not None:
                        empty(f"xe{tile_at(s, FN)}", chunk(tile_at(s, FN)))
                    if tile_at(s, ROUTE + 1) is not None:
                        t = tile_at(s, ROUTE + 1)
                        n = t % 2
                        act.wait_ge(router_max_made, i * TILES + t + 1)
                        nc.scalar.activation(logits[:, n], logits[:, n], ACT.Exp, bias=router_max[:, n:n + 1],
                                             accum_out=router_sum[:, n:n + 1]).then_inc(router_exp_made, 1)
                    if tile_at(s, LOWT) is not None:
                        t = tile_at(s, LOWT)
                        act.wait_ge(a_filled, A.full(i, f"lowt{t}"))
                        nc.scalar.activation(low_t[:, t % 2, :], A.bank(i, f"lowt{t}")[:, 0:P], ACT.Copy).then_inc(a_emptied, 1)
                    if tile_at(s, FFN + 2) is not None:
                        t = tile_at(s, FFN + 2)
                        act.wait_ge(d_emptied, Dr.done(i, f"f3_{t}"))
                        act.dma_start(out_tiles[i][:, t, :], x[:, t, :]).then_inc(x_stored[t], DMA)
                if "none" in a_loop:
                    act.wait_ge(a_filled, A.full(i, "none"))
                    act.sem_inc(a_emptied, 1)

        @block.tensor
        def _(pe):
            pe.wait_ge(consts_made, 4)
            pe.wait_ge(router_in, DMA)
            for label, raw, n in (("low_a", low_raw, 4), ("low_r", router_raw, 4), ("low_b", up_raw, 4)):
                pe.wait_ge(a_emptied, A.free(None, label))
                out = A.bank(None, label)
                for c in range(n):
                    if label == "low_r":
                        last = nc.tensor.transpose(out[:, c * H3:(c + 1) * H3], raw[0:H3, c * P:(c + 1) * P], ident[0:H3, 0:H3])
                    else:
                        src = raw[:, c * P:(c + 1) * P] if label == "low_a" else raw[:, c, :]
                        last = nc.tensor.transpose(out[:, c * P:(c + 1) * P], src, ident[:, :])
                last.then_inc(a_filled, 1)
            pe.wait_ge(a_emptied, A.done(None, "low_b"))
            pe.sem_inc(a_filled, 1)
            pe.wait_ge(wq_ordered, C * REP)
            pe.wait_ge(masks_made, 4)

            with pe.Fori(0, GROUPS) as i:
                def turn_x(kind, t):
                    pe.wait_ge(xn_made, ln(i, f"{kind}{t}"))
                    pe.wait_ge(a_emptied, A.free(i, f"x{kind}{t}"))
                    turned(nc, A.bank(i, f"x{kind}{t}"), xn[:, t, :], ident).then_inc(a_filled, 1)

                pe.wait_ge(ctx_loaded, 2 * DMA * (i + 1))
                pe.wait_ge(d_emptied, Dr.free(i, "k"))
                heads.pe_keys(Dr.bank(i, "k"), wk, ctxt).then_inc(d_filled, 1)
                pe.wait_ge(d_emptied, Dr.free(i, "v"))
                heads.pe_values_in(Dr.bank(i, "v"), wv, ctxt).then_inc(d_filled, 1)
                for t in range(TILES):
                    turn_x("d", t)
                pe.wait_ge(a_emptied, A.done(i, f"xd{TILES - 1}"))
                for r in range(REP):
                    pe.wait_ge(a_emptied, A.free(i, f"q{r}"))
                    heads.pe_queries(A.bank(i, f"q{r}"), wq, xnt, r).then_inc(a_filled, 1)
                pe.wait_ge(a_emptied, A.done(i, f"q{REP - 1}"))
                pe.wait_ge(d_emptied, Dr.done(i, "v"))
                pe.sem_inc(ctx_free, 1)
                for s in range(STEPS):
                    if s < UNITS:
                        pe.wait_ge(s_emptied, S.free(i, f"s{s}"))
                        heads.pe_scores(S.bank(i, f"s{s}"), s).then_inc(s_filled, 1)
                    if 0 <= s - 2 < UNITS:
                        u = s - 2
                        pe.wait_ge(heads.exp_made, i * UNITS + u + 1)
                        pe.wait_ge(a_emptied, A.free(i, f"pt{u}"))
                        heads.pe_turn_probs(A.bank(i, f"pt{u}"), u, ident).then_inc(a_filled, 1)
                    if 0 <= s - 3 < UNITS:
                        u = s - 3
                        pe.wait_ge(a_emptied, A.done(i, f"pt{u}"))
                        pe.wait_ge(o_emptied, O.free(i, f"av{u}"))
                        heads.pe_attend(O.bank(i, f"av{u}"), u).then_inc(o_filled, 1)
                    if 0 <= s - 4 < UNITS:
                        u = s - 4
                        pe.wait_ge(o_emptied, O.done(i, f"av{u}"))
                        pe.wait_ge(o_emptied, O.free(i, f"ot{u}"))
                        heads.pe_turn_back(O.bank(i, f"ot{u}"), u, ident).then_inc(o_filled, 1)
                    if tile_at(s, OUT) is not None:
                        t = tile_at(s, OUT)
                        pe.wait_ge(o_emptied, O.done(i, f"ot{4 * t + 3}"))
                        pe.wait_ge(d_emptied, Dr.free(i, f"out{t}"))
                        heads.pe_project(Dr.bank(i, f"out{t}"), t, wo).then_inc(d_filled, 1)
                    if tile_at(s, FN) is not None:
                        turn_x("e", tile_at(s, FN))
                    if tile_at(s, ROUTE) is not None:
                        t = tile_at(s, ROUTE)
                        pe.wait_ge(a_emptied, A.done(i, f"xe{t}"))
                        pe.wait_ge(d_emptied, Dr.free(i, f"route{t}"))
                        for c in range(C):
                            last = nc.tensor.matmul(Dr.bank(i, f"route{t}")[:, 0:LOW + H3], xnt[:, c, t * P:(t + 1) * P],
                                                    w_low[:, c, :], start=(c == 0), stop=(c == C - 1))
                        last.then_inc(d_filled, 1)
                    if tile_at(s, LOWT) is not None:
                        t = tile_at(s, LOWT)
                        pe.wait_ge(d_emptied, Dr.done(i, f"route{t}"))
                        pe.wait_ge(a_emptied, A.free(i, f"lowt{t}"))
                        nc.tensor.transpose(A.bank(i, f"lowt{t}")[:, 0:P], low[:, t % 2].rearrange("p h r -> p (h r)"),
                                            ident[:, :]).then_inc(a_filled, 1)
                    if tile_at(s, FFN) is not None:
                        t = tile_at(s, FFN)
                        pe.wait_ge(a_emptied, A.done(i, f"lowt{t}"))
                        pe.wait_ge(d_emptied, Dr.free(i, f"f3_{t}"))
                        nc.tensor.matmul(Dr.bank(i, f"f3_{t}")[:, :], low_t[:, t % 2, :], w_up[:, :],
                                         start=True, stop=True).then_inc(d_filled, 1)
                if "none" in a_loop:
                    pe.wait_ge(a_emptied, A.free(i, "none"))
                    pe.sem_inc(a_filled, 1)

        @block.vector
        def _(dve):
            for emptied in (d_emptied, s_emptied, o_emptied):
                dve.sem_inc(emptied, 2)
            dve.wait_ge(masks_made, 4)
            dve.wait_ge(gated_made, 1)

            with dve.Fori(0, GROUPS) as i:
                def statistics(label):
                    t = int(label[-1])
                    nc.vector.bn_stats(stats[:, t, :], x[:, t, :]).then_inc(stats_made, 1)
                    dve.wait_ge(stats_made, ln(i, label))
                    dve.sem_inc(gate, 1)
                    nc.vector.bn_aggr(mv[:, t, :], stats[:, t, :]).then_inc(mv_made, 1)

                def normalise(label):
                    t = int(label[-1])
                    dve.wait_ge(rstd_made, ln(i, label))
                    nc.vector.tensor_scalar(xn[:, t, :], x[:, t, :], mv[:, t, 0:1], rstd[:, t:t + 1],
                                            ALU.subtract, ALU.mult).then_inc(xn_made, 1)

                def residual(label, t, scale, bias=None):
                    if bias is not None:
                        dve.wait_ge(bias_added, biased(i, bias))
                    dve.wait_ge(d_filled, Dr.full(i, label))
                    nc.vector.scalar_tensor_tensor(out=x[:, t, :], in0=Dr.bank(i, label)[:, :], scalar=scale,
                                                   in1=x[:, t, :], op0=ALU.mult, op1=ALU.add).then_inc(d_emptied, 1)
                    dve.wait_ge(d_emptied, Dr.done(i, label))

                for t in range(TILES):
                    dve.wait_ge(x_loaded[t], DMA * (i + 1))
                    statistics(f"d{t}")
                for t in range(TILES):
                    normalise(f"d{t}")
                dve.wait_ge(d_filled, Dr.full(i, "k"))
                heads.dve_spread_keys(Dr.bank(i, "k"), bk[:, 0:1]).then_inc(d_emptied, 1)
                dve.wait_ge(d_filled, Dr.full(i, "v"))
                heads.dve_spread_values(Dr.bank(i, "v"), bv[:, :, :, :]).then_inc(d_emptied, 1)
                for s in range(STEPS):
                    if s < UNITS:
                        dve.wait_ge(s_filled, S.full(i, f"s{s}"))
                        heads.dve_max(S.bank(i, f"s{s}"), s).then_inc(heads.max_made, 1)
                    if 0 <= s - 3 < UNITS:
                        u = s - 3
                        dve.wait_ge(o_filled, O.full(i, f"av{u}"))
                        heads.dve_inverse(O.bank(i, f"av{u}"), u).then_inc(heads.inv_made, 1)
                    if s < UNITS:
                        dve.wait_ge(heads.max_made, i * UNITS + s + 1)
                        heads.dve_shift(S.bank(i, f"s{s}"), s).then_inc(s_emptied, 1)
                    if 0 <= s - 3 < UNITS:
                        dve.wait_ge(heads.inv_made, i * UNITS + u + 1)
                        heads.dve_norm(O.bank(i, f"av{u}"), u).then_inc(o_emptied, 1)
                    if 0 <= s - 4 < UNITS:
                        dve.wait_ge(o_filled, O.full(i, f"ot{s - 4}"))
                        heads.dve_copy_back(O.bank(i, f"ot{s - 4}"), s - 4).then_inc(o_emptied, 1)
                    if tile_at(s, OUT + 1) is not None:
                        t = tile_at(s, OUT + 1)
                        residual(f"out{t}", t, tgates[:, 0:1], f"d{t}")
                        statistics(f"e{t}")
                    if tile_at(s, OUT + 2) is not None:
                        normalise(f"e{tile_at(s, OUT + 2)}")
                    if tile_at(s, ROUTE + 1) is not None:
                        t = tile_at(s, ROUTE + 1)
                        n = t % 2
                        dve.wait_ge(d_filled, Dr.full(i, f"route{t}"))
                        nc.vector.tensor_tensor(logits[:, n], Dr.bank(i, f"route{t}")[:, LOW:LOW + H3], router_bias[:, :],
                                                ALU.add).then_inc(logits_made, 1)
                        dve.wait_ge(logits_made, i * TILES + t + 1)
                        nc.vector.tensor_reduce(router_max[:, n:n + 1], logits[:, n], AX_X, ALU.max, negate=True)\
                            .then_inc(router_max_made, 1)
                    if tile_at(s, ROUTE + 2) is not None:
                        t = tile_at(s, ROUTE + 2)
                        n = t % 2
                        dve.wait_ge(router_exp_made, i * TILES + t + 1)
                        nc.vector.reciprocal(router_inv[:, n:n + 1], router_sum[:, n:n + 1]).then_inc(router_inv_made, 1)
                        dve.wait_ge(router_inv_made, i * TILES + t + 1)
                        nc.vector.tensor_scalar(mix[:, n], logits[:, n], router_inv[:, n:n + 1], 2.0 * H3,
                                                ALU.mult, ALU.mult).then_inc(mix_made, 1)
                        dve.wait_ge(mix_made, i * TILES + t + 1)
                        nc.vector.tensor_tensor(low[:, n], Dr.bank(i, f"route{t}")[:, 0:LOW].rearrange("p (h r) -> p h r", h=H3),
                                                along(mix[:, n], R3), ALU.mult).then_inc(d_emptied, 1)
                    if tile_at(s, FFN + 2) is not None:
                        residual(f"f3_{tile_at(s, FFN + 2)}", tile_at(s, FFN + 2), tgates[:, 1:2])


class Ring:

    def __init__(self, banks, order, loop_labels, tiles_per_turn):
        self.banks, self.order = banks, order
        first, last = order.index(loop_labels[0]), order.index(loop_labels[-1])
        self.per_turn = last - first + 1
        assert self.per_turn % len(banks) == 0
        for name, t in loop_labels:
            assert order.index((name, t + tiles_per_turn)) == order.index((name, t)) + self.per_turn

    def turn(self, label, shift):
        return self.order.index(label) + self.per_turn * shift

    def free(self, label, shift=0):
        return self.turn(label, shift) + 1

    def full(self, label, shift=0):
        return self.turn(label, shift) + 1

    def done(self, label, shift=0):
        return self.turn(label, shift) + len(self.banks) + 1

    def bank(self, label):
        return self.banks[self.order.index(label) % len(self.banks)]


def window_attention(nc, io, x_in, ctx_in, x_out, last_weights):
    TILES = TOKENS // P
    W = 16
    LEFT = W // 2
    HEADS2, HD2 = 8, 8
    BH = 2 * HEADS2
    SCALE2 = HD2 ** -0.5
    R0, R1, E = 32, 8, 3
    POOL_W = (2, 6, 10, 13)
    DVE_W = tuple(w for w in range(W) if w not in POOL_W)
    HALF = W // 2
    FOURS, ADDS = W // 4, 3 * W // 4
    NP, ND = len(POOL_W), len(DVE_W)
    POOL_AHEAD = 3
    U = 4
    FILL = range(-1, 3)
    TURN = range(3, 3 + U)
    TURNS = (TILES - 2 - 3 + 1) // U
    DRAIN = range(3 + U * TURNS, TILES + 3)
    ALL = range(-1, TILES + 3)
    assert 3 + U * TURNS == TILES - 1

    def is_tile(t):
        return 0 <= t < TILES

    def in_order(steps, parts):
        return [(name, m + off) for m in steps for name, off in parts if is_tile(m + off)]

    A_PARTS = [("xa", 1), ("xc", -3), ("q2", 1), ("k2", 1), ("v2", 1)]
    F_PARTS = [("f1", 1), ("f2", -3)]
    LN_PARTS = [("a", 1), ("c", -3), ("b", 1)]
    G_PARTS = [("g0", 0), ("g1", 0)]
    O_PARTS, S_PARTS, Y_PARTS = [(f"b{w}", -2) for w in range(W)], [("dots0", 0), ("dots1", 0)], [("y", -2)]

    with ExitStack() as ctx:
        chip = Chip(nc, ctx, "l2")
        sb, sem = chip.sb, chip.sem
        a_setup = [("gt", 0)] + [("fold", c) for c in range(C)] + [("w2", 0)]
        bank_a, bank_g = chip.banks("bank_ag")
        A = Ring([bank_a], a_setup + in_order(ALL, A_PARTS), in_order(TURN, A_PARTS), U)
        S = Ring(chip.banks("bank_s"), in_order(ALL, S_PARTS), in_order(TURN, S_PARTS), U)
        O = Ring(chip.banks("bank_o"), in_order(ALL, O_PARTS), in_order(TURN, O_PARTS), U)
        bank_y, bank_f = chip.banks("bank_yf")
        Y = Ring([bank_y], in_order(ALL, Y_PARTS), in_order(TURN, Y_PARTS), U)
        F = Ring([bank_f], in_order(ALL, F_PARTS), in_order(TURN, F_PARTS), U)
        G = Ring([bank_g], in_order(ALL, G_PARTS), in_order(TURN, G_PARTS), U)
        ln_order = in_order(ALL, LN_PARTS)

        def ln(kind, t, i):
            return ln_order.index((kind, t)) + 1 + i * U * len(LN_PARTS)

        def added(w):
            return 3 * (w // 4) + max(w % 4, 1)

        def biased(kind, t, i):
            return 2 * t + {"a": 0, "b": 1}[kind] + 1 + i * 2 * U

        x_tiles = x_in.rearrange("(t p) d -> t p d", p=P)
        ctx_tiles = ctx_in.rearrange("(t p) d -> t p d", p=P)
        out_tiles = x_out.rearrange("(t p) d -> t p d", p=P)

        ident = sb("ident", [P, P])
        LAST = (HALF - 1) * BH
        head_sum = sb("head_sum", [P, LAST + HALF * BH])
        eps_col, half_col = sb("eps_col", [P, 1]), sb("half_col", [P, 1])
        w_f1, w_f2 = sb("w_f1", [P, C, D]), sb("w_f2", [P, C, D])
        w2, b2 = sb("w2", [P, 4, P]), sb("b2", [P, 4])
        gates, tgates = sb("gates", [P, 4]), sb("tgates", [P, 3])
        f2_gate = sb("f2_gate", [P, 1])
        gated_b1, gated_b2 = sb("gated_b1", [P, D]), sb("gated_b2", [P, 1])

        region = sb("region", [P, 2 * 4 * W * P])
        carve = Region(region).carve
        base_raw, fourier = carve("base_raw", [P, C, D]), carve("fourier", [P, C, D])
        coefs = [carve("coefs0", [P, C, E, R0]), carve("coefs1", [P, C, E, R1])]
        flags = [carve("flags0", [P, C, E, R0 // 4], I32), carve("flags1", [P, C, E, R1 // 4], I32)]
        masked = [carve("masked0", [P, C, E, R0]), carve("masked1", [P, C, E, R1])]
        pair_sum, expert_sum = carve("pair_sum", [P, C, R0 + R1]), carve("expert_sum", [P, C, R0 + R1])
        enc, gt = carve("enc", [P, D]), carve("gt", [P, D])
        w2_raw = carve("w2_raw", [P, 4, P])
        signs_raw = carve("signs_raw", [P, C, D // 4], I32)
        b1_raw = carve("b1_raw", [P, D])

        x_a, x_b, x_c, x_d = sb("x_a", [P, 4, D]), sb("x_b", [P, 4, D]), sb("x_c", [P, 2, D]), sb("x_d", [P, 4, D])
        ctx_new = sb("ctx_new", [P, 4, D])
        xn = {kind: sb(f"xn_{kind}", [P, D]) for kind in "abc"}
        xnt = {kind: sb(f"xnt_{kind}", [P, C, P]) for kind in "ac"}
        stats, mv = sb("stats", [P, 3, 6]), sb("mv", [P, 3, 2])
        small, rstd = sb("small", [P, 3]), sb("rstd", [P, 3])
        q2 = sb("q2", [P, 2, D])
        k2, v2 = sb("k2", [P, 2, D + W]), sb("v2", [P, 4, D + W])
        prods, prods_pool = sb("prods", [P, 4, D]), sb("prods_pool", [P, 3, D])
        values, fours = sb("values", [P, 4, D]), sb("fours", [P, 2, D])
        scores_t = sb("scores_t", [P, 2, D])
        probs2 = sb("probs2", [P, 2, 2 * BH, W])
        wide = region[:, :].rearrange("p (n t w c) -> p n t w c", n=2, t=4, w=W)
        neg_max2, sums2, inv2 = sb("neg_max2", [P, 2, 2 * BH]), sb("sums2", [P, 2, 2 * BH]), sb("inv2", [P, 2, 2 * BH])

        fold_in, w_in, small_in, last_in = sem("fold_in"), sem("w_in"), sem("small_in"), sem("last_in")
        consts_made, raw_cleared = sem("consts_made"), sem("raw_cleared")
        gates_ready, gated_made = sem("gates_ready"), sem("gated_made")
        masked_made, pair_made, experts_made, signs_made = \
            sem("masked_made"), sem("pair_made"), sem("experts_made"), sem("signs_made")
        x_loaded, ctx_loaded = [sem(f"x_loaded{t}") for t in range(4)], [sem(f"ctx_loaded{t}") for t in range(4)]
        x_used, ctx_used = sem("x_used"), sem("ctx_used")
        x_stored = [sem(f"x_stored{t}") for t in range(4)]
        a_filled, a_emptied = sem("a_filled"), sem("a_emptied")
        s_filled, s_emptied = sem("s_filled"), sem("s_emptied")
        o_filled, o_emptied = sem("o_filled"), sem("o_emptied")
        y_filled, y_emptied = sem("y_filled"), sem("y_emptied")
        f_filled, f_emptied = sem("f_filled"), sem("f_emptied")
        stats_made, mv_made, rstd_step, rstd_made = sem("stats_made"), sem("mv_made"), sem("rstd_step"), sem("rstd_made")
        xn_made, bias_added = sem("xn_made"), sem("bias_added")
        prods_made, pool_prods_made, prods_used = sem("prods_made"), sem("pool_prods_made"), sem("prods_used")
        values_added, fours_used, g_emptied = sem("values_added"), sem("fours_used"), sem("g_emptied")
        max2_made, exp2_made, sum2_made, inv2_made, probs2_made, wide_made = \
            sem("max2_made"), sem("exp2_made"), sem("sum2_made"), sem("inv2_made"), sem("probs2_made"), sem("wide_made")
        gate = sem("gate")

        FOLD_LOADS = 2 + 4 * C + 2
        LOADS = 1 + 8
        SMALL = 4 + 8 + 1

        block = ctx.enter_context(nc.Block())

        @block.sync
        def _(sp):
            def fold_load(out, src):
                sp.dma_start(out, src).then_inc(fold_in, DMA)

            for n in range(2):
                for c in range(C):
                    rows = slice(c * P, (c + 1) * P)
                    fold_load(coefs[n][:, c], io[f"L1_ffn_coefs{n}"][:, rows, :].rearrange("e p r -> p e r"))
                    fold_load(flags[n][:, c], io[f"L1_ffn_mask{n}"][:, rows, :].rearrange("e p r -> p e r"))
            fold_load(fourier, io["fourier"].rearrange("(c p) d -> p c d", p=P))
            fold_load(base_raw, io["L1_ffn_W_base"].rearrange("(c p) d -> p c d", p=P))
            fold_load(enc[0:R0, :], io["L1_ffn_enc0"])
            fold_load(enc[R0:R0 + R1, :], io["L1_ffn_enc1"])
            for t in range(4):
                sp.dma_start(x_a[:, t, :], x_tiles[t]).then_inc(x_loaded[t], DMA)
                sp.dma_start(ctx_new[:, t, :], ctx_tiles[t]).then_inc(ctx_loaded[t], DMA)
                if t == 0:
                    sp.dma_start(signs_raw, io["L2_ffn_kernel"].rearrange("(c p) f -> p c f", p=P)).then_inc(w_in, DMA)
                    sp.wait_ge(raw_cleared, 1)
                    for n, name in enumerate("qkvo"):
                        for b in range(2):
                            sp.dma_start(w2_raw[b * SEQ:(b + 1) * SEQ, n, b * SEQ:(b + 1) * SEQ], io[f"L2_xattn_W{name}"])\
                              .then_inc(w_in, DMA)
            loads = last_weights.loads(io)
            for out, src in loads:
                sp.dma_start(out, src).then_inc(last_in, DMA)
            with sp.Fori(0, TILES // 4 - 1) as i:
                for t in range(4):
                    sp.wait_ge(x_used, i * 4 + t + 1)
                    sp.dma_start(x_a[:, t, :], x_tiles[i * 4 + 4 + t]).then_inc(x_loaded[t], DMA)
                    sp.wait_ge(ctx_used, i * 4 + t + 1)
                    sp.dma_start(ctx_new[:, t, :], ctx_tiles[i * 4 + 4 + t]).then_inc(ctx_loaded[t], DMA)
            sp.wait_ge(last_in, DMA * len(loads))
            for t in range(4):
                sp.wait_ge(x_stored[t], 1 + DMA * TILES // 4)

        @block.gpsimd
        def _(pool):
            for t in range(4):
                pool.sem_inc(x_stored[t], 1)
            nc.gpsimd.memset(w2_raw, 0.0).then_inc(raw_cleared, 1)
            nc.gpsimd.memset(ident[:, :], 0.0).then_inc(consts_made, 1)
            nc.gpsimd.memset(eps_col[:, :], EPS).then_inc(consts_made, 1)
            nc.gpsimd.memset(half_col[:, :], -0.5).then_inc(consts_made, 1)
            nc.gpsimd.memset(k2[:, :, :], 0.0).then_inc(consts_made, 1)
            nc.gpsimd.memset(v2[:, :, :], 0.0).then_inc(consts_made, 1)
            nc.gpsimd.memset(head_sum[:, :], 0.0).then_inc(consts_made, 1)
            pool.wait_ge(consts_made, 6)
            agree = head_sum[:, LAST:LAST + BH]
            nc.gpsimd.memset(agree, 1.0).then_inc(consts_made, 1)
            nc.gpsimd.affine_select(out=ident[:, :], in_=ident[:, :], compare_op=ALU.not_equal, fill=1.0,
                                    base=0, pattern=[[-1, P]], channel_multiplier=1).then_inc(consts_made, 1)
            pool.wait_ge(consts_made, 8)
            nc.gpsimd.affine_select(out=agree, in_=agree, compare_op=ALU.is_ge, fill=0.0,
                                    base=0, pattern=[[-HD2, BH]], channel_multiplier=1).then_inc(consts_made, 1)
            pool.wait_ge(consts_made, 9)
            nc.gpsimd.affine_select(out=agree, in_=agree, compare_op=ALU.is_ge, fill=0.0,
                                    base=HD2 - 1, pattern=[[HD2, BH]], channel_multiplier=-1).then_inc(consts_made, 1)
            pool.wait_ge(small_in, SMALL * DMA)
            pool.wait_ge(gates_ready, 1)
            nc.gpsimd.tensor_tensor(gated_b1[:, :], b1_raw, tgates[:, 0:1].to_broadcast([P, D]), ALU.mult)\
                .then_inc(gated_made, 1)
            nc.gpsimd.tensor_tensor(gated_b2[:, :], b2[:, 3:4], tgates[:, 1:2], ALU.mult).then_inc(gated_made, 1)
            nc.gpsimd.tensor_tensor(f2_gate[:, :], gates[:, 3:4], tgates[:, 2:3], ALU.mult).then_inc(gated_made, 1)
            pool.wait_ge(gated_made, 3)

            def step(m, i):
                def inverse_deviation(kind, t):
                    k = "abc".index(kind)
                    pool.wait_ge(mv_made, ln(kind, t, i))
                    nc.gpsimd.tensor_tensor(small[:, k:k + 1], mv[:, k, 1:2], eps_col[:, :], ALU.add).then_inc(rstd_step, 1)
                    pool.wait_ge(rstd_step, ln(kind, t, i))
                    nc.gpsimd.tensor_tensor(rstd[:, k:k + 1], small[:, k:k + 1], half_col[:, :], ALU.pow)\
                        .then_inc(rstd_made, 1)

                def add_bias(kind, t):
                    x, row = {"a": (x_a, gated_b1[:, :]), "b": (x_b, gated_b2[:, 0:1].to_broadcast([P, D]))}[kind]
                    pool.wait_ge(xn_made, ln(kind, t, i))
                    nc.gpsimd.tensor_tensor(x[:, t % 4, :], x[:, t % 4, :], row, ALU.add).then_inc(bias_added, 1)

                def product(w):
                    n = m * NP + POOL_W.index(w)
                    if w == POOL_W[0]:
                        pool.wait_ge(a_emptied, A.done(("k2", m), i))
                    if n >= 3:
                        used, used_w = (n - 3) // NP, POOL_W[(n - 3) % NP]
                        pool.wait_ge(prods_used, (used + i * U) * W + used_w + 1)
                    nc.gpsimd.tensor_tensor(prods_pool[:, n % 3, :], q2[:, m % 2, :], k2[:, m % 2, w:w + D], ALU.mult)\
                        .then_inc(pool_prods_made, 1)

                def add_value(w):
                    v, k = m - 2, w // 4
                    pool.wait_ge(o_emptied, O.done((f"b{w}", v), i))
                    if w % 4 == 1:
                        if v > 0 or k >= 2:
                            pool.wait_ge(fours_used, (v + i * U) * FOURS + k - 1)
                        before = values[:, (w - 1) % 4, :]
                    else:
                        pool.wait_ge(values_added, (v + i * U) * ADDS + added(w - 1))
                        before = fours[:, k % 2, :]
                    nc.gpsimd.tensor_tensor(fours[:, k % 2, :], before, values[:, w % 4, :], ALU.add).then_inc(values_added, 1)

                for w in range(-POOL_AHEAD, W + 1):
                    if is_tile(m) and w + POOL_AHEAD in POOL_W:
                        product(w + POOL_AHEAD)
                    if is_tile(m - 2) and w >= 1 and (w - 1) % 4:
                        add_value(w - 1)
                    if is_tile(m + 1):
                        if w == 1:
                            inverse_deviation("a", m + 1)
                        if w == 4:
                            add_bias("a", m + 1)
                    if is_tile(m - 3) and w == 3:
                        inverse_deviation("c", m - 3)
                    if is_tile(m + 1):
                        if w == 11:
                            inverse_deviation("b", m + 1)
                        if w == 13:
                            add_bias("b", m + 1)

            for m in FILL:
                step(m, 0)
            with pool.Fori(0, TURNS) as i:
                for m in TURN:
                    step(m, i)
            for m in DRAIN:
                step(m, 0)

        @block.scalar
        def _(act):
            def load(out, src, **more):
                act.dma_start(out, src, **more).then_inc(small_in, DMA)

            for n, (name, k) in enumerate((("g_ffn", 1), ("g_xattn", 2), ("g_ffn", 2), ("L2_ffn_scale", 0))):
                load(gates[:, n:n + 1], io[name][k:k + 1].partition_broadcast(P))
            for n, name in enumerate("qkvo"):
                for b in range(2):
                    load(b2[b * SEQ:(b + 1) * SEQ, n:n + 1], io[f"L2_xattn_b{name}"].rearrange("(p a) -> p a", a=1))
            load(b1_raw, io["L1_ffn_b_base"].partition_broadcast(P))
            act.sem_inc(a_emptied, 1)
            act.sem_inc(g_emptied, 1)
            act.wait_ge(small_in, SMALL * DMA)
            nc.scalar.activation(tgates[:, :], gates[:, 0:3], ACT.Tanh).then_inc(gates_ready, 1)

            def empty(label, out, i=0, bias=None):
                src = A.bank(label)[:, :]
                act.wait_ge(a_filled, A.full(label, i))
                if len(out.shape) == 3:
                    src = src.rearrange("p (b n) -> p b n", b=out.shape[1])
                if bias is None:
                    nc.scalar.activation(out, src, ACT.Copy).then_inc(a_emptied, 1)
                else:
                    nc.scalar.activation(out, src, ACT.Identity, bias=bias).then_inc(a_emptied, 1)

            act.wait_ge(a_filled, A.full(("gt", 0)))
            nc.scalar.activation(gt[0:R0 + R1, :], A.bank(("gt", 0))[0:R0 + R1, :], ACT.Copy, scale=0.5).then_inc(a_emptied, 1)
            for c in range(C):
                empty(("fold", c), w_f1[:, c, :])
            empty(("w2", 0), w2[:, :, :])

            def step(m, i):
                def spread(half):
                    t = m - 1
                    act.wait_ge(probs2_made, (t + i * U) * 2 + half + 1)
                    for n in range(2):
                        src = probs2[:, half, n * BH:(n + 1) * BH, :].rearrange("p b w -> p w b")\
                            .unsqueeze(3).to_broadcast([P, W, BH, HD2])
                        out = wide[:, t % 2, 2 * half + n].rearrange("p w (b c) -> p w b c", b=BH)
                        nc.scalar.activation(out, src, ACT.Copy).then_inc(wide_made, 1)

                def exponentials(half):
                    act.wait_ge(s_emptied, S.done((f"dots{half}", m - 1), i))
                    nc.scalar.activation(probs2[:, half], probs2[:, half], ACT.Exp, scale=SCALE2).then_inc(exp2_made, 1)

                def empty_scores(half):
                    act.wait_ge(prods_used, (m + i * U) * W + (half + 1) * HALF)
                    nc.scalar.activation(scores_t[:, half, :], bank_g[:, :], ACT.Copy).then_inc(g_emptied, 1)

                if is_tile(m - 1):
                    exponentials(0)
                if is_tile(m + 1):
                    empty(("xa", m + 1), xnt["a"][:, :, :], i)
                if is_tile(m - 1):
                    exponentials(1)
                if is_tile(m):
                    empty_scores(0)
                if is_tile(m - 1):
                    spread(0)
                if is_tile(m - 3):
                    empty(("xc", m - 3), xnt["c"][:, :, :], i)
                if is_tile(m - 1):
                    spread(1)
                if is_tile(m):
                    empty_scores(1)
                if is_tile(m + 1):
                    t = m + 1
                    empty(("q2", t), q2[:, t % 2, :], i, b2[:, 0:1])
                    empty(("k2", t), k2[:, t % 2, LEFT:LEFT + D], i, b2[:, 1:2])
                    empty(("v2", t), v2[:, t % 4, LEFT:LEFT + D], i, b2[:, 2:3])
                    act.sem_inc(ctx_used, 1)
                if is_tile(m - 3):
                    act.wait_ge(f_emptied, F.done(("f2", m - 3), i))
                    act.dma_start(out_tiles[m - 3 + i * U], x_d[:, (m - 3) % 4, :]).then_inc(x_stored[(m - 3) % 4], DMA)

            for m in FILL:
                step(m, 0)
            with act.Fori(0, TURNS) as i:
                for m in TURN:
                    step(m, i)
            for m in DRAIN:
                step(m, 0)

        @block.tensor
        def _(pe):
            pe.wait_ge(consts_made, 10)
            pe.wait_ge(fold_in, FOLD_LOADS * DMA)
            pe.wait_ge(experts_made, 2)
            pe.wait_ge(a_emptied, A.free(("gt", 0)))
            for c in range(C):
                last = nc.tensor.matmul(A.bank(("gt", 0))[0:R0 + R1, :], expert_sum[:, c, :], fourier[:, c, :],
                                        start=(c == 0), stop=(c == C - 1))
            last.then_inc(a_filled, 1)
            for c in range(C):
                pe.wait_ge(a_emptied, A.free(("fold", c)))
                out = A.bank(("fold", c))
                for o in range(C):
                    nc.tensor.matmul(out[:, o * P:(o + 1) * P], base_raw[:, o, c * P:(c + 1) * P], ident[:, :],
                                     start=(o == 0), stop=False, skip_group_check=True)
                if c == 0:
                    pe.wait_ge(a_emptied, A.done(("gt", 0)))
                nc.tensor.matmul(out[:, :], enc[0:R0 + R1, c * P:(c + 1) * P], gt[0:R0 + R1, :],
                                 start=False, stop=True, skip_group_check=True).then_inc(a_filled, 1)
            pe.wait_ge(w_in, LOADS * DMA)
            pe.wait_ge(a_emptied, A.free(("w2", 0)))
            for n in range(4):
                last = nc.tensor.transpose(A.bank(("w2", 0))[:, n * P:(n + 1) * P], w2_raw[:, n, :], ident[:, :])
            last.then_inc(a_filled, 1)
            pe.wait_ge(a_emptied, A.done(("w2", 0)))
            pe.wait_ge(signs_made, 1)

            def step(m, i):
                def turn_x(kind, t):
                    pe.wait_ge(xn_made, ln(kind, t, i))
                    pe.wait_ge(a_emptied, A.free((f"x{kind}", t), i))
                    turned(nc, A.bank((f"x{kind}", t)), xn[kind][:, :], ident).then_inc(a_filled, 1)

                def feed_forward(label, kind, t, w, c):
                    if c == 0:
                        pe.wait_ge(a_emptied, A.done((f"x{kind}", t), i))
                        pe.wait_ge(f_emptied, F.free((label, t), i))
                    last = nc.tensor.matmul(bank_f[:, :], xnt[kind][:, c, :], w[:, c, :],
                                            start=(c == 0), stop=(c == C - 1))
                    if c == C - 1:
                        last.then_inc(f_filled, 1)

                def project(k):
                    v = m - 2
                    pe.wait_ge(values_added, (v + i * U) * ADDS + 3 * (k + 1))
                    if k == 0:
                        pe.wait_ge(y_emptied, Y.free(("y", v), i))
                    last = nc.tensor.matmul(bank_y[:, :], w2[:, 3, :], fours[:, k % 2, :],
                                            start=(k == 0), stop=(k == FOURS - 1))
                    if k < FOURS - 1:
                        last.then_inc(fours_used, 1)
                    else:
                        last.then_inc(y_filled, 1)
                        pe.wait_ge(y_filled, Y.full(("y", v), i))
                        pe.sem_inc(fours_used, 1)

                def project_layer2(n):
                    t = m + 1
                    label, src = (("q2", xn["b"][:, :]), ("k2", ctx_new[:, t % 4, :]), ("v2", ctx_new[:, t % 4, :]))[n]
                    if n == 0:
                        pe.wait_ge(xn_made, ln("b", t, i))
                    else:
                        pe.wait_ge(ctx_loaded[t % 4], DMA * (t // 4 + 1) + i * DMA)
                    pe.wait_ge(a_emptied, A.free((label, t), i))
                    nc.tensor.matmul(bank_a[:, :], w2[:, n, :], src, start=True, stop=True).then_inc(a_filled, 1)

                def turn_scores():
                    pe.wait_ge(g_emptied, G.done(("g1", m), i))
                    for n in range(2):
                        pe.wait_ge(s_emptied, S.free((f"dots{n}", m), i))
                        for c in range(2):
                            for half in range(2):
                                last = nc.tensor.transpose(S.bank((f"dots{n}", m))[:, (2 * c + half) * P:(2 * c + half + 1) * P],
                                                           scores_t[:, half, (2 * n + c) * P:(2 * n + c + 1) * P], ident[:, :])
                        last.then_inc(s_filled, 1)

                if is_tile(m - 2):
                    pe.wait_ge(wide_made, (m - 1 + i * U) * 4)
                for w in range(W):
                    if is_tile(m - 2):
                        label = (f"b{w}", m - 2)
                        pe.wait_ge(o_emptied, O.free(label, i))
                        for c in range(C):
                            last = nc.tensor.transpose(O.bank(label)[:, c * P:(c + 1) * P], wide[:, m % 2, c, w, :],
                                                       ident[:, :])
                        last.then_inc(o_filled, 1)
                    if is_tile(m):
                        if w % HALF == 0:
                            pe.wait_ge(g_emptied, G.free((f"g{w // HALF}", m), i))
                        if w in POOL_W:
                            n = m * NP + POOL_W.index(w)
                            pe.wait_ge(pool_prods_made, n + 1 + i * U * NP)
                            src = prods_pool[:, n % 3, :]
                        else:
                            n = m * ND + DVE_W.index(w)
                            pe.wait_ge(prods_made, n + 1 + i * U * ND)
                            src = prods[:, n % 4, :]
                        start = LAST - w % HALF * BH
                        nc.tensor.matmul(bank_g[:, :], head_sum[:, start:start + P], src, start=(w % HALF == 0),
                                         stop=(w % HALF == HALF - 1)).then_inc(prods_used, 1)
                    if is_tile(m - 2) and w % 4 == 2 and w >= 6:
                        project(w // 4 - 1)
                    if is_tile(m + 1):
                        if w == 4:
                            turn_x("a", m + 1)
                        if 6 <= w < 6 + C:
                            feed_forward("f1", "a", m + 1, w_f1, w - 6)
                    if is_tile(m - 3):
                        if w == 8:
                            turn_x("c", m - 3)
                        if w >= W - C:
                            feed_forward("f2", "c", m - 3, w_f2, w - (W - C))
                if is_tile(m + 1):
                    project_layer2(0)
                if is_tile(m):
                    turn_scores()
                if is_tile(m + 1):
                    project_layer2(1)
                if is_tile(m - 2):
                    project(FOURS - 1)
                if is_tile(m + 1):
                    project_layer2(2)

            for m in FILL:
                step(m, 0)
            with pe.Fori(0, TURNS) as i:
                for m in TURN:
                    step(m, i)
            for m in DRAIN:
                step(m, 0)

        @block.vector
        def _(dve):
            dve.sem_inc(s_emptied, 2)
            dve.sem_inc(o_emptied, 2)
            dve.sem_inc(y_emptied, 1)
            dve.sem_inc(f_emptied, 1)
            dve.wait_ge(fold_in, FOLD_LOADS * DMA)
            for n, r in enumerate((R0, R1)):
                mask = flags[n].bitcast(U8)
                for c in range(C):
                    nc.vector.tensor_tensor(masked[n][:, c], coefs[n][:, c], mask[:, c], ALU.mult).then_inc(masked_made, 1)
            dve.wait_ge(masked_made, 2 * C)
            for n, (lo, r) in enumerate(((0, R0), (R0, R1))):
                nc.vector.tensor_tensor(pair_sum[:, :, lo:lo + r], masked[n][:, :, 0], masked[n][:, :, 1], ALU.add)\
                    .then_inc(pair_made, 1)
            dve.wait_ge(pair_made, 2)
            for n, (lo, r) in enumerate(((0, R0), (R0, R1))):
                nc.vector.tensor_tensor(expert_sum[:, :, lo:lo + r], pair_sum[:, :, lo:lo + r], masked[n][:, :, 2], ALU.add)\
                    .then_inc(experts_made, 1)
            dve.wait_ge(w_in, LOADS * DMA)
            nc.vector.tensor_scalar(w_f2[:, :, :], signs_raw.bitcast(U8), 2.0, -1.0, ALU.mult, ALU.add).then_inc(signs_made, 1)
            dve.wait_ge(gated_made, 3)

            def step(m, i):
                def statistics(kind, t, x):
                    k = "abc".index(kind)
                    nc.vector.bn_stats(stats[:, k, :], x).then_inc(stats_made, 1)
                    dve.wait_ge(stats_made, ln(kind, t, i))
                    dve.sem_inc(gate, 1)
                    nc.vector.bn_aggr(mv[:, k, :], stats[:, k, :]).then_inc(mv_made, 1)

                def normalise(kind, t, x):
                    k = "abc".index(kind)
                    dve.wait_ge(rstd_made, ln(kind, t, i))
                    nc.vector.tensor_scalar(xn[kind][:, :], x, mv[:, k, 0:1], rstd[:, k:k + 1],
                                            ALU.subtract, ALU.mult).then_inc(xn_made, 1)

                def product(w):
                    n = m * ND + DVE_W.index(w)
                    if w == 0:
                        dve.wait_ge(a_emptied, A.done(("k2", m), i))
                    if n >= 4:
                        used, used_w = (n - 4) // ND, DVE_W[(n - 4) % ND]
                        dve.wait_ge(prods_used, (used + i * U) * W + used_w + 1)
                    nc.vector.tensor_tensor(prods[:, n % 4, :], q2[:, m % 2, :], k2[:, m % 2, w:w + D], ALU.mult)\
                        .then_inc(prods_made, 1)

                new, old, last = m + 1, m - 2, m - 3
                if is_tile(m):
                    product(0)
                    product(1)
                for w in range(W):
                    if is_tile(m) and w + 2 in DVE_W:
                        product(w + 2)
                    if is_tile(old):
                        label = (f"b{w}", old)
                        if w == 0:
                            dve.wait_ge(a_emptied, A.done(("v2", old), i))
                        if old > 0 or w >= 4:
                            dve.wait_ge(values_added, (old - 1 + (w + W - 4) // W) * ADDS + added((w - 4) % W) + i * U * ADDS)
                        dve.wait_ge(o_filled, O.full(label, i))
                        nc.vector.tensor_tensor(values[:, w % 4, :], O.bank(label)[:, :],
                                                v2[:, old % 4, w:w + D], ALU.mult).then_inc(o_emptied, 1)
                    if is_tile(m - 1):
                        t = m - 1
                        scores = [S.bank((f"dots{n}", t))[:, :].rearrange("p (c w b) -> p c b w", c=2, w=W) for n in range(2)]
                        if w < 4:
                            half = w // 2
                            count = (t + i * U) * 2 + half + 1
                            row = probs2[:, half].rearrange("p (c b) w -> p c b w", c=2)
                            most = neg_max2[:, half].rearrange("p (c b) -> p c b", c=2)
                            if w % 2 == 0:
                                dve.wait_ge(s_filled, S.full((f"dots{half}", t), i))
                                nc.vector.tensor_reduce(most, scores[half], AX_X, ALU.max, negate=True).then_inc(max2_made, 1)
                            else:
                                if t > 0 and half == 0:
                                    dve.wait_ge(wide_made, (t + i * U) * 4)
                                dve.wait_ge(max2_made, count)
                                nc.vector.tensor_tensor(row, scores[half], most.unsqueeze(3).to_broadcast([P, 2, BH, W]),
                                                        ALU.add).then_inc(s_emptied, 1)
                        half = w % 2
                        count = (t + i * U) * 2 + half + 1
                        if 4 <= w < 6:
                            dve.wait_ge(exp2_made, count)
                            nc.vector.tensor_reduce(sums2[:, half], probs2[:, half], AX_X, ALU.add).then_inc(sum2_made, 1)
                        if 6 <= w < 8:
                            dve.wait_ge(sum2_made, count)
                            nc.vector.reciprocal(inv2[:, half], sums2[:, half]).then_inc(inv2_made, 1)
                        if 8 <= w < 10:
                            dve.wait_ge(inv2_made, count)
                            nc.vector.tensor_tensor(probs2[:, half], probs2[:, half], along(inv2[:, half], W), ALU.mult)\
                                .then_inc(probs2_made, 1)
                    if is_tile(new):
                        x, y = x_a[:, new % 4, :], x_b[:, new % 4, :]
                        if w == 0:
                            dve.wait_ge(x_loaded[new % 4], DMA * (new // 4 + 1) + i * DMA)
                            statistics("a", new, x)
                        if w == 2:
                            normalise("a", new, x)
                        if w == 10:
                            dve.wait_ge(bias_added, biased("a", new, i))
                            dve.wait_ge(f_filled, F.full(("f1", new), i))
                            nc.vector.scalar_tensor_tensor(out=y, in0=bank_f[:, :], scalar=tgates[:, 0:1], in1=x,
                                                           op0=ALU.mult, op1=ALU.add).then_inc(f_emptied, 1)
                            dve.wait_ge(f_emptied, F.done(("f1", new), i))
                            dve.sem_inc(x_used, 1)
                            statistics("b", new, y)
                        if w == 12:
                            normalise("b", new, y)
                    if is_tile(last):
                        x = x_c[:, last % 2, :]
                        if w == 1:
                            dve.wait_ge(bias_added, biased("b", last, i))
                            dve.wait_ge(y_filled, Y.full(("y", last), i))
                            nc.vector.scalar_tensor_tensor(out=x, in0=bank_y[:, :], scalar=tgates[:, 1:2],
                                                           in1=x_b[:, last % 4, :], op0=ALU.mult, op1=ALU.add)\
                                .then_inc(y_emptied, 1)
                            dve.wait_ge(y_emptied, Y.done(("y", last), i))
                            statistics("c", last, x)
                        if w == 4:
                            normalise("c", last, x)
                if is_tile(last):
                    dve.wait_ge(x_stored[last % 4], 1 + DMA * (last // 4) + i * DMA)
                    dve.wait_ge(f_filled, F.full(("f2", last), i))
                    nc.vector.scalar_tensor_tensor(out=x_d[:, last % 4, :], in0=bank_f[:, :], scalar=f2_gate[:, 0:1],
                                                   in1=x_c[:, last % 2, :], op0=ALU.mult, op1=ALU.add).then_inc(f_emptied, 1)

            for m in FILL:
                step(m, 0)
            with dve.Fori(0, TURNS) as i:
                for m in TURN:
                    step(m, i)
            for m in DRAIN:
                step(m, 0)


UNUSED = ("L0_ffn_lut8",)


def flamingo_layers(nc, io, out):
    ctx_t = nc.dram_tensor("ctx_transposed", (TOKENS // 256, P, C, 256), F32, kind="Internal").ap()
    x_1 = nc.dram_tensor("x_after_layer_0", (TOKENS, D), F32, kind="Internal").ap()
    x_2 = nc.dram_tensor("x_after_latents", (TOKENS, D), F32, kind="Internal").ap()
    x_3 = nc.dram_tensor("x_after_layer_2", (TOKENS, D), F32, kind="Internal").ap()
    with ExitStack() as ctx:
        early = ctx.enter_context(nc.sbuf_tensor("early", [P, 4 * C * D], F32))
        cross_attention_and_quantised_ffn(nc, io, io["x"], io["ctx_4096"], x_1, ctx_t, early)
        latent_attention(nc, io, x_1, ctx_t, x_2, early)
    with ExitStack() as ctx:
        last_weights = LastWeights(nc, ctx)
        window_attention(nc, io, x_2, io["ctx_4096"], x_3, last_weights)
        last_layer(nc, io, x_3, ctx_t, out, last_weights)


def fourier_rows(n):
    import numpy as np
    j = np.arange(n)
    rows = np.empty((n, n))
    rows[0] = 1 / np.sqrt(n)
    for m in range(1, (n - 1) // 2 + 1):
        rows[2 * m - 1] = np.sqrt(2 / n) * np.cos(2 * np.pi * ((m * j) % n) / n)
        rows[2 * m] = np.sqrt(2 / n) * np.sin(2 * np.pi * ((m * j) % n) / n)
    if n % 2 == 0:
        rows[n - 1] = (-1.0) ** j / np.sqrt(n)
    return rows.astype(np.float32)


def kernel(**inputs):
    import numpy as np
    import concourse.bacc as bacc
    from concourse import mybir as mb
    from concourse.bass_utils import run_bass_kernel_spmd

    nc = bacc.Bacc("TRN2", target_bir_lowering=False, num_devices=1)
    arrays, io = {}, {}
    for name, value in inputs.items():
        if name in UNUSED:
            continue
        a = np.ascontiguousarray(value)
        if a.dtype == np.bool_:
            a = a.view(np.int32)
        if name in ("x", "ctx_4096"):
            a = a.reshape(TOKENS, D)
        if a.ndim == 0:
            a = a.reshape(1)
        arrays[f"in_{name}"] = a
        io[name] = nc.dram_tensor(f"in_{name}", a.shape, mb.dt.from_np(a.dtype), kind="ExternalInput").ap()
    arrays["in_fourier"] = fourier_rows(D)
    io["fourier"] = nc.dram_tensor("in_fourier", (D, D), mb.dt.float32, kind="ExternalInput").ap()
    out = nc.dram_tensor("out_x", (TOKENS, D), mb.dt.float32, kind="ExternalOutput").ap()
    flamingo_layers(nc, io, out)
    result = run_bass_kernel_spmd(nc, [arrays], core_ids=[0])
    return result.results[0]["out_x"].reshape(32, SEQ, D)
```

```python
from contextlib import ExitStack

import concourse.bass as bass
from concourse import mybir

F32 = mybir.dt.float32
I32 = mybir.dt.int32
U8 = mybir.dt.uint8
ALU = mybir.AluOpType
ACT = mybir.ActivationFunctionType
AX_X = mybir.AxisListType.X

P = 128
D = 512
C = D // P
TOKENS = 32 * 64
SEQ = 64
EPS = 1e-5
DMA = 16

KV = 8
HD = 16
REP = 4
ENTRY = 64


def heads_as_given(ap):
    return ap.rearrange("p (k r d) -> p k r d", k=KV, r=REP)


def heads_by_rep(ap):
    return ap.rearrange("p (r k d) -> p k r d", k=KV, r=REP)


class Banks:

    def __init__(self, banks, setup, loop):
        assert len(setup) % 2 == 0 and len(loop) % 2 == 0 and len(set(loop)) == len(loop)
        self.banks, self.setup, self.loop = banks, setup, loop

    def turn(self, i, label):
        if i is None:
            return self.setup.index(label)
        return len(self.setup) + i * len(self.loop) + self.loop.index(label)

    def free(self, i, label):
        return self.turn(i, label) + 1

    def full(self, i, label):
        return self.turn(i, label) + 1

    def done(self, i, label):
        return self.turn(i, label) + 3

    def bank(self, i, label):
        return self.banks[(self.setup if i is None else self.loop).index(label) % 2]


class Chip:

    def __init__(self, nc, ctx, phase):
        self.nc, self.ctx, self.phase = nc, ctx, phase
        self.sems = []
        ctx.callback(self.clear_semaphores)

    def clear_semaphores(self):
        self.nc.clear_and_free_semaphores(self.sems)
        self.nc.all_engine_barrier()

    def sb(self, name, shape, dtype=F32):
        return self.ctx.enter_context(self.nc.sbuf_tensor(f"{self.phase}_{name}", shape, dtype))

    def banks(self, name):
        return [self.ctx.enter_context(self.nc.psum_tensor(f"{self.phase}_{name}{n}", [P, D], F32))
                for n in range(2)]

    def sem(self, name):
        self.sems.append(self.nc.alloc_semaphore(f"{self.phase}_{name}"))
        return self.sems[-1]


def split4(ap):
    return ap.rearrange("p (c n) -> p c n", c=4)


class Region:

    def __init__(self, tensor):
        self.tensor, self.at = tensor, 0

    def carve(self, name, shape, dtype=F32):
        size = 1
        for n in shape[1:]:
            size *= n
        ap = self.tensor[0:shape[0], self.at:self.at + size]
        self.at += size
        assert self.at <= self.tensor.shape[1]
        if dtype != F32:
            ap = ap.bitcast(dtype)
        names = "abcd"[:len(shape) - 1]
        sizes = dict(zip(names[1:], shape[2:]))
        return ap if len(shape) == 2 else ap.rearrange(f"p ({' '.join(names)}) -> p {' '.join(names)}", **sizes)


def along(ap, n):
    return ap.unsqueeze(2).to_broadcast([ap.shape[0], ap.shape[1], n])


def turned(nc, out, src, ident):
    for c in range(C):
        last = nc.tensor.transpose(out[:, c * P:(c + 1) * P], src[:, c * P:(c + 1) * P], ident[:, :])
    return last


class HeadsOf16:

    def __init__(self, chip, batches, depth=3):
        sb, sem = chip.sb, chip.sem
        self.depth = depth
        T = batches * SEQ
        self.nc, self.B, self.UNITS, self.T = chip.nc, batches, 2 * batches, T
        self.kmask = sb("kmask", [P, KV])
        self.qt, self.kbd = sb("qt", [P, batches, REP, SEQ]), sb("kbd", [P, batches, KV, SEQ])
        self.vbd = sb("vbd", [P, batches, KV // 2, ENTRY])
        self.probs, self.probs_t = sb("probs", [P, depth, KV, SEQ]), sb("probs_t", [P, 2, KV // 2 * P])
        self.neg_max, self.inv_sum = sb("neg_max", [P, 2, KV]), sb("inv_sum", [P, 2, KV // 2, 2])
        self.o_tok, self.ot = sb("o_tok", [P, 2, KV // 2, 2, HD]), sb("ot", [P, REP, T])
        self.s_filled, self.s_emptied = sem("s_filled"), sem("s_emptied")
        self.o_filled, self.o_emptied = sem("o_filled"), sem("o_emptied")
        self.max_made, self.exp_made, self.inv_made = sem("max_made"), sem("exp_made"), sem("inv_made")

    def order(self, steps):
        s_labels = [f"s{u}" for u in range(self.UNITS)]
        o_labels = []
        for s in range(steps):
            if 0 <= s - 3 < self.UNITS:
                o_labels.append(f"av{s - 3}")
            if 0 <= s - 4 < self.UNITS:
                o_labels.append(f"ot{s - 4}")
        return s_labels, o_labels

    def make_masks(self, pool, cleared, made):
        nc = self.nc
        nc.gpsimd.memset(self.kmask[:, :], 1.0).then_inc(cleared, 1)
        nc.gpsimd.memset(self.vbd[:, :, :, :], 0.0).then_inc(cleared, 1)
        pool.wait_ge(cleared, 2)
        nc.gpsimd.affine_select(out=self.kmask[:, :], in_=self.kmask[:, :], compare_op=ALU.is_ge, fill=0.0,
                                base=0, pattern=[[-HD, KV]], channel_multiplier=1).then_inc(made, 1)
        for half in range(2):
            rows = slice(half * SEQ, (half + 1) * SEQ)
            pool.wait_ge(made, 1 + half)
            nc.gpsimd.memset(self.vbd[rows, :, :, 2 * HD + half:2 * HD + half + 1], 1.0).then_inc(made, 1)
        pool.wait_ge(made, 3)
        nc.gpsimd.affine_select(out=self.kmask[:, :], in_=self.kmask[:, :], compare_op=ALU.is_ge, fill=0.0,
                                base=HD - 1, pattern=[[HD, KV]], channel_multiplier=-1).then_inc(made, 1)


    def pe_keys(self, out, wk, ctxt):
        for c in range(C):
            last = self.nc.tensor.matmul(out[:, :], wk[:, c, :], ctxt[:, c, :], start=(c == 0), stop=(c == C - 1))
        return last

    def pe_values_in(self, out, wv, ctxt):
        for t in range(self.T // P):
            for c in range(C):
                last = self.nc.tensor.matmul(out[:, t * P:(t + 1) * P], ctxt[:, c, t * P:(t + 1) * P], wv[:, c, :],
                                             start=(c == 0), stop=(c == C - 1))
        return last

    def pe_queries(self, out, wq, xnt, r):
        for c in range(C):
            last = self.nc.tensor.matmul(out[:, :], wq[:, c, r * P:(r + 1) * P], xnt[:, c, :],
                                         start=(c == 0), stop=(c == C - 1))
        return last

    def pe_scores(self, out, u):
        b, j = u // 2, u % 2
        return self.nc.tensor.matmul(out[:, :], self.qt[:, b, 2 * j:2 * j + 2, :].rearrange("p r s -> p (r s)"),
                                     self.kbd[:, b, :, :], start=True, stop=True)

    def pe_turn_probs(self, out, u, ident):
        return turned(self.nc, out, self.probs[:, u % self.depth].rearrange("p k s -> p (k s)"), ident)

    def pe_attend(self, out, u):
        for p in range(KV // 2):
            last = self.nc.tensor.matmul(out[:, p * ENTRY:(p + 1) * ENTRY], self.probs_t[:, u % 2, p * P:(p + 1) * P],
                                         self.vbd[:, u // 2, p, :], start=True, stop=True)
        return last

    def pe_turn_back(self, out, u, ident):
        return self.nc.tensor.transpose(out[:, 0:P], self.o_tok[:, u % 2].rearrange("p a b d -> p (a b d)"),
                                        ident[:, :])

    def pe_project(self, out, t, wo):
        for r in range(REP):
            last = self.nc.tensor.matmul(out[:, :], self.ot[:, r, t * P:(t + 1) * P], wo[:, r, :],
                                         start=(r == 0), stop=(r == REP - 1))
        return last


    def dve_spread_keys(self, bank, bk=None):
        for b in range(self.B):
            keys = bank[:, b * SEQ:(b + 1) * SEQ].unsqueeze(1).to_broadcast([P, KV, SEQ])
            mask, out = along(self.kmask[:, :], SEQ), self.kbd[:, b, :, :]
            if bk is None:
                last = self.nc.vector.tensor_tensor(out, keys, mask, ALU.mult)
            else:
                last = self.nc.vector.scalar_tensor_tensor(out=out, in0=keys, scalar=bk, in1=mask,
                                                           op0=ALU.add, op1=ALU.mult)
        return last

    def dve_spread_values(self, bank, bv=None):
        values = bank[:, :].rearrange("p (t a h d) -> p t a h d", a=KV // 2, h=2, d=HD)
        vbd = self.vbd[:, :, :, :].rearrange("p (t b) a e -> p t b a e", b=2)
        for b in range(2):
            keys = slice(b * SEQ, (b + 1) * SEQ)
            for h in range(2):
                for t in range(self.T // P):
                    out = vbd[h * SEQ:(h + 1) * SEQ, t, b, :, h * HD:(h + 1) * HD]
                    if bv is None:
                        last = self.nc.vector.tensor_copy(out, values[keys, t, :, h, :])
                    else:
                        last = self.nc.vector.tensor_tensor(out, values[keys, t, :, h, :], bv[keys, :, h, :], ALU.add)
        return last

    def dve_max(self, bank, u):
        return self.nc.vector.tensor_reduce(self.neg_max[:, u % 2, :], bank[:, :].rearrange("p (k s) -> p k s", k=KV),
                                            AX_X, ALU.max, negate=True)

    def dve_shift(self, bank, u):
        return self.nc.vector.tensor_tensor(self.probs[:, u % self.depth], bank[:, :].rearrange("p (k s) -> p k s", k=KV),
                                            along(self.neg_max[:, u % 2, :], SEQ), ALU.add)

    def dve_inverse(self, bank, u):
        sums = bank[:, 0:KV // 2 * ENTRY].rearrange("p (a e) -> p a e", e=ENTRY)[:, :, 2 * HD:2 * HD + 2]
        return self.nc.vector.reciprocal(self.inv_sum[:, u % 2], sums)

    def dve_norm(self, bank, u):
        values = bank[:, 0:KV // 2 * ENTRY].rearrange("p (a e) -> p a e", e=ENTRY)
        for h in range(2):
            last = self.nc.vector.tensor_tensor(self.o_tok[:, u % 2, :, h, :], values[:, :, h * HD:(h + 1) * HD],
                                                along(self.inv_sum[:, u % 2, :, h], HD), ALU.mult)
        return last

    def dve_copy_back(self, bank, u):
        b, j = u // 2, u % 2
        return self.nc.vector.tensor_copy(self.ot[:, 2 * j:2 * j + 2, b * SEQ:(b + 1) * SEQ],
                                          bank[:, 0:P].rearrange("p (r s) -> p r s", r=2))


    def act_exp(self, u):
        return self.nc.scalar.activation(self.probs[:, u % self.depth], self.probs[:, u % self.depth], ACT.Exp, scale=HD ** -0.5)


class Ring:

    def __init__(self, banks, order, loop_labels, tiles_per_turn):
        self.banks, self.order = banks, order
        first, last = order.index(loop_labels[0]), order.index(loop_labels[-1])
        self.per_turn = last - first + 1
        assert self.per_turn % len(banks) == 0
        for name, t in loop_labels:
            assert order.index((name, t + tiles_per_turn)) == order.index((name, t)) + self.per_turn

    def turn(self, label, shift):
        return self.order.index(label) + self.per_turn * shift

    def free(self, label, shift=0):
        return self.turn(label, shift) + 1

    def full(self, label, shift=0):
        return self.turn(label, shift) + 1

    def done(self, label, shift=0):
        return self.turn(label, shift) + len(self.banks) + 1

    def bank(self, label):
        return self.banks[self.order.index(label) % len(self.banks)]


def cross_attention_and_quantised_ffn(nc, io, x_in, ctx_in, x_out, ctx_t_out, early):
    TILES = TOKENS // P
    SLOTS = 4
    U = 4
    TURNS = (TILES - 2 - 4) // U
    FILL, TURN, DRAIN = range(-2, 4), range(4, 4 + U), range(4 + U * TURNS, TILES + 4)
    ALL = range(-2, TILES + 4)
    ENTRIES = 16

    def is_tile(t):
        return 0 <= t < TILES

    def in_order(steps, parts):
        return [(name, m + off) for m in steps for name, off in parts if is_tile(m + off)]

    def unit(m, j, back):
        return (SLOTS * m + j - back) // SLOTS, (SLOTS * m + j - back) % SLOTS

    A_PARTS = [("pt2", -1), ("xe", -3), ("ctx", 1), ("pt3", -1), ("xd", 1), ("pt0", 0), ("q", 1), ("pt1", 0)]
    D_PARTS = [("out", -2), ("kv", 1), ("ffn", -3)]
    S_PARTS = [(f"s{j}", 0) for j in range(SLOTS)]
    O_PARTS = [("av1", -1), ("ot0", -1), ("av2", -1), ("ot1", -1), ("av3", -1), ("ot2", -1), ("av0", 0), ("ot3", -1)]
    LN_PARTS = [("e", -2), ("d", 2)]
    CHAIN = {"d": 6, "e": 1}

    with ExitStack() as ctx:
        chip = Chip(nc, ctx, "l0")
        sb, sem = chip.sb, chip.sem
        heads = HeadsOf16(chip, 4, depth=4)
        a_setup = [("wq", c) for c in range(C)] + [("wk", 0), ("wv", 0)] + [("wo", r) for r in range(REP)] + \
                  [("lut", o) for o in range(C)]
        A = Ring(chip.banks("bank_a"), a_setup + in_order(ALL, A_PARTS), in_order(TURN, A_PARTS), U)
        Dr = Ring(chip.banks("bank_d"), in_order(ALL, D_PARTS), in_order(TURN, D_PARTS), U)
        S = Ring(chip.banks("bank_s"), in_order(ALL, S_PARTS), in_order(TURN, S_PARTS), U)
        O = Ring(chip.banks("bank_o"), in_order(ALL, O_PARTS), in_order(TURN, O_PARTS), U)
        ln_order = in_order(ALL, LN_PARTS)

        def ln(kind, t, i):
            return ln_order.index((kind, t)) + 1 + i * U * len(LN_PARTS)

        def chained(kind, t, i):
            return sum(CHAIN[k] for k, _ in ln_order[:ln_order.index((kind, t))]) + i * U * sum(CHAIN.values())

        def units(t, j, i):
            return t * SLOTS + j + 1 + i * U * SLOTS

        x_tiles = x_in.rearrange("(t p) d -> t p d", p=P)
        ctx_tiles = ctx_in.rearrange("(t p) d -> t p d", p=P)
        out_tiles = x_out.rearrange("(t p) d -> t p d", p=P)

        ident = sb("ident", [P, P])
        x_c, wo_raw = sb("x_c", [P, 4, D]), sb("wo_raw", [P, C, D])
        wq_raw = x_c
        wk_raw, wv_raw = sb("wk_raw", [P, D]), sb("wv_raw", [P, D])
        wq, wo = sb("wq", [P, C, D]), sb("wo", [P, REP, D])
        wk, wv = sb("wk", [P, C, P]), sb("wv", [P, C, P])
        w_low = sb("w_low", [P, C, D])
        wo_by_rep = sb("wo_by_rep", [P, C, D])
        ln_w = sb("ln_w", [P, C])
        gates, tgates = sb("gates", [P, 2]), sb("tgates", [P, 2])
        bias, gated_bias = sb("bias", [P, D]), sb("gated_bias", [P, D])
        planes = sb("planes", [P, 4, C * 16], I32)
        lut = sb("lut", [P, C, ENTRIES])
        bits = Region(early).carve("bits", [P, 4, C * 16, 32], I32)
        codes = sb("codes", [P, C * D])
        picked = sb("picked", [P, 4, D])
        eps_col, half_col = sb("eps_col", [P, 1]), sb("half_col", [P, 1])
        x_ln, x_a, x_b = sb("x_ln", [P, 4, D]), sb("x_a", [P, 4, D]), sb("x_b", [P, 4, D])
        ctx_new, ctxt = sb("ctx_new", [P, 4, D]), sb("ctxt", [P, 4, C, P])
        xn = {kind: sb(f"xn_{kind}", [P, D]) for kind in "de"}
        xnt = {kind: sb(f"xnt_{kind}", [P, C, P]) for kind in "de"}
        stats, mv = sb("stats", [P, 2, 6]), sb("mv", [P, 2, 2])
        small, rstd = sb("small", [P, 2, 6]), sb("rstd", [P, 2])

        weights_in, quant_in, small_in = sem("weights_in"), sem("quant_in"), sem("small_in")
        ln_loaded, a_loaded, ctx_loaded = ([sem(f"{name}_loaded{t}") for t in range(4)] for name in ("ln", "a", "ctx"))
        ln_used, a_used, ctx_used = sem("ln_used"), sem("a_used"), sem("ctx_used")
        x_stored, ctx_stored = [sem(f"x_stored{t}") for t in range(4)], [sem(f"ctx_stored{t}") for t in range(4)]
        cleared, consts_made, masks_made = sem("cleared"), sem("consts_made"), sem("masks_made")
        wo_ordered = sem("wo_ordered")
        gates_ready, gated_bias_made = sem("gates_ready"), sem("gated_bias_made")
        bits_made, codes_made, early_in = sem("bits_made"), sem("codes_made"), sem("early_in")
        picked_made, picked_used = sem("picked_made"), sem("picked_used")
        a_filled, a_emptied = sem("a_filled"), sem("a_emptied")
        d_filled, d_emptied = sem("d_filled"), sem("d_emptied")
        s_filled, s_emptied, o_filled, o_emptied = heads.s_filled, heads.s_emptied, heads.o_filled, heads.o_emptied
        stats_made, mv_made, rstd_step, rstd_made = sem("stats_made"), sem("mv_made"), sem("rstd_step"), sem("rstd_made")
        xn_made, bias_added = sem("xn_made"), sem("bias_added")
        gate = sem("gate")

        block = ctx.enter_context(nc.Block())

        @block.sync
        def _(sp):
            sp.dma_start(wq_raw[:, :, :], io["L0_xattn_wq"].rearrange("(c p) d -> p c d", p=P)).then_inc(weights_in, DMA)
            sp.dma_start(wk_raw[:, :], io["L0_xattn_wk"]).then_inc(weights_in, DMA)
            sp.dma_start(wv_raw[:, :], io["L0_xattn_wv"]).then_inc(weights_in, DMA)
            sp.dma_start(wo_raw[:, :, :], io["L0_xattn_wo"].rearrange("(c p) d -> p c d", p=P)).then_inc(weights_in, DMA)
            for t in range(4):
                sp.dma_start(x_ln[:, t, :], x_tiles[t]).then_inc(ln_loaded[t], DMA)
                sp.dma_start(ctx_new[:, t, :], ctx_tiles[t]).then_inc(ctx_loaded[t], DMA)
            for t in range(4):
                sp.dma_start(x_a[:, t, :], x_tiles[t]).then_inc(a_loaded[t], DMA)
            with sp.Fori(0, TILES // 4 - 1) as i:
                for t in range(4):
                    sp.wait_ge(ln_used, i * 4 + t + 1)
                    sp.dma_start(x_ln[:, t, :], x_tiles[i * 4 + 4 + t]).then_inc(ln_loaded[t], DMA)
                    sp.wait_ge(ctx_used, i * 4 + t + 1)
                    sp.dma_start(ctx_new[:, t, :], ctx_tiles[i * 4 + 4 + t]).then_inc(ctx_loaded[t], DMA)
                    sp.wait_ge(a_used, i * 4 + t + 1)
                    sp.dma_start(x_a[:, t, :], x_tiles[i * 4 + 4 + t]).then_inc(a_loaded[t], DMA)
            sp.wait_ge(codes_made, 3)
            loads = early_latent_weights(io, early)
            for out, src in loads:
                sp.dma_start(out, src).then_inc(early_in, DMA)
            sp.wait_ge(early_in, DMA * len(loads))
            for t in range(4):
                sp.wait_ge(x_stored[t], 1 + DMA * TILES // 4)
                sp.wait_ge(ctx_stored[t], 1 + DMA * TILES // 4)

        @block.gpsimd
        def _(pool):
            nc.gpsimd.memset(ident[:, :], 0.0).then_inc(consts_made, 1)
            nc.gpsimd.memset(eps_col[:, :], EPS).then_inc(consts_made, 1)
            nc.gpsimd.memset(half_col[:, :], -0.5).then_inc(consts_made, 1)
            pool.wait_ge(consts_made, 3)
            nc.gpsimd.affine_select(out=ident[:, :], in_=ident[:, :], compare_op=ALU.not_equal, fill=1.0,
                                    base=0, pattern=[[-1, P]], channel_multiplier=1).then_inc(consts_made, 1)
            heads.make_masks(pool, cleared, masks_made)
            pool.wait_ge(weights_in, 4 * DMA)
            for o in range(C):
                for r in range(REP):
                    nc.gpsimd.tensor_copy(heads_by_rep(wo_by_rep[:, o, :])[:, :, r, :],
                                          heads_as_given(wo_raw[:, o, :])[:, :, r, :]).then_inc(wo_ordered, 1)
            pool.wait_ge(small_in, 4 * DMA)
            pool.wait_ge(gates_ready, 1)
            nc.gpsimd.tensor_tensor(gated_bias[:, :], bias[:, :], tgates[:, 1:2].to_broadcast([P, D]), ALU.mult)\
                .then_inc(gated_bias_made, 1)
            pool.wait_ge(gated_bias_made, 1)

            def step(m, i):
                if is_tile(m - 2):
                    t = m - 2
                    pool.wait_ge(mv_made, ln("e", t, i))
                    nc.gpsimd.tensor_tensor(small[:, 1, 0:1], mv[:, 1, 1:2], eps_col[:, :], ALU.add).then_inc(rstd_step, 1)
                    pool.wait_ge(rstd_step, chained("e", t, i) + 1)
                    nc.gpsimd.tensor_tensor(rstd[:, 1:2], small[:, 1, 0:1], half_col[:, :], ALU.pow).then_inc(rstd_made, 1)
                if is_tile(m + 2):
                    t = m + 2
                    s = [small[:, 0, k:k + 1] for k in range(6)]
                    var = mv[:, 0, 1:2]
                    chain = [(s[0], var, eps_col[:, :], ALU.add), (s[1], s[0], half_col[:, :], ALU.pow),
                             (s[2], s[1], s[1], ALU.mult), (s[3], s[2], var, ALU.mult),
                             (s[4], s[3], eps_col[:, :], ALU.add), (s[5], s[4], half_col[:, :], ALU.pow)]
                    pool.wait_ge(mv_made, ln("d", t, i))
                    for n, (out, in0, in1, op) in enumerate(chain):
                        if n:
                            pool.wait_ge(rstd_step, chained("d", t, i) + n)
                        nc.gpsimd.tensor_tensor(out, in0, in1, op).then_inc(rstd_step, 1)
                    pool.wait_ge(rstd_step, chained("d", t, i) + len(chain))
                    nc.gpsimd.tensor_tensor(rstd[:, 0:1], s[1], s[5], ALU.mult).then_inc(rstd_made, 1)
                if is_tile(m - 2):
                    pool.wait_ge(xn_made, ln("e", m - 2, i))
                    nc.gpsimd.tensor_tensor(x_b[:, (m - 2) % 4, :], x_b[:, (m - 2) % 4, :], gated_bias[:, :], ALU.add)\
                        .then_inc(bias_added, 1)

            for m in FILL:
                step(m, 0)
            with pool.Fori(0, TURNS) as i:
                for m in TURN:
                    step(m, i)
            for m in DRAIN:
                step(m, 0)

        @block.scalar
        def _(act):
            act.dma_start(gates[:, 0:1], io["g_xattn"][0:1].partition_broadcast(P)).then_inc(small_in, DMA)
            act.dma_start(gates[:, 1:2], io["g_ffn"][0:1].partition_broadcast(P)).then_inc(small_in, DMA)
            act.dma_start(bias[:, :], io["L0_ffn_bias"].partition_broadcast(P)).then_inc(small_in, DMA)
            act.dma_start(ln_w[:, :], io["L0_xattn_ln_w"].rearrange("(c p) -> p c", p=P),
                          allow_slow_non_contiguous=True).then_inc(small_in, DMA)
            act.dma_start(lut[:, :, :], io["L0_ffn_lut4"].rearrange("(o p) e -> p o e", p=P)).then_inc(quant_in, DMA)
            for n in range(4):
                act.dma_start(planes[:, n, :].rearrange("p (o w) -> p o w", o=C),
                              io["L0_ffn_qweight"][n].rearrange("(o p) w -> p o w", p=P)).then_inc(quant_in, DMA)
            act.sem_inc(a_emptied, 2)
            for t in range(4):
                act.sem_inc(x_stored[t], 1)
                act.sem_inc(ctx_stored[t], 1)
            act.wait_ge(small_in, 4 * DMA)
            nc.scalar.activation(tgates[:, :], gates[:, :], ACT.Tanh).then_inc(gates_ready, 1)
            for c in range(C):
                act.wait_ge(a_filled, A.full(("wq", c)))
                nc.scalar.activation(heads_by_rep(wq[:, c, :]), heads_as_given(A.bank(("wq", c))[:, :]),
                                     ACT.Copy, scale=ln_w[:, c:c + 1])\
                    .then_inc(a_emptied, 1)
            for label, w in (("wk", wk), ("wv", wv)):
                act.wait_ge(a_filled, A.full((label, 0)))
                nc.scalar.activation(w[:, :, :], split4(A.bank((label, 0))[:, :]), ACT.Copy).then_inc(a_emptied, 1)
            for r in range(REP):
                act.wait_ge(a_filled, A.full(("wo", r)))
                nc.scalar.activation(wo[:, r, :], A.bank(("wo", r))[:, :], ACT.Copy).then_inc(a_emptied, 1)
            for o in range(C):
                act.wait_ge(a_filled, A.full(("lut", o)))
                nc.scalar.activation(w_low[:, :, o * P:(o + 1) * P], split4(A.bank(("lut", o))[:, :]), ACT.Copy)\
                    .then_inc(a_emptied, 1)

            def step(m, i):
                def empty(label, out):
                    act.wait_ge(a_filled, A.full(label, i))
                    src = A.bank(label)[:, :]
                    nc.scalar.activation(out, split4(src) if len(out.shape) == 3 else src, ACT.Copy).then_inc(a_emptied, 1)

                for j in range(SLOTS):
                    t, n = unit(m, j, 1)
                    if is_tile(t):
                        act.wait_ge(s_emptied, S.done((f"s{n}", t), i))
                        heads.act_exp(SLOTS * (t % 2) + n).then_inc(heads.exp_made, 1)
                    t, n = unit(m, j, 2)
                    if is_tile(t):
                        empty((f"pt{n}", t), heads.probs_t[:, n % 2])
                    if j == 0 and is_tile(m - 3):
                        empty(("xe", m - 3), xnt["e"][:, :, :])
                    if j == 0 and is_tile(m + 1):
                        t = m + 1
                        act.wait_ge(ctx_stored[t % 4], 1 + DMA * (t // 4) + i * DMA)
                        empty(("ctx", t), ctxt[:, t % 4])
                        act.sem_inc(ctx_used, 1)
                        act.wait_ge(a_emptied, A.done(("ctx", t), i))
                        act.dma_start(ctx_t_out[t // 2 + i * 2][:, :, t % 2 * P:(t % 2 + 1) * P], ctxt[:, t % 4])\
                           .then_inc(ctx_stored[t % 4], DMA)
                    if j == 1 and is_tile(m + 1):
                        empty(("xd", m + 1), xnt["d"][:, :, :])
                    if j == 2 and is_tile(m + 1):
                        t = m + 1
                        act.wait_ge(a_filled, A.full(("q", t), i))
                        src = A.bank(("q", t))[:, :].rearrange("p (r b s) -> p b r s", r=REP, b=2)
                        for b in range(2):
                            last = nc.scalar.activation(heads.qt[:, t % 2 * 2 + b], src[:, b], ACT.Copy)
                        last.then_inc(a_emptied, 1)
                if is_tile(m - 4):
                    t = m - 4
                    act.wait_ge(d_emptied, Dr.done(("ffn", t), i))
                    act.dma_start(out_tiles[t + i * U], x_c[:, t % 4, :]).then_inc(x_stored[t % 4], DMA)

            for m in FILL:
                step(m, 0)
            with act.Fori(0, TURNS) as i:
                for m in TURN:
                    step(m, i)
            for m in DRAIN:
                step(m, 0)

        @block.tensor
        def _(pe):
            pe.wait_ge(consts_made, 4)
            pe.wait_ge(weights_in, 4 * DMA)
            for c in range(C):
                pe.wait_ge(a_emptied, A.free(("wq", c)))
                out = A.bank(("wq", c))
                for h in range(C):
                    last = nc.tensor.transpose(out[:, h * P:(h + 1) * P], wq_raw[:, h, c * P:(c + 1) * P], ident[:, :])
                last.then_inc(a_filled, 1)
            for label, raw in (("wk", wk_raw), ("wv", wv_raw)):
                pe.wait_ge(a_emptied, A.free((label, 0)))
                turned(nc, A.bank((label, 0)), raw, ident).then_inc(a_filled, 1)
            for r in range(REP):
                pe.wait_ge(a_emptied, A.free(("wo", r)))
                out = A.bank(("wo", r))
                pe.wait_ge(wo_ordered, C * REP)
                for o in range(C):
                    last = nc.tensor.transpose(out[:, o * P:(o + 1) * P], wo_by_rep[:, o, r * P:(r + 1) * P], ident[:, :])
                last.then_inc(a_filled, 1)
            for o in range(C):
                pe.wait_ge(a_emptied, A.free(("lut", o)))
                out = A.bank(("lut", o))
                for e in range(ENTRIES):
                    n = ENTRIES * o + e
                    pe.wait_ge(picked_made, n + 1)
                    for c in range(C):
                        last = nc.tensor.matmul(out[:, c * P:(c + 1) * P], picked[:, n % 4, c * P:(c + 1) * P],
                                                ident[:, :], start=(e == 0 and c == 0), stop=(e == ENTRIES - 1),
                                                skip_group_check=True)
                    last.then_inc(picked_used if e < ENTRIES - 1 else a_filled, 1)

            pe.wait_ge(masks_made, 4)

            def step(m, i):
                def turn_x(kind, t):
                    pe.wait_ge(xn_made, ln(kind, t, i))
                    pe.wait_ge(a_emptied, A.free((f"x{kind}", t), i))
                    turned(nc, A.bank((f"x{kind}", t)), xn[kind][:, :], ident).then_inc(a_filled, 1)

                for j in range(SLOTS):
                    if is_tile(m):
                        if j == 0:
                            pe.wait_ge(a_emptied, A.done(("q", m), i))
                            pe.wait_ge(d_emptied, Dr.done(("kv", m), i))
                        label = (f"s{j}", m)
                        pe.wait_ge(s_emptied, S.free(label, i))
                        heads.pe_scores(S.bank(label), SLOTS * (m % 2) + j).then_inc(s_filled, 1)
                    t, n = unit(m, j, 2)
                    if is_tile(t):
                        label = (f"pt{n}", t)
                        pe.wait_ge(heads.exp_made, units(t, n, i))
                        pe.wait_ge(a_emptied, A.free(label, i))
                        heads.pe_turn_probs(A.bank(label), SLOTS * (t % 2) + n, ident).then_inc(a_filled, 1)
                    t, n = unit(m, j, 3)
                    if is_tile(t):
                        pe.wait_ge(a_emptied, A.done((f"pt{n}", t), i))
                        pe.wait_ge(o_emptied, O.free((f"av{n}", t), i))
                        heads.pe_attend(O.bank((f"av{n}", t)), SLOTS * (t % 2) + n).then_inc(o_filled, 1)
                    t, n = unit(m, j, 4)
                    if is_tile(t):
                        pe.wait_ge(o_emptied, O.done((f"av{n}", t), i))
                        pe.wait_ge(o_emptied, O.free((f"ot{n}", t), i))
                        heads.pe_turn_back(O.bank((f"ot{n}", t)), SLOTS * (t % 2) + n, ident).then_inc(o_filled, 1)
                    if j == 0 and is_tile(m - 3):
                        turn_x("e", m - 3)
                    if j == 0 and is_tile(m + 1):
                        t = m + 1
                        pe.wait_ge(ctx_loaded[t % 4], DMA * (t // 4 + 1) + i * DMA)
                        pe.wait_ge(a_emptied, A.free(("ctx", t), i))
                        turned(nc, A.bank(("ctx", t)), ctx_new[:, t % 4, :], ident).then_inc(a_filled, 1)
                    if j == 1 and is_tile(m - 2):
                        t = m - 2
                        pe.wait_ge(o_emptied, O.done(("ot3", t), i))
                        pe.wait_ge(d_emptied, Dr.free(("out", t), i))
                        heads.pe_project(Dr.bank(("out", t)), t % 2, wo).then_inc(d_filled, 1)
                    if j == 1 and is_tile(m + 1):
                        turn_x("d", m + 1)
                    if j == 2 and is_tile(m + 1):
                        t = m + 1
                        pe.wait_ge(a_emptied, A.done(("ctx", t), i))
                        pe.wait_ge(d_emptied, Dr.free(("kv", t), i))
                        out = Dr.bank(("kv", t))
                        for c in range(C):
                            nc.tensor.matmul(out[:, 0:P], wk[:, c, :], ctxt[:, t % 4, c, :], start=(c == 0), stop=(c == C - 1))
                        for c in range(C):
                            last = nc.tensor.matmul(out[:, P:2 * P], ctxt[:, t % 4, c, :], wv[:, c, :],
                                                    start=(c == 0), stop=(c == C - 1))
                        last.then_inc(d_filled, 1)
                        pe.wait_ge(a_emptied, A.done(("xd", t), i))
                        pe.wait_ge(a_emptied, A.free(("q", t), i))
                        for r in range(REP):
                            for c in range(C):
                                last = nc.tensor.matmul(A.bank(("q", t))[:, r * P:(r + 1) * P], wq[:, c, r * P:(r + 1) * P],
                                                        xnt["d"][:, c, :], start=(c == 0), stop=(c == C - 1))
                        last.then_inc(a_filled, 1)
                    if j == 3 and is_tile(m - 3):
                        t = m - 3
                        pe.wait_ge(a_emptied, A.done(("xe", t), i))
                        pe.wait_ge(d_emptied, Dr.free(("ffn", t), i))
                        for c in range(C):
                            last = nc.tensor.matmul(Dr.bank(("ffn", t))[:, :], xnt["e"][:, c, :], w_low[:, c, :],
                                                    start=(c == 0), stop=(c == C - 1))
                        last.then_inc(d_filled, 1)

            for m in FILL:
                step(m, 0)
            with pe.Fori(0, TURNS) as i:
                for m in TURN:
                    step(m, i)
            for m in DRAIN:
                step(m, 0)

        @block.vector
        def _(dve):
            for emptied in (d_emptied, s_emptied, o_emptied):
                dve.sem_inc(emptied, 2)
            dve.wait_ge(quant_in, 5 * DMA)
            for s in range(32):
                nc.vector.tensor_scalar(bits[:, :, :, s], planes[:, :, :], s, 1,
                                        ALU.logical_shift_right, ALU.bitwise_and).then_inc(bits_made, 1)
            dve.wait_ge(bits_made, 32)
            plane = [bits[:, n].rearrange("p w s -> p (w s)") for n in range(4)]
            nc.vector.scalar_tensor_tensor(out=codes[:, :], in0=plane[3], scalar=2.0, in1=plane[2],
                                           op0=ALU.mult, op1=ALU.add).then_inc(codes_made, 1)
            for n in (1, 0):
                dve.wait_ge(codes_made, 2 - n)
                nc.vector.scalar_tensor_tensor(out=codes[:, :], in0=codes[:, :], scalar=2.0, in1=plane[n],
                                               op0=ALU.mult, op1=ALU.add).then_inc(codes_made, 1)
            dve.wait_ge(codes_made, 3)
            for o in range(C):
                for e in range(ENTRIES):
                    n = ENTRIES * o + e
                    if n >= 4:
                        used = n - 4
                        if used % ENTRIES == ENTRIES - 1:
                            dve.wait_ge(a_filled, A.full(("lut", used // ENTRIES)))
                        else:
                            dve.wait_ge(picked_used, used - used // ENTRIES + 1)
                    nc.vector.tensor_scalar(picked[:, n % 4, :], codes[:, o * D:(o + 1) * D], float(e),
                                            lut[:, o, e:e + 1], ALU.is_equal, ALU.mult).then_inc(picked_made, 1)
            dve.wait_ge(masks_made, 4)
            dve.wait_ge(gates_ready, 1)

            def step(m, i):
                def statistics(kind, t, x):
                    k = "de".index(kind)
                    nc.vector.bn_stats(stats[:, k, :], x).then_inc(stats_made, 1)
                    dve.wait_ge(stats_made, ln(kind, t, i))
                    dve.sem_inc(gate, 1)
                    nc.vector.bn_aggr(mv[:, k, :], stats[:, k, :]).then_inc(mv_made, 1)

                def normalise(kind, t, x):
                    k = "de".index(kind)
                    dve.wait_ge(rstd_made, ln(kind, t, i))
                    nc.vector.tensor_scalar(xn[kind][:, :], x, mv[:, k, 0:1], rstd[:, k:k + 1],
                                            ALU.subtract, ALU.mult).then_inc(xn_made, 1)

                def spread_keys_and_values(t):
                    bank = Dr.bank(("kv", t))
                    dve.wait_ge(d_filled, Dr.full(("kv", t), i))
                    for b in range(2):
                        keys = bank[:, b * SEQ:(b + 1) * SEQ].unsqueeze(1).to_broadcast([P, KV, SEQ])
                        nc.vector.tensor_tensor(heads.kbd[:, t % 2 * 2 + b, :, :], keys, along(heads.kmask[:, :], SEQ), ALU.mult)
                    values = bank[:, P:2 * P].rearrange("p (a h d) -> p a h d", a=KV // 2, h=2, d=HD)
                    for b in range(2):
                        rows = slice(b * SEQ, (b + 1) * SEQ)
                        for h in range(2):
                            out = heads.vbd[h * SEQ:(h + 1) * SEQ, t % 2 * 2 + b, :, h * HD:(h + 1) * HD]
                            last = nc.vector.tensor_copy(out, values[rows, :, h, :])
                    last.then_inc(d_emptied, 1)

                for j in range(SLOTS):
                    if is_tile(m):
                        label, u = (f"s{j}", m), SLOTS * (m % 2) + j
                        dve.wait_ge(s_filled, S.full(label, i))
                        heads.dve_max(S.bank(label), u).then_inc(heads.max_made, 1)
                    t, n = unit(m, j, 3)
                    if is_tile(t):
                        dve.wait_ge(o_filled, O.full((f"av{n}", t), i))
                        heads.dve_inverse(O.bank((f"av{n}", t)), n).then_inc(heads.inv_made, 1)
                    if is_tile(m):
                        dve.wait_ge(heads.max_made, units(m, j, i))
                        heads.dve_shift(S.bank(label), u).then_inc(s_emptied, 1)
                    if is_tile(t):
                        dve.wait_ge(heads.inv_made, units(t, n, i))
                        heads.dve_norm(O.bank((f"av{n}", t)), n).then_inc(o_emptied, 1)
                    t, n = unit(m, j, 4)
                    if is_tile(t):
                        dve.wait_ge(o_filled, O.full((f"ot{n}", t), i))
                        heads.dve_copy_back(O.bank((f"ot{n}", t)), SLOTS * (t % 2) + n).then_inc(o_emptied, 1)
                    if j == 1 and is_tile(m - 4):
                        t = m - 4
                        dve.wait_ge(x_stored[t % 4], 1 + DMA * (t // 4) + i * DMA)
                        dve.wait_ge(bias_added, t + 1 + i * U)
                        dve.wait_ge(d_filled, Dr.full(("ffn", t), i))
                        nc.vector.scalar_tensor_tensor(out=x_c[:, t % 4, :], in0=Dr.bank(("ffn", t))[:, :], scalar=tgates[:, 1:2],
                                                       in1=x_b[:, t % 4, :], op0=ALU.mult, op1=ALU.add).then_inc(d_emptied, 1)
                    if j == 2 and is_tile(m - 2):
                        t = m - 2
                        dve.wait_ge(a_loaded[t % 4], DMA * (t // 4 + 1) + i * DMA)
                        dve.wait_ge(d_filled, Dr.full(("out", t), i))
                        nc.vector.scalar_tensor_tensor(out=x_b[:, t % 4, :], in0=Dr.bank(("out", t))[:, :], scalar=tgates[:, 0:1],
                                                       in1=x_a[:, t % 4, :], op0=ALU.mult, op1=ALU.add).then_inc(d_emptied, 1)
                        dve.wait_ge(d_emptied, Dr.done(("out", t), i))
                        dve.sem_inc(a_used, 1)
                        statistics("e", t, x_b[:, t % 4, :])
                    if j == 2 and is_tile(m + 2):
                        t = m + 2
                        dve.wait_ge(ln_loaded[t % 4], DMA * (t // 4 + 1) + i * DMA)
                        statistics("d", t, x_ln[:, t % 4, :])
                    if j == 3:
                        if is_tile(m + 1):
                            spread_keys_and_values(m + 1)
                        if is_tile(m - 2):
                            normalise("e", m - 2, x_b[:, (m - 2) % 4, :])
                        if is_tile(m + 2):
                            normalise("d", m + 2, x_ln[:, (m + 2) % 4, :])
                            dve.wait_ge(xn_made, ln("d", m + 2, i))
                            dve.sem_inc(ln_used, 1)

            for m in FILL:
                step(m, 0)
            with dve.Fori(0, TURNS) as i:
                for m in TURN:
                    step(m, i)
            for m in DRAIN:
                step(m, 0)


def early_latent_memory(early):
    carve = Region(early).carve
    return carve("wk", [P, C, D]), carve("wv", [P, C, D]), carve("wq0", [P, C, 2 * D])


def early_latent_weights(io, early):
    wk, wv, wq0 = early_latent_memory(early)
    return [(wk, io["L1_xattn_Wk"].rearrange("(c p) n -> p c n", p=P)),
            (wv, io["L1_xattn_Wv"].rearrange("(c p) n -> p c n", p=P)),
            (wq0, io["L1_xattn_Wq"].rearrange("(c p) n -> p c n", p=P)[:, :, 0:2 * D])]


def latent_attention(nc, io, x_in, ctx_t, x_out, early):
    B = 4
    T = B * SEQ
    TILES = T // P
    GROUPS = TOKENS // T
    G, PAIRS = 4, 4
    UNITS = G * PAIRS
    KEYS = 2 * SEQ
    SCALE = 128 ** -0.5
    LN_AT = 11

    with ExitStack() as ctx:
        chip = Chip(nc, ctx, "l1")
        sb, sem = chip.sb, chip.sem
        a_loop = [f"x{t}" for t in range(TILES)] + ["k0", "v0", "q0"]
        for s in range(UNITS):
            if s + 1 < UNITS:
                a_loop.append(f"q{s + 1}")
                if s % PAIRS == 2 and s // PAIRS + 1 < G:
                    a_loop.append(f"k{s // PAIRS + 1}")
                if s % PAIRS == 3:
                    a_loop.append(f"v{s // PAIRS + 1}")
            a_loop.append(f"pt{s}")
        A = Banks(chip.banks("bank_a"), [], a_loop)
        S = Banks(chip.banks("bank_s"), [], [f"s{u}" for u in range(UNITS)])
        V = Banks(chip.banks("bank_v"), [], [f"av{u}" for u in range(UNITS)])
        y = chip.banks("bank_y")

        x_tiles = x_in.rearrange("(g t p) d -> g p t d", p=P, t=TILES)
        out_tiles = x_out.rearrange("(g t p) d -> g p t d", p=P, t=TILES)

        ident = sb("ident", [P, P])
        wk, wv, wq0 = early_latent_memory(early)
        wq = [wq0] + [sb(f"wq{g}", [P, C, 8 * P]) for g in range(1, G)]
        wo = [sb(f"wo{g}", [P, 8, D]) for g in range(G)]
        tgate = sb("tgate", [P, 1])
        eps_col, half_col = sb("eps_col", [P, 1]), sb("half_col", [P, 1])
        xn, x = sb("xn", [P, TILES, D]), sb("x", [P, TILES, D])
        both = sb("both", [P, C, B, 2, SEQ])
        kt, v = sb("kt", [P, 2, B, KEYS]), sb("v", [P, 2, B, P])
        qt = sb("qt", [P, 2, B, 2, SEQ])
        probs, probs_t = sb("probs", [P, 2, B, KEYS]), sb("probs_t", [P, 2, B, P])
        ot = sb("ot", [P, 2, 2, B, SEQ])
        gated = sb("gated", [P, TILES, D])
        neg_max, sums, inv_sum = sb("neg_max", [P, 2, B]), sb("sums", [P, 2, B]), sb("inv_sum", [P, 2, B])
        stats, mv = sb("stats", [P, TILES, 6]), sb("mv", [P, TILES, 2])
        small, rstd = sb("small", [P, TILES]), sb("rstd", [P, TILES])

        gate_in = sem("gate_in")
        wq_in, wo_in = [sem(f"wq_in{g}") for g in range(G)], [sem(f"wo_in{g}") for g in range(G)]
        xn_loaded, ctx_loaded, x_loaded, x_stored = sem("xn_loaded"), sem("ctx_loaded"), sem("x_loaded"), sem("x_stored")
        xn_free, ctx_free = sem("xn_free"), sem("ctx_free")
        consts_made, tgate_ready = sem("consts_made"), sem("tgate_ready")
        a_filled, a_emptied = sem("a_filled"), sem("a_emptied")
        s_filled, s_emptied = sem("s_filled"), sem("s_emptied")
        v_filled, v_emptied = sem("v_filled"), sem("v_emptied")
        y_filled, y_emptied = sem("y_filled"), sem("y_emptied")
        stats_made, mv_made, rstd_step, rstd_made = sem("stats_made"), sem("mv_made"), sem("rstd_step"), sem("rstd_made")
        xn_made, x_made = sem("xn_made"), sem("x_made")
        max_made, exp_made, sum_made, inv_made, probs_made = \
            sem("max_made"), sem("exp_made"), sem("sum_made"), sem("inv_made"), sem("probs_made")
        gate = sem("gate")

        block = ctx.enter_context(nc.Block())

        @block.sync
        def _(sp):
            sp.sem_inc(xn_free, 1)
            sp.sem_inc(ctx_free, 1)
            sp.sem_inc(x_stored, 1)
            with sp.Fori(0, GROUPS) as i:
                sp.wait_ge(xn_free, i + 1)
                sp.dma_start(xn[:, :, :], x_tiles[i]).then_inc(xn_loaded, DMA)
                sp.wait_ge(ctx_free, i + 1)
                for c in range(C):
                    sp.dma_start(both[:, c, :, 0, :], ctx_t[i][:, c, :].rearrange("p (b s) -> p b s", b=B))\
                      .then_inc(ctx_loaded, DMA)
                sp.wait_ge(x_stored, 1 + DMA * TILES * i)
                sp.dma_start(x[:, :, :], x_tiles[i]).then_inc(x_loaded, DMA)
            sp.wait_ge(x_stored, 1 + DMA * TILES * GROUPS)

        @block.gpsimd
        def _(pool):
            nc.gpsimd.memset(ident[:, :], 0.0).then_inc(consts_made, 1)
            nc.gpsimd.memset(eps_col[:, :], EPS).then_inc(consts_made, 1)
            nc.gpsimd.memset(half_col[:, :], -0.5).then_inc(consts_made, 1)
            pool.wait_ge(consts_made, 3)
            nc.gpsimd.affine_select(out=ident[:, :], in_=ident[:, :], compare_op=ALU.not_equal, fill=1.0,
                                    base=0, pattern=[[-1, P]], channel_multiplier=1).then_inc(consts_made, 1)

            def inverse_deviations(i):
                for t in range(TILES):
                    pool.wait_ge(mv_made, i * TILES + t + 1)
                    nc.gpsimd.tensor_tensor(small[:, t:t + 1], mv[:, t, 1:2], eps_col[:, :], ALU.add).then_inc(rstd_step, 1)
                    pool.wait_ge(rstd_step, i * TILES + t + 1)
                    nc.gpsimd.tensor_tensor(rstd[:, t:t + 1], small[:, t:t + 1], half_col[:, :], ALU.pow)\
                        .then_inc(rstd_made, 1)

            def residuals(i):
                pool.wait_ge(x_loaded, DMA * (i + 1))
                pool.sem_inc(gate, 1)
                for t in range(TILES):
                    pool.wait_ge(y_emptied, 1 + i * TILES + t + 1)
                    nc.gpsimd.tensor_tensor(x[:, t, :], x[:, t, :], gated[:, t, :], ALU.add).then_inc(x_made, 1)

            inverse_deviations(0)
            with pool.Fori(0, GROUPS - 1) as i:
                inverse_deviations(i + 1)
                residuals(i)
            residuals(GROUPS - 1)

        @block.scalar
        def _(act):
            act.dma_start(tgate[:, :], io["g_xattn"][1:2].partition_broadcast(P)).then_inc(gate_in, DMA)
            act.wait_ge(ctx_loaded, DMA * C)
            for g in range(G):
                if g:
                    act.dma_start(wq[g][:, :, :], io["L1_xattn_Wq"].rearrange("(c p) n -> p c n", p=P)
                                  [:, :, g * 8 * P:(g + 1) * 8 * P]).then_inc(wq_in[g], DMA)
                act.dma_start(wo[g][:, :, :], io["L1_xattn_Wo"].rearrange("(h p) n -> p h n", p=P)
                              [:, 8 * g:8 * g + 8, :]).then_inc(wo_in[g], DMA)
            act.sem_inc(a_emptied, 2)
            act.sem_inc(y_emptied, 1)
            act.wait_ge(gate_in, DMA)
            nc.scalar.activation(tgate[:, :], tgate[:, :], ACT.Tanh).then_inc(tgate_ready, 1)
            act.wait_ge(tgate_ready, 1)
            with act.Fori(0, GROUPS) as i:
                def empty(label, out):
                    src = A.bank(i, label)[:, :]
                    if len(out.shape) == 3:
                        src = src.rearrange("p (b n) -> p b n", b=out.shape[1])
                    act.wait_ge(a_filled, A.full(i, label))
                    nc.scalar.activation(out, src, ACT.Copy).then_inc(a_emptied, 1)

                def empty_queries(u):
                    src = A.bank(i, f"q{u}")[:, :].rearrange("p (h b s) -> p b h s", h=2, b=B)
                    act.wait_ge(a_filled, A.full(i, f"q{u}"))
                    nc.scalar.activation(qt[:, u % 2], src, ACT.Copy).then_inc(a_emptied, 1)

                for t in range(TILES):
                    act.wait_ge(a_filled, A.full(i, f"x{t}"))
                    for b in range(2):
                        last = nc.scalar.activation(both[:, :, 2 * t + b, 1, :],
                                                    split4(A.bank(i, f"x{t}")[:, :])[:, :, b * SEQ:(b + 1) * SEQ], ACT.Copy)
                    last.then_inc(a_emptied, 1)
                empty("k0", kt[:, 0].rearrange("p b k -> p (b k)"))
                empty("v0", v[:, 0].rearrange("p b k -> p (b k)"))
                empty_queries(0)
                for s in range(UNITS):
                    act.wait_ge(s_emptied, S.done(i, f"s{s}"))
                    nc.scalar.activation(probs[:, s % 2], probs[:, s % 2], ACT.Exp, scale=SCALE).then_inc(exp_made, 1)
                    if s + 1 < UNITS:
                        empty_queries(s + 1)
                        g = s // PAIRS + 1
                        if s % PAIRS == 2 and g < G:
                            empty(f"k{g}", kt[:, g % 2].rearrange("p b k -> p (b k)"))
                        if s % PAIRS == 3:
                            empty(f"v{g}", v[:, g % 2].rearrange("p b k -> p (b k)"))
                    empty(f"pt{s}", probs_t[:, s % 2].rearrange("p b k -> p (b k)"))
                for t in range(TILES):
                    act.wait_ge(y_filled, i * TILES + t + 1)
                    nc.scalar.activation(gated[:, t, :], y[t][:, :], ACT.Copy, scale=tgate[:, 0:1]).then_inc(y_emptied, 1)
                for t in range(TILES):
                    act.wait_ge(x_made, i * TILES + t + 1)
                    act.dma_start(out_tiles[i][:, t, :], x[:, t, :]).then_inc(x_stored, DMA)

        @block.tensor
        def _(pe):
            pe.wait_ge(consts_made, 4)
            with pe.Fori(0, GROUPS) as i:
                def keys(g):
                    pe.wait_ge(a_emptied, A.free(i, f"k{g}"))
                    for c in range(C):
                        last = nc.tensor.matmul(A.bank(i, f"k{g}")[:, :], wk[:, c, g * P:(g + 1) * P],
                                                both[:, c].rearrange("p b h s -> p (b h s)"), start=(c == 0), stop=(c == C - 1))
                    last.then_inc(a_filled, 1)

                def values(g):
                    pe.wait_ge(a_emptied, A.free(i, f"v{g}"))
                    for b in range(B):
                        for c in range(C):
                            last = nc.tensor.matmul(A.bank(i, f"v{g}")[:, b * P:(b + 1) * P],
                                                    both[:, c, b].rearrange("p h s -> p (h s)"), wv[:, c, g * P:(g + 1) * P],
                                                    start=(c == 0), stop=(c == C - 1))
                    last.then_inc(a_filled, 1)

                def queries(u):
                    g = u // PAIRS
                    if u % PAIRS == 0 and g:
                        pe.wait_ge(wq_in[g], DMA)
                    pe.wait_ge(a_emptied, A.free(i, f"q{u}"))
                    for h in range(2):
                        col = (2 * (u % PAIRS) + h) * P
                        for c in range(C):
                            last = nc.tensor.matmul(A.bank(i, f"q{u}")[:, h * T:(h + 1) * T], wq[g][:, c, col:col + P],
                                                    both[:, c, :, 1, :], start=(c == 0), stop=(c == C - 1))
                    last.then_inc(a_filled, 1)

                def scores(u):
                    pe.wait_ge(a_emptied, A.done(i, f"q{u}"))
                    pe.wait_ge(s_emptied, S.free(i, f"s{u}"))
                    for b in range(B):
                        last = nc.tensor.matmul(S.bank(i, f"s{u}")[:, b * KEYS:(b + 1) * KEYS],
                                                qt[:, u % 2, b].rearrange("p h s -> p (h s)"), kt[:, u // PAIRS % 2, b, :],
                                                start=True, stop=True)
                    last.then_inc(s_filled, 1)

                def turn_probs(u):
                    pe.wait_ge(probs_made, i * UNITS + u + 1)
                    pe.wait_ge(a_emptied, A.free(i, f"pt{u}"))
                    turned(nc, A.bank(i, f"pt{u}"), probs[:, u % 2].rearrange("p b k -> p (b k)"), ident)\
                        .then_inc(a_filled, 1)

                def attend(u):
                    pe.wait_ge(a_emptied, A.done(i, f"pt{u}"))
                    pe.wait_ge(v_emptied, V.free(i, f"av{u}"))
                    for b in range(B):
                        last = nc.tensor.matmul(V.bank(i, f"av{u}")[:, b * P:(b + 1) * P], v[:, u // PAIRS % 2, b, :],
                                                probs_t[:, u % 2, b, :], start=True, stop=True)
                    last.then_inc(v_filled, 1)

                def project(u):
                    g = u // PAIRS
                    if u % PAIRS == 0:
                        pe.wait_ge(wo_in[g], DMA)
                    if u == 0:
                        pe.wait_ge(y_emptied, 1 + i * TILES)
                    pe.wait_ge(v_emptied, V.done(i, f"av{u}"))
                    for t in range(TILES):
                        for h in range(2):
                            tokens = ot[:, u % 2, h, 2 * t:2 * t + 2, :].rearrange("p b s -> p (b s)")
                            last = nc.tensor.matmul(y[t][:, :], tokens, wo[g][:, 2 * (u % PAIRS) + h, :],
                                                    start=(u == 0 and h == 0), stop=(u == UNITS - 1 and h == 1))
                        if u == UNITS - 1:
                            last.then_inc(y_filled, 1)

                for t in range(TILES):
                    pe.wait_ge(xn_made, i * TILES + t + 1)
                    pe.wait_ge(a_emptied, A.free(i, f"x{t}"))
                    turned(nc, A.bank(i, f"x{t}"), xn[:, t, :], ident).then_inc(a_filled, 1)
                pe.wait_ge(a_emptied, A.done(i, f"x{TILES - 1}"))
                pe.sem_inc(xn_free, 1)
                pe.wait_ge(ctx_loaded, DMA * C * (i + 1))
                keys(0)
                values(0)
                queries(0)
                for s in range(UNITS + 1):
                    if s < UNITS:
                        if s % PAIRS == 0:
                            pe.wait_ge(a_emptied, A.done(i, f"v{s // PAIRS}"))
                            if s // PAIRS == G - 1:
                                pe.sem_inc(ctx_free, 1)
                        scores(s)
                    if s >= 1:
                        attend(s - 1)
                    if s + 1 < UNITS:
                        queries(s + 1)
                        if s % PAIRS == 2 and s // PAIRS + 1 < G:
                            keys(s // PAIRS + 1)
                        if s % PAIRS == 3:
                            values(s // PAIRS + 1)
                    if s < UNITS:
                        turn_probs(s)
                    if s >= 1:
                        project(s - 1)

        @block.vector
        def _(dve):
            dve.sem_inc(s_emptied, 2)
            dve.sem_inc(v_emptied, 2)

            def statistics(i):
                dve.wait_ge(xn_loaded, DMA * (i + 1))
                for t in range(TILES):
                    nc.vector.bn_stats(stats[:, t, :], xn[:, t, :]).then_inc(stats_made, 1)
                for t in range(TILES):
                    dve.wait_ge(stats_made, i * TILES + t + 1)
                    dve.sem_inc(gate, 1)
                    nc.vector.bn_aggr(mv[:, t, :], stats[:, t, :]).then_inc(mv_made, 1)

            def normalise(i):
                for t in range(TILES):
                    dve.wait_ge(rstd_made, i * TILES + t + 1)
                    nc.vector.tensor_scalar(xn[:, t, :], xn[:, t, :], mv[:, t, 0:1], rstd[:, t:t + 1],
                                            ALU.subtract, ALU.mult).then_inc(xn_made, 1)

            def attention(i, last):
                for s in range(UNITS + 1):
                    n = s % 2
                    if s == LN_AT and not last:
                        statistics(i + 1)
                    if s == LN_AT + 1 and not last:
                        normalise(i + 1)
                    if s < UNITS:
                        scores = S.bank(i, f"s{s}")[:, :].rearrange("p (b k) -> p b k", b=B)
                        dve.wait_ge(s_filled, S.full(i, f"s{s}"))
                        nc.vector.tensor_reduce(neg_max[:, n, :], scores, AX_X, ALU.max, negate=True).then_inc(max_made, 1)
                        dve.wait_ge(max_made, i * UNITS + s + 1)
                        nc.vector.tensor_tensor(probs[:, n], scores, along(neg_max[:, n, :], KEYS), ALU.add)\
                            .then_inc(s_emptied, 1)
                    if s >= 1:
                        dve.wait_ge(v_filled, V.full(i, f"av{s - 1}"))
                        nc.vector.tensor_copy(ot[:, (s - 1) % 2].rearrange("p h b s -> p b h s"),
                                              V.bank(i, f"av{s - 1}")[:, :].rearrange("p (b h s) -> p b h s", b=B, h=2))\
                            .then_inc(v_emptied, 1)
                    if s < UNITS:
                        dve.wait_ge(exp_made, i * UNITS + s + 1)
                        nc.vector.tensor_reduce(sums[:, n, :], probs[:, n], AX_X, ALU.add).then_inc(sum_made, 1)
                        dve.wait_ge(sum_made, i * UNITS + s + 1)
                        nc.vector.reciprocal(inv_sum[:, n, :], sums[:, n, :]).then_inc(inv_made, 1)
                        dve.wait_ge(inv_made, i * UNITS + s + 1)
                        nc.vector.tensor_tensor(probs[:, n], probs[:, n], along(inv_sum[:, n, :], KEYS), ALU.mult)\
                            .then_inc(probs_made, 1)

            statistics(0)
            normalise(0)
            with dve.Fori(0, GROUPS - 1) as i:
                attention(i, False)
            attention(GROUPS - 1, True)


class LastWeights:

    def __init__(self, nc, ctx):
        def sb(name, shape):
            return ctx.enter_context(nc.sbuf_tensor(f"last_{name}", shape, F32))

        self.wk, self.wv, self.wo = sb("wk", [P, C, P]), sb("wv", [P, C, P]), sb("wo", [P, REP, D])
        self.wq_raw, self.up_raw = sb("wq_raw", [P, C, D])[:, :, :], sb("up_raw", [P, C, P])[:, :, :]
        self.low_raw = sb("low_raw", [P, D])[:, :]

    def loads(self, io):
        experts = io["L3_ffn_Wr"].shape[0]
        pairs = [(self.wq_raw, io["L3_xattn_Wq"].rearrange("(c p) n -> p c n", p=P)),
                 (self.low_raw, io["L3_ffn_A"].rearrange("h r d -> (h r) d")),
                 (self.wk[:, :, :], io["L3_xattn_Wk"].rearrange("(c p) n -> p c n", p=P)),
                 (self.wv[:, :, :], io["L3_xattn_Wv"].rearrange("(c p) n -> p c n", p=P))]
        pairs += [(self.up_raw[:, c].rearrange("p (h r) -> p h r", h=experts),
                   io["L3_ffn_B"][:, c * P:(c + 1) * P, :].rearrange("h p r -> p h r")) for c in range(C)]
        pairs += [(self.wo[k * HD:(k + 1) * HD, :, :],
                   io["L3_xattn_Wo"][k * REP * HD:(k + 1) * REP * HD, :].rearrange("(r d) n -> d r n", r=REP))
                  for k in range(KV)]
        return pairs


def window_attention(nc, io, x_in, ctx_in, x_out, last_weights):
    TILES = TOKENS // P
    W = 16
    LEFT = W // 2
    HEADS2, HD2 = 8, 8
    BH = 2 * HEADS2
    SCALE2 = HD2 ** -0.5
    R0, R1, E = 32, 8, 3
    POOL_W = (2, 6, 10, 13)
    DVE_W = tuple(w for w in range(W) if w not in POOL_W)
    HALF = W // 2
    FOURS, ADDS = W // 4, 3 * W // 4
    NP, ND = len(POOL_W), len(DVE_W)
    POOL_AHEAD = 3
    U = 4
    FILL = range(-1, 3)
    TURN = range(3, 3 + U)
    TURNS = (TILES - 2 - 3 + 1) // U
    DRAIN = range(3 + U * TURNS, TILES + 3)
    ALL = range(-1, TILES + 3)
    assert 3 + U * TURNS == TILES - 1

    def is_tile(t):
        return 0 <= t < TILES

    def in_order(steps, parts):
        return [(name, m + off) for m in steps for name, off in parts if is_tile(m + off)]

    A_PARTS = [("xa", 1), ("xc", -3), ("q2", 1), ("k2", 1), ("v2", 1)]
    F_PARTS = [("f1", 1), ("f2", -3)]
    LN_PARTS = [("a", 1), ("c", -3), ("b", 1)]
    G_PARTS = [("g0", 0), ("g1", 0)]
    O_PARTS, S_PARTS, Y_PARTS = [(f"b{w}", -2) for w in range(W)], [("dots0", 0), ("dots1", 0)], [("y", -2)]

    with ExitStack() as ctx:
        chip = Chip(nc, ctx, "l2")
        sb, sem = chip.sb, chip.sem
        a_setup = [("gt", 0)] + [("fold", c) for c in range(C)] + [("w2", 0)]
        bank_a, bank_g = chip.banks("bank_ag")
        A = Ring([bank_a], a_setup + in_order(ALL, A_PARTS), in_order(TURN, A_PARTS), U)
        S = Ring(chip.banks("bank_s"), in_order(ALL, S_PARTS), in_order(TURN, S_PARTS), U)
        O = Ring(chip.banks("bank_o"), in_order(ALL, O_PARTS), in_order(TURN, O_PARTS), U)
        bank_y, bank_f = chip.banks("bank_yf")
        Y = Ring([bank_y], in_order(ALL, Y_PARTS), in_order(TURN, Y_PARTS), U)
        F = Ring([bank_f], in_order(ALL, F_PARTS), in_order(TURN, F_PARTS), U)
        G = Ring([bank_g], in_order(ALL, G_PARTS), in_order(TURN, G_PARTS), U)
        ln_order = in_order(ALL, LN_PARTS)

        def ln(kind, t, i):
            return ln_order.index((kind, t)) + 1 + i * U * len(LN_PARTS)

        def added(w):
            return 3 * (w // 4) + max(w % 4, 1)

        def biased(kind, t, i):
            return 2 * t + {"a": 0, "b": 1}[kind] + 1 + i * 2 * U

        x_tiles = x_in.rearrange("(t p) d -> t p d", p=P)
        ctx_tiles = ctx_in.rearrange("(t p) d -> t p d", p=P)
        out_tiles = x_out.rearrange("(t p) d -> t p d", p=P)

        ident = sb("ident", [P, P])
        LAST = (HALF - 1) * BH
        head_sum = sb("head_sum", [P, LAST + HALF * BH])
        eps_col, half_col = sb("eps_col", [P, 1]), sb("half_col", [P, 1])
        w_f1, w_f2 = sb("w_f1", [P, C, D]), sb("w_f2", [P, C, D])
        w2, b2 = sb("w2", [P, 4, P]), sb("b2", [P, 4])
        gates, tgates = sb("gates", [P, 4]), sb("tgates", [P, 3])
        f2_gate = sb("f2_gate", [P, 1])
        gated_b1, gated_b2 = sb("gated_b1", [P, D]), sb("gated_b2", [P, 1])

        region = sb("region", [P, 2 * 4 * W * P])
        carve = Region(region).carve
        base_raw, fourier = carve("base_raw", [P, C, D]), carve("fourier", [P, C, D])
        coefs = [carve("coefs0", [P, C, E, R0]), carve("coefs1", [P, C, E, R1])]
        flags = [carve("flags0", [P, C, E, R0 // 4], I32), carve("flags1", [P, C, E, R1 // 4], I32)]
        masked = [carve("masked0", [P, C, E, R0]), carve("masked1", [P, C, E, R1])]
        pair_sum, expert_sum = carve("pair_sum", [P, C, R0 + R1]), carve("expert_sum", [P, C, R0 + R1])
        enc, gt = carve("enc", [P, D]), carve("gt", [P, D])
        w2_raw = carve("w2_raw", [P, 4, P])
        signs_raw = carve("signs_raw", [P, C, D // 4], I32)
        b1_raw = carve("b1_raw", [P, D])

        x_a, x_b, x_c, x_d = sb("x_a", [P, 4, D]), sb("x_b", [P, 4, D]), sb("x_c", [P, 2, D]), sb("x_d", [P, 4, D])
        ctx_new = sb("ctx_new", [P, 4, D])
        xn = {kind: sb(f"xn_{kind}", [P, D]) for kind in "abc"}
        xnt = {kind: sb(f"xnt_{kind}", [P, C, P]) for kind in "ac"}
        stats, mv = sb("stats", [P, 3, 6]), sb("mv", [P, 3, 2])
        small, rstd = sb("small", [P, 3]), sb("rstd", [P, 3])
        q2 = sb("q2", [P, 2, D])
        k2, v2 = sb("k2", [P, 2, D + W]), sb("v2", [P, 4, D + W])
        prods, prods_pool = sb("prods", [P, 4, D]), sb("prods_pool", [P, 3, D])
        values, fours = sb("values", [P, 4, D]), sb("fours", [P, 2, D])
        scores_t = sb("scores_t", [P, 2, D])
        probs2 = sb("probs2", [P, 2, 2 * BH, W])
        wide = region[:, :].rearrange("p (n t w c) -> p n t w c", n=2, t=4, w=W)
        neg_max2, sums2, inv2 = sb("neg_max2", [P, 2, 2 * BH]), sb("sums2", [P, 2, 2 * BH]), sb("inv2", [P, 2, 2 * BH])

        fold_in, w_in, small_in, last_in = sem("fold_in"), sem("w_in"), sem("small_in"), sem("last_in")
        consts_made, raw_cleared = sem("consts_made"), sem("raw_cleared")
        gates_ready, gated_made = sem("gates_ready"), sem("gated_made")
        masked_made, pair_made, experts_made, signs_made = \
            sem("masked_made"), sem("pair_made"), sem("experts_made"), sem("signs_made")
        x_loaded, ctx_loaded = [sem(f"x_loaded{t}") for t in range(4)], [sem(f"ctx_loaded{t}") for t in range(4)]
        x_used, ctx_used = sem("x_used"), sem("ctx_used")
        x_stored = [sem(f"x_stored{t}") for t in range(4)]
        a_filled, a_emptied = sem("a_filled"), sem("a_emptied")
        s_filled, s_emptied = sem("s_filled"), sem("s_emptied")
        o_filled, o_emptied = sem("o_filled"), sem("o_emptied")
        y_filled, y_emptied = sem("y_filled"), sem("y_emptied")
        f_filled, f_emptied = sem("f_filled"), sem("f_emptied")
        stats_made, mv_made, rstd_step, rstd_made = sem("stats_made"), sem("mv_made"), sem("rstd_step"), sem("rstd_made")
        xn_made, bias_added = sem("xn_made"), sem("bias_added")
        prods_made, pool_prods_made, prods_used = sem("prods_made"), sem("pool_prods_made"), sem("prods_used")
        values_added, fours_used, g_emptied = sem("values_added"), sem("fours_used"), sem("g_emptied")
        max2_made, exp2_made, sum2_made, inv2_made, probs2_made, wide_made = \
            sem("max2_made"), sem("exp2_made"), sem("sum2_made"), sem("inv2_made"), sem("probs2_made"), sem("wide_made")
        gate = sem("gate")

        FOLD_LOADS = 2 + 4 * C + 2
        LOADS = 1 + 8
        SMALL = 4 + 8 + 1

        block = ctx.enter_context(nc.Block())

        @block.sync
        def _(sp):
            def fold_load(out, src):
                sp.dma_start(out, src).then_inc(fold_in, DMA)

            for n in range(2):
                for c in range(C):
                    rows = slice(c * P, (c + 1) * P)
                    fold_load(coefs[n][:, c], io[f"L1_ffn_coefs{n}"][:, rows, :].rearrange("e p r -> p e r"))
                    fold_load(flags[n][:, c], io[f"L1_ffn_mask{n}"][:, rows, :].rearrange("e p r -> p e r"))
            fold_load(fourier, io["fourier"].rearrange("(c p) d -> p c d", p=P))
            fold_load(base_raw, io["L1_ffn_W_base"].rearrange("(c p) d -> p c d", p=P))
            fold_load(enc[0:R0, :], io["L1_ffn_enc0"])
            fold_load(enc[R0:R0 + R1, :], io["L1_ffn_enc1"])
            for t in range(4):
                sp.dma_start(x_a[:, t, :], x_tiles[t]).then_inc(x_loaded[t], DMA)
                sp.dma_start(ctx_new[:, t, :], ctx_tiles[t]).then_inc(ctx_loaded[t], DMA)
                if t == 0:
                    sp.dma_start(signs_raw, io["L2_ffn_kernel"].rearrange("(c p) f -> p c f", p=P)).then_inc(w_in, DMA)
                    sp.wait_ge(raw_cleared, 1)
                    for n, name in enumerate("qkvo"):
                        for b in range(2):
                            sp.dma_start(w2_raw[b * SEQ:(b + 1) * SEQ, n, b * SEQ:(b + 1) * SEQ], io[f"L2_xattn_W{name}"])\
                              .then_inc(w_in, DMA)
            loads = last_weights.loads(io)
            for out, src in loads:
                sp.dma_start(out, src).then_inc(last_in, DMA)
            with sp.Fori(0, TILES // 4 - 1) as i:
                for t in range(4):
                    sp.wait_ge(x_used, i * 4 + t + 1)
                    sp.dma_start(x_a[:, t, :], x_tiles[i * 4 + 4 + t]).then_inc(x_loaded[t], DMA)
                    sp.wait_ge(ctx_used, i * 4 + t + 1)
                    sp.dma_start(ctx_new[:, t, :], ctx_tiles[i * 4 + 4 + t]).then_inc(ctx_loaded[t], DMA)
            sp.wait_ge(last_in, DMA * len(loads))
            for t in range(4):
                sp.wait_ge(x_stored[t], 1 + DMA * TILES // 4)

        @block.gpsimd
        def _(pool):
            for t in range(4):
                pool.sem_inc(x_stored[t], 1)
            nc.gpsimd.memset(w2_raw, 0.0).then_inc(raw_cleared, 1)
            nc.gpsimd.memset(ident[:, :], 0.0).then_inc(consts_made, 1)
            nc.gpsimd.memset(eps_col[:, :], EPS).then_inc(consts_made, 1)
            nc.gpsimd.memset(half_col[:, :], -0.5).then_inc(consts_made, 1)
            nc.gpsimd.memset(k2[:, :, :], 0.0).then_inc(consts_made, 1)
            nc.gpsimd.memset(v2[:, :, :], 0.0).then_inc(consts_made, 1)
            nc.gpsimd.memset(head_sum[:, :], 0.0).then_inc(consts_made, 1)
            pool.wait_ge(consts_made, 6)
            agree = head_sum[:, LAST:LAST + BH]
            nc.gpsimd.memset(agree, 1.0).then_inc(consts_made, 1)
            nc.gpsimd.affine_select(out=ident[:, :], in_=ident[:, :], compare_op=ALU.not_equal, fill=1.0,
                                    base=0, pattern=[[-1, P]], channel_multiplier=1).then_inc(consts_made, 1)
            pool.wait_ge(consts_made, 8)
            nc.gpsimd.affine_select(out=agree, in_=agree, compare_op=ALU.is_ge, fill=0.0,
                                    base=0, pattern=[[-HD2, BH]], channel_multiplier=1).then_inc(consts_made, 1)
            pool.wait_ge(consts_made, 9)
            nc.gpsimd.affine_select(out=agree, in_=agree, compare_op=ALU.is_ge, fill=0.0,
                                    base=HD2 - 1, pattern=[[HD2, BH]], channel_multiplier=-1).then_inc(consts_made, 1)
            pool.wait_ge(small_in, SMALL * DMA)
            pool.wait_ge(gates_ready, 1)
            nc.gpsimd.tensor_tensor(gated_b1[:, :], b1_raw, tgates[:, 0:1].to_broadcast([P, D]), ALU.mult)\
                .then_inc(gated_made, 1)
            nc.gpsimd.tensor_tensor(gated_b2[:, :], b2[:, 3:4], tgates[:, 1:2], ALU.mult).then_inc(gated_made, 1)
            nc.gpsimd.tensor_tensor(f2_gate[:, :], gates[:, 3:4], tgates[:, 2:3], ALU.mult).then_inc(gated_made, 1)
            pool.wait_ge(gated_made, 3)

            def step(m, i):
                def inverse_deviation(kind, t):
                    k = "abc".index(kind)
                    pool.wait_ge(mv_made, ln(kind, t, i))
                    nc.gpsimd.tensor_tensor(small[:, k:k + 1], mv[:, k, 1:2], eps_col[:, :], ALU.add).then_inc(rstd_step, 1)
                    pool.wait_ge(rstd_step, ln(kind, t, i))
                    nc.gpsimd.tensor_tensor(rstd[:, k:k + 1], small[:, k:k + 1], half_col[:, :], ALU.pow)\
                        .then_inc(rstd_made, 1)

                def add_bias(kind, t):
                    x, row = {"a": (x_a, gated_b1[:, :]), "b": (x_b, gated_b2[:, 0:1].to_broadcast([P, D]))}[kind]
                    pool.wait_ge(xn_made, ln(kind, t, i))
                    nc.gpsimd.tensor_tensor(x[:, t % 4, :], x[:, t % 4, :], row, ALU.add).then_inc(bias_added, 1)

                def product(w):
                    n = m * NP + POOL_W.index(w)
                    if w == POOL_W[0]:
                        pool.wait_ge(a_emptied, A.done(("k2", m), i))
                    if n >= 3:
                        used, used_w = (n - 3) // NP, POOL_W[(n - 3) % NP]
                        pool.wait_ge(prods_used, (used + i * U) * W + used_w + 1)
                    nc.gpsimd.tensor_tensor(prods_pool[:, n % 3, :], q2[:, m % 2, :], k2[:, m % 2, w:w + D], ALU.mult)\
                        .then_inc(pool_prods_made, 1)

                def add_value(w):
                    v, k = m - 2, w // 4
                    pool.wait_ge(o_emptied, O.done((f"b{w}", v), i))
                    if w % 4 == 1:
                        if v > 0 or k >= 2:
                            pool.wait_ge(fours_used, (v + i * U) * FOURS + k - 1)
                        before = values[:, (w - 1) % 4, :]
                    else:
                        pool.wait_ge(values_added, (v + i * U) * ADDS + added(w - 1))
                        before = fours[:, k % 2, :]
                    nc.gpsimd.tensor_tensor(fours[:, k % 2, :], before, values[:, w % 4, :], ALU.add).then_inc(values_added, 1)

                for w in range(-POOL_AHEAD, W + 1):
                    if is_tile(m) and w + POOL_AHEAD in POOL_W:
                        product(w + POOL_AHEAD)
                    if is_tile(m - 2) and w >= 1 and (w - 1) % 4:
                        add_value(w - 1)
                    if is_tile(m + 1):
                        if w == 1:
                            inverse_deviation("a", m + 1)
                        if w == 4:
                            add_bias("a", m + 1)
                    if is_tile(m - 3) and w == 3:
                        inverse_deviation("c", m - 3)
                    if is_tile(m + 1):
                        if w == 11:
                            inverse_deviation("b", m + 1)
                        if w == 13:
                            add_bias("b", m + 1)

            for m in FILL:
                step(m, 0)
            with pool.Fori(0, TURNS) as i:
                for m in TURN:
                    step(m, i)
            for m in DRAIN:
                step(m, 0)

        @block.scalar
        def _(act):
            def load(out, src, **more):
                act.dma_start(out, src, **more).then_inc(small_in, DMA)

            for n, (name, k) in enumerate((("g_ffn", 1), ("g_xattn", 2), ("g_ffn", 2), ("L2_ffn_scale", 0))):
                load(gates[:, n:n + 1], io[name][k:k + 1].partition_broadcast(P))
            for n, name in enumerate("qkvo"):
                for b in range(2):
                    load(b2[b * SEQ:(b + 1) * SEQ, n:n + 1], io[f"L2_xattn_b{name}"].rearrange("(p a) -> p a", a=1))
            load(b1_raw, io["L1_ffn_b_base"].partition_broadcast(P))
            act.sem_inc(a_emptied, 1)
            act.sem_inc(g_emptied, 1)
            act.wait_ge(small_in, SMALL * DMA)
            nc.scalar.activation(tgates[:, :], gates[:, 0:3], ACT.Tanh).then_inc(gates_ready, 1)

            def empty(label, out, i=0, bias=None):
                src = A.bank(label)[:, :]
                act.wait_ge(a_filled, A.full(label, i))
                if len(out.shape) == 3:
                    src = src.rearrange("p (b n) -> p b n", b=out.shape[1])
                if bias is None:
                    nc.scalar.activation(out, src, ACT.Copy).then_inc(a_emptied, 1)
                else:
                    nc.scalar.activation(out, src, ACT.Identity, bias=bias).then_inc(a_emptied, 1)

            act.wait_ge(a_filled, A.full(("gt", 0)))
            nc.scalar.activation(gt[0:R0 + R1, :], A.bank(("gt", 0))[0:R0 + R1, :], ACT.Copy, scale=0.5).then_inc(a_emptied, 1)
            for c in range(C):
                empty(("fold", c), w_f1[:, c, :])
            empty(("w2", 0), w2[:, :, :])

            def step(m, i):
                def spread(half):
                    t = m - 1
                    act.wait_ge(probs2_made, (t + i * U) * 2 + half + 1)
                    for n in range(2):
                        src = probs2[:, half, n * BH:(n + 1) * BH, :].rearrange("p b w -> p w b")\
                            .unsqueeze(3).to_broadcast([P, W, BH, HD2])
                        out = wide[:, t % 2, 2 * half + n].rearrange("p w (b c) -> p w b c", b=BH)
                        nc.scalar.activation(out, src, ACT.Copy).then_inc(wide_made, 1)

                def exponentials(half):
                    act.wait_ge(s_emptied, S.done((f"dots{half}", m - 1), i))
                    nc.scalar.activation(probs2[:, half], probs2[:, half], ACT.Exp, scale=SCALE2).then_inc(exp2_made, 1)

                def empty_scores(half):
                    act.wait_ge(prods_used, (m + i * U) * W + (half + 1) * HALF)
                    nc.scalar.activation(scores_t[:, half, :], bank_g[:, :], ACT.Copy).then_inc(g_emptied, 1)

                if is_tile(m - 1):
                    exponentials(0)
                if is_tile(m + 1):
                    empty(("xa", m + 1), xnt["a"][:, :, :], i)
                if is_tile(m - 1):
                    exponentials(1)
                if is_tile(m):
                    empty_scores(0)
                if is_tile(m - 1):
                    spread(0)
                if is_tile(m - 3):
                    empty(("xc", m - 3), xnt["c"][:, :, :], i)
                if is_tile(m - 1):
                    spread(1)
                if is_tile(m):
                    empty_scores(1)
                if is_tile(m + 1):
                    t = m + 1
                    empty(("q2", t), q2[:, t % 2, :], i, b2[:, 0:1])
                    empty(("k2", t), k2[:, t % 2, LEFT:LEFT + D], i, b2[:, 1:2])
                    empty(("v2", t), v2[:, t % 4, LEFT:LEFT + D], i, b2[:, 2:3])
                    act.sem_inc(ctx_used, 1)
                if is_tile(m - 3):
                    act.wait_ge(f_emptied, F.done(("f2", m - 3), i))
                    act.dma_start(out_tiles[m - 3 + i * U], x_d[:, (m - 3) % 4, :]).then_inc(x_stored[(m - 3) % 4], DMA)

            for m in FILL:
                step(m, 0)
            with act.Fori(0, TURNS) as i:
                for m in TURN:
                    step(m, i)
            for m in DRAIN:
                step(m, 0)

        @block.tensor
        def _(pe):
            pe.wait_ge(consts_made, 10)
            pe.wait_ge(fold_in, FOLD_LOADS * DMA)
            pe.wait_ge(experts_made, 2)
            pe.wait_ge(a_emptied, A.free(("gt", 0)))
            for c in range(C):
                last = nc.tensor.matmul(A.bank(("gt", 0))[0:R0 + R1, :], expert_sum[:, c, :], fourier[:, c, :],
                                        start=(c == 0), stop=(c == C - 1))
            last.then_inc(a_filled, 1)
            for c in range(C):
                pe.wait_ge(a_emptied, A.free(("fold", c)))
                out = A.bank(("fold", c))
                for o in range(C):
                    nc.tensor.matmul(out[:, o * P:(o + 1) * P], base_raw[:, o, c * P:(c + 1) * P], ident[:, :],
                                     start=(o == 0), stop=False, skip_group_check=True)
                if c == 0:
                    pe.wait_ge(a_emptied, A.done(("gt", 0)))
                nc.tensor.matmul(out[:, :], enc[0:R0 + R1, c * P:(c + 1) * P], gt[0:R0 + R1, :],
                                 start=False, stop=True, skip_group_check=True).then_inc(a_filled, 1)
            pe.wait_ge(w_in, LOADS * DMA)
            pe.wait_ge(a_emptied, A.free(("w2", 0)))
            for n in range(4):
                last = nc.tensor.transpose(A.bank(("w2", 0))[:, n * P:(n + 1) * P], w2_raw[:, n, :], ident[:, :])
            last.then_inc(a_filled, 1)
            pe.wait_ge(a_emptied, A.done(("w2", 0)))
            pe.wait_ge(signs_made, 1)

            def step(m, i):
                def turn_x(kind, t):
                    pe.wait_ge(xn_made, ln(kind, t, i))
                    pe.wait_ge(a_emptied, A.free((f"x{kind}", t), i))
                    turned(nc, A.bank((f"x{kind}", t)), xn[kind][:, :], ident).then_inc(a_filled, 1)

                def feed_forward(label, kind, t, w, c):
                    if c == 0:
                        pe.wait_ge(a_emptied, A.done((f"x{kind}", t), i))
                        pe.wait_ge(f_emptied, F.free((label, t), i))
                    last = nc.tensor.matmul(bank_f[:, :], xnt[kind][:, c, :], w[:, c, :],
                                            start=(c == 0), stop=(c == C - 1))
                    if c == C - 1:
                        last.then_inc(f_filled, 1)

                def project(k):
                    v = m - 2
                    pe.wait_ge(values_added, (v + i * U) * ADDS + 3 * (k + 1))
                    if k == 0:
                        pe.wait_ge(y_emptied, Y.free(("y", v), i))
                    last = nc.tensor.matmul(bank_y[:, :], w2[:, 3, :], fours[:, k % 2, :],
                                            start=(k == 0), stop=(k == FOURS - 1))
                    if k < FOURS - 1:
                        last.then_inc(fours_used, 1)
                    else:
                        last.then_inc(y_filled, 1)
                        pe.wait_ge(y_filled, Y.full(("y", v), i))
                        pe.sem_inc(fours_used, 1)

                def project_layer2(n):
                    t = m + 1
                    label, src = (("q2", xn["b"][:, :]), ("k2", ctx_new[:, t % 4, :]), ("v2", ctx_new[:, t % 4, :]))[n]
                    if n == 0:
                        pe.wait_ge(xn_made, ln("b", t, i))
                    else:
                        pe.wait_ge(ctx_loaded[t % 4], DMA * (t // 4 + 1) + i * DMA)
                    pe.wait_ge(a_emptied, A.free((label, t), i))
                    nc.tensor.matmul(bank_a[:, :], w2[:, n, :], src, start=True, stop=True).then_inc(a_filled, 1)

                def turn_scores():
                    pe.wait_ge(g_emptied, G.done(("g1", m), i))
                    for n in range(2):
                        pe.wait_ge(s_emptied, S.free((f"dots{n}", m), i))
                        for c in range(2):
                            for half in range(2):
                                last = nc.tensor.transpose(S.bank((f"dots{n}", m))[:, (2 * c + half) * P:(2 * c + half + 1) * P],
                                                           scores_t[:, half, (2 * n + c) * P:(2 * n + c + 1) * P], ident[:, :])
                        last.then_inc(s_filled, 1)

                if is_tile(m - 2):
                    pe.wait_ge(wide_made, (m - 1 + i * U) * 4)
                for w in range(W):
                    if is_tile(m - 2):
                        label = (f"b{w}", m - 2)
                        pe.wait_ge(o_emptied, O.free(label, i))
                        for c in range(C):
                            last = nc.tensor.transpose(O.bank(label)[:, c * P:(c + 1) * P], wide[:, m % 2, c, w, :],
                                                       ident[:, :])
                        last.then_inc(o_filled, 1)
                    if is_tile(m):
                        if w % HALF == 0:
                            pe.wait_ge(g_emptied, G.free((f"g{w // HALF}", m), i))
                        if w in POOL_W:
                            n = m * NP + POOL_W.index(w)
                            pe.wait_ge(pool_prods_made, n + 1 + i * U * NP)
                            src = prods_pool[:, n % 3, :]
                        else:
                            n = m * ND + DVE_W.index(w)
                            pe.wait_ge(prods_made, n + 1 + i * U * ND)
                            src = prods[:, n % 4, :]
                        start = LAST - w % HALF * BH
                        nc.tensor.matmul(bank_g[:, :], head_sum[:, start:start + P], src, start=(w % HALF == 0),
                                         stop=(w % HALF == HALF - 1)).then_inc(prods_used, 1)
                    if is_tile(m - 2) and w % 4 == 2 and w >= 6:
                        project(w // 4 - 1)
                    if is_tile(m + 1):
                        if w == 4:
                            turn_x("a", m + 1)
                        if 6 <= w < 6 + C:
                            feed_forward("f1", "a", m + 1, w_f1, w - 6)
                    if is_tile(m - 3):
                        if w == 8:
                            turn_x("c", m - 3)
                        if w >= W - C:
                            feed_forward("f2", "c", m - 3, w_f2, w - (W - C))
                if is_tile(m + 1):
                    project_layer2(0)
                if is_tile(m):
                    turn_scores()
                if is_tile(m + 1):
                    project_layer2(1)
                if is_tile(m - 2):
                    project(FOURS - 1)
                if is_tile(m + 1):
                    project_layer2(2)

            for m in FILL:
                step(m, 0)
            with pe.Fori(0, TURNS) as i:
                for m in TURN:
                    step(m, i)
            for m in DRAIN:
                step(m, 0)

        @block.vector
        def _(dve):
            dve.sem_inc(s_emptied, 2)
            dve.sem_inc(o_emptied, 2)
            dve.sem_inc(y_emptied, 1)
            dve.sem_inc(f_emptied, 1)
            dve.wait_ge(fold_in, FOLD_LOADS * DMA)
            for n, r in enumerate((R0, R1)):
                mask = flags[n].bitcast(U8)
                for c in range(C):
                    nc.vector.tensor_tensor(masked[n][:, c], coefs[n][:, c], mask[:, c], ALU.mult).then_inc(masked_made, 1)
            dve.wait_ge(masked_made, 2 * C)
            for n, (lo, r) in enumerate(((0, R0), (R0, R1))):
                nc.vector.tensor_tensor(pair_sum[:, :, lo:lo + r], masked[n][:, :, 0], masked[n][:, :, 1], ALU.add)\
                    .then_inc(pair_made, 1)
            dve.wait_ge(pair_made, 2)
            for n, (lo, r) in enumerate(((0, R0), (R0, R1))):
                nc.vector.tensor_tensor(expert_sum[:, :, lo:lo + r], pair_sum[:, :, lo:lo + r], masked[n][:, :, 2], ALU.add)\
                    .then_inc(experts_made, 1)
            dve.wait_ge(w_in, LOADS * DMA)
            nc.vector.tensor_scalar(w_f2[:, :, :], signs_raw.bitcast(U8), 2.0, -1.0, ALU.mult, ALU.add).then_inc(signs_made, 1)
            dve.wait_ge(gated_made, 3)

            def step(m, i):
                def statistics(kind, t, x):
                    k = "abc".index(kind)
                    nc.vector.bn_stats(stats[:, k, :], x).then_inc(stats_made, 1)
                    dve.wait_ge(stats_made, ln(kind, t, i))
                    dve.sem_inc(gate, 1)
                    nc.vector.bn_aggr(mv[:, k, :], stats[:, k, :]).then_inc(mv_made, 1)

                def normalise(kind, t, x):
                    k = "abc".index(kind)
                    dve.wait_ge(rstd_made, ln(kind, t, i))
                    nc.vector.tensor_scalar(xn[kind][:, :], x, mv[:, k, 0:1], rstd[:, k:k + 1],
                                            ALU.subtract, ALU.mult).then_inc(xn_made, 1)

                def product(w):
                    n = m * ND + DVE_W.index(w)
                    if w == 0:
                        dve.wait_ge(a_emptied, A.done(("k2", m), i))
                    if n >= 4:
                        used, used_w = (n - 4) // ND, DVE_W[(n - 4) % ND]
                        dve.wait_ge(prods_used, (used + i * U) * W + used_w + 1)
                    nc.vector.tensor_tensor(prods[:, n % 4, :], q2[:, m % 2, :], k2[:, m % 2, w:w + D], ALU.mult)\
                        .then_inc(prods_made, 1)

                new, old, last = m + 1, m - 2, m - 3
                if is_tile(m):
                    product(0)
                    product(1)
                for w in range(W):
                    if is_tile(m) and w + 2 in DVE_W:
                        product(w + 2)
                    if is_tile(old):
                        label = (f"b{w}", old)
                        if w == 0:
                            dve.wait_ge(a_emptied, A.done(("v2", old), i))
                        if old > 0 or w >= 4:
                            dve.wait_ge(values_added, (old - 1 + (w + W - 4) // W) * ADDS + added((w - 4) % W) + i * U * ADDS)
                        dve.wait_ge(o_filled, O.full(label, i))
                        nc.vector.tensor_tensor(values[:, w % 4, :], O.bank(label)[:, :],
                                                v2[:, old % 4, w:w + D], ALU.mult).then_inc(o_emptied, 1)
                    if is_tile(m - 1):
                        t = m - 1
                        scores = [S.bank((f"dots{n}", t))[:, :].rearrange("p (c w b) -> p c b w", c=2, w=W) for n in range(2)]
                        if w < 4:
                            half = w // 2
                            count = (t + i * U) * 2 + half + 1
                            row = probs2[:, half].rearrange("p (c b) w -> p c b w", c=2)
                            most = neg_max2[:, half].rearrange("p (c b) -> p c b", c=2)
                            if w % 2 == 0:
                                dve.wait_ge(s_filled, S.full((f"dots{half}", t), i))
                                nc.vector.tensor_reduce(most, scores[half], AX_X, ALU.max, negate=True).then_inc(max2_made, 1)
                            else:
                                if t > 0 and half == 0:
                                    dve.wait_ge(wide_made, (t + i * U) * 4)
                                dve.wait_ge(max2_made, count)
                                nc.vector.tensor_tensor(row, scores[half], most.unsqueeze(3).to_broadcast([P, 2, BH, W]),
                                                        ALU.add).then_inc(s_emptied, 1)
                        half = w % 2
                        count = (t + i * U) * 2 + half + 1
                        if 4 <= w < 6:
                            dve.wait_ge(exp2_made, count)
                            nc.vector.tensor_reduce(sums2[:, half], probs2[:, half], AX_X, ALU.add).then_inc(sum2_made, 1)
                        if 6 <= w < 8:
                            dve.wait_ge(sum2_made, count)
                            nc.vector.reciprocal(inv2[:, half], sums2[:, half]).then_inc(inv2_made, 1)
                        if 8 <= w < 10:
                            dve.wait_ge(inv2_made, count)
                            nc.vector.tensor_tensor(probs2[:, half], probs2[:, half], along(inv2[:, half], W), ALU.mult)\
                                .then_inc(probs2_made, 1)
                    if is_tile(new):
                        x, y = x_a[:, new % 4, :], x_b[:, new % 4, :]
                        if w == 0:
                            dve.wait_ge(x_loaded[new % 4], DMA * (new // 4 + 1) + i * DMA)
                            statistics("a", new, x)
                        if w == 2:
                            normalise("a", new, x)
                        if w == 10:
                            dve.wait_ge(bias_added, biased("a", new, i))
                            dve.wait_ge(f_filled, F.full(("f1", new), i))
                            nc.vector.scalar_tensor_tensor(out=y, in0=bank_f[:, :], scalar=tgates[:, 0:1], in1=x,
                                                           op0=ALU.mult, op1=ALU.add).then_inc(f_emptied, 1)
                            dve.wait_ge(f_emptied, F.done(("f1", new), i))
                            dve.sem_inc(x_used, 1)
                            statistics("b", new, y)
                        if w == 12:
                            normalise("b", new, y)
                    if is_tile(last):
                        x = x_c[:, last % 2, :]
                        if w == 1:
                            dve.wait_ge(bias_added, biased("b", last, i))
                            dve.wait_ge(y_filled, Y.full(("y", last), i))
                            nc.vector.scalar_tensor_tensor(out=x, in0=bank_y[:, :], scalar=tgates[:, 1:2],
                                                           in1=x_b[:, last % 4, :], op0=ALU.mult, op1=ALU.add)\
                                .then_inc(y_emptied, 1)
                            dve.wait_ge(y_emptied, Y.done(("y", last), i))
                            statistics("c", last, x)
                        if w == 4:
                            normalise("c", last, x)
                if is_tile(last):
                    dve.wait_ge(x_stored[last % 4], 1 + DMA * (last // 4) + i * DMA)
                    dve.wait_ge(f_filled, F.full(("f2", last), i))
                    nc.vector.scalar_tensor_tensor(out=x_d[:, last % 4, :], in0=bank_f[:, :], scalar=f2_gate[:, 0:1],
                                                   in1=x_c[:, last % 2, :], op0=ALU.mult, op1=ALU.add).then_inc(f_emptied, 1)

            for m in FILL:
                step(m, 0)
            with dve.Fori(0, TURNS) as i:
                for m in TURN:
                    step(m, i)
            for m in DRAIN:
                step(m, 0)


def last_layer(nc, io, x_in, ctx_t, x_out, weights):
    TILES = TOKENS // P
    H3, R3 = 8, 16
    LOW = H3 * R3
    SLOTS = 4
    U = 4
    TURNS = (TILES - 2 - 5) // U
    FILL, TURN, DRAIN = range(-2, 5), range(5, 5 + U), range(5 + U * TURNS, TILES + 5)
    ALL = range(-2, TILES + 5)

    def is_tile(t):
        return 0 <= t < TILES

    def in_order(steps, parts):
        return [(name, m + off) for m in steps for name, off in parts if is_tile(m + off)]

    def unit(m, j, back):
        return (4 * m + j - back) // SLOTS, (4 * m + j - back) % SLOTS

    A_PARTS = [("pt2", -1), ("xe", -3), ("pt3", -1), ("xd", 1), ("pt0", 0), ("q", 1), ("lowt", -4), ("pt1", 0)]
    D_PARTS = [("out", -2), ("kv", 1), ("route", -3), ("f3", -4)]
    S_PARTS = [(f"s{j}", 0) for j in range(SLOTS)]
    O_PARTS = [("av1", -1), ("ot0", -1), ("av2", -1), ("ot1", -1), ("av3", -1), ("ot2", -1), ("av0", 0), ("ot3", -1)]
    LN_PARTS = [("e", -2), ("d", 2)]

    with ExitStack() as ctx:
        chip = Chip(nc, ctx, "l3")
        sb, sem = chip.sb, chip.sem
        heads = HeadsOf16(chip, 4, depth=4)
        a_setup = [("low_a", 0), ("low_r", 0), ("low_b", 0), ("none", 0)]
        A = Ring(chip.banks("bank_a"), a_setup + in_order(ALL, A_PARTS), in_order(TURN, A_PARTS), U)
        Dr = Ring(chip.banks("bank_d"), in_order(ALL, D_PARTS), in_order(TURN, D_PARTS), U)
        S = Ring(chip.banks("bank_s"), in_order(ALL, S_PARTS), in_order(TURN, S_PARTS), U)
        O = Ring(chip.banks("bank_o"), in_order(ALL, O_PARTS), in_order(TURN, O_PARTS), U)
        ln_order = in_order(ALL, LN_PARTS)

        def ln(kind, t, i):
            return ln_order.index((kind, t)) + 1 + i * U * len(LN_PARTS)

        def units(t, j, i):
            return t * SLOTS + j + 1 + i * U * SLOTS

        x_tiles = x_in.rearrange("(t p) d -> t p d", p=P)
        out_tiles = x_out.rearrange("(t p) d -> t p d", p=P)

        ident = sb("ident", [P, P])
        eps_col, half_col = sb("eps_col", [P, 1]), sb("half_col", [P, 1])
        wq = sb("wq", [P, C, D])
        wk, wv, wo = weights.wk, weights.wv, weights.wo
        bq, bk, bv = sb("bq", [P, REP]), sb("bk", [P, 1]), sb("bv", [P, KV // 2, 2, HD])
        w_low, w_up = sb("w_low", [P, C, LOW + H3]), sb("w_up", [P, D])
        router_bias = sb("router_bias", [P, H3])
        gates, tgates = sb("gates", [P, 2]), sb("tgates", [P, 2])
        gated_b3 = sb("gated_b3", [P, D])
        router_raw, b3_raw = sb("router_raw", [P, D]), sb("b3_raw", [P, D])

        x_ln, x_a = sb("x_ln", [P, 4, D]), sb("x_a", [P, 4, D])
        x_b, x_c = sb("x_b", [P, 4, D]), sb("x_c", [P, 4, D])
        ctxt = sb("ctxt", [P, 4, C, P])
        xn = {kind: sb(f"xn_{kind}", [P, D]) for kind in "de"}
        xnt = {kind: sb(f"xnt_{kind}", [P, C, P]) for kind in "de"}
        stats, mv = sb("stats", [P, 2, 6]), sb("mv", [P, 2, 2])
        small, rstd = sb("small", [P, 2]), sb("rstd", [P, 2])
        logits, router_max = sb("logits", [P, 2, H3]), sb("router_max", [P, 2])
        router_sum, router_inv, mix = sb("router_sum", [P, 2]), sb("router_inv", [P, 2]), sb("mix", [P, 2, H3])
        low, low_t = sb("low", [P, 2, H3, R3]), sb("low_t", [P, 2, P])

        small_in, router_in = sem("small_in"), sem("router_in")
        cleared, consts_made, masks_made = sem("cleared"), sem("consts_made"), sem("masks_made")
        gates_ready, gated_made, wq_ordered = sem("gates_ready"), sem("gated_made"), sem("wq_ordered")
        ln_loaded, a_loaded, ctx_loaded = ([sem(f"{name}_loaded{t}") for t in range(4)] for name in ("ln", "a", "ctx"))
        x_stored = [sem(f"x_stored{t}") for t in range(4)]
        ln_used, a_used, ctx_used = sem("ln_used"), sem("a_used"), sem("ctx_used")
        a_filled, a_emptied = sem("a_filled"), sem("a_emptied")
        d_filled, d_emptied = sem("d_filled"), sem("d_emptied")
        s_filled, s_emptied, o_filled, o_emptied = heads.s_filled, heads.s_emptied, heads.o_filled, heads.o_emptied
        stats_made, mv_made, rstd_step, rstd_made = sem("stats_made"), sem("mv_made"), sem("rstd_step"), sem("rstd_made")
        xn_made, bias_added = sem("xn_made"), sem("bias_added")
        logits_made, router_max_made, router_exp_made, router_inv_made, mix_made = \
            sem("logits_made"), sem("router_max_made"), sem("router_exp_made"), sem("router_inv_made"), sem("mix_made")
        gate = sem("gate")

        SMALL = 2 + 2 * KV + 4

        block = ctx.enter_context(nc.Block())

        @block.sync
        def _(sp):
            sp.dma_start(router_raw[0:H3, :], io["L3_ffn_Wr"]).then_inc(router_in, DMA)
            for t in range(4):
                sp.dma_start(x_ln[:, t, :], x_tiles[t]).then_inc(ln_loaded[t], DMA)
                sp.dma_start(ctxt[:, t], ctx_t[t // 2][:, :, t % 2 * P:(t % 2 + 1) * P]).then_inc(ctx_loaded[t], DMA)
            for t in range(4):
                sp.dma_start(x_a[:, t, :], x_tiles[t]).then_inc(a_loaded[t], DMA)
            with sp.Fori(0, TILES // 4 - 1) as i:
                for t in range(4):
                    sp.wait_ge(ln_used, i * 4 + t + 1)
                    sp.dma_start(x_ln[:, t, :], x_tiles[i * 4 + 4 + t]).then_inc(ln_loaded[t], DMA)
                    sp.wait_ge(ctx_used, i * 4 + t + 1)
                    sp.dma_start(ctxt[:, t], ctx_t[i * 2 + 2 + t // 2][:, :, t % 2 * P:(t % 2 + 1) * P])\
                      .then_inc(ctx_loaded[t], DMA)
                    sp.wait_ge(a_used, i * 4 + t + 1)
                    sp.dma_start(x_a[:, t, :], x_tiles[i * 4 + 4 + t]).then_inc(a_loaded[t], DMA)
            for t in range(4):
                sp.wait_ge(x_stored[t], 1 + DMA * TILES // 4)

        @block.gpsimd
        def _(pool):
            for t in range(4):
                pool.sem_inc(x_stored[t], 1)
            nc.gpsimd.memset(ident[:, :], 0.0).then_inc(consts_made, 1)
            nc.gpsimd.memset(eps_col[:, :], EPS).then_inc(consts_made, 1)
            nc.gpsimd.memset(half_col[:, :], -0.5).then_inc(consts_made, 1)
            pool.wait_ge(consts_made, 3)
            nc.gpsimd.affine_select(out=ident[:, :], in_=ident[:, :], compare_op=ALU.not_equal, fill=1.0,
                                    base=0, pattern=[[-1, P]], channel_multiplier=1).then_inc(consts_made, 1)
            heads.make_masks(pool, cleared, masks_made)
            for c in range(C):
                for r in range(REP):
                    nc.gpsimd.tensor_copy(heads_by_rep(wq[:, c, :])[:, :, r, :],
                                          heads_as_given(weights.wq_raw[:, c, :])[:, :, r, :]).then_inc(wq_ordered, 1)
            pool.wait_ge(small_in, SMALL * DMA)
            pool.wait_ge(gates_ready, 1)
            nc.gpsimd.tensor_tensor(gated_b3[:, :], b3_raw[:, :], tgates[:, 0:1].to_broadcast([P, D]), ALU.mult)\
                .then_inc(gated_made, 1)
            pool.wait_ge(gated_made, 1)

            def step(m, i):
                def inverse_deviation(kind, t):
                    k = "de".index(kind)
                    pool.wait_ge(mv_made, ln(kind, t, i))
                    nc.gpsimd.tensor_tensor(small[:, k:k + 1], mv[:, k, 1:2], eps_col[:, :], ALU.add).then_inc(rstd_step, 1)
                    pool.wait_ge(rstd_step, ln(kind, t, i))
                    nc.gpsimd.tensor_tensor(rstd[:, k:k + 1], small[:, k:k + 1], half_col[:, :], ALU.pow)\
                        .then_inc(rstd_made, 1)

                if is_tile(m):
                    pool.wait_ge(a_loaded[m % 4], DMA * (m // 4 + 1) + i * DMA)
                    nc.gpsimd.tensor_tensor(x_a[:, m % 4, :], x_a[:, m % 4, :], gated_b3[:, :], ALU.add).then_inc(bias_added, 1)
                if is_tile(m - 2):
                    inverse_deviation("e", m - 2)
                if is_tile(m + 2):
                    inverse_deviation("d", m + 2)

            for m in FILL:
                step(m, 0)
            with pool.Fori(0, TURNS) as i:
                for m in TURN:
                    step(m, i)
            for m in DRAIN:
                step(m, 0)

        @block.scalar
        def _(act):
            def load(out, src, **more):
                act.dma_start(out, src, **more).then_inc(small_in, DMA)

            for n, name in enumerate(("g_xattn", "g_ffn")):
                load(gates[:, n:n + 1], io[name][3:4].partition_broadcast(P))
            for k in range(KV):
                for half in range(2):
                    reps = slice(2 * half, 2 * half + 2)
                    load(bq[k * HD:(k + 1) * HD, reps],
                         io["L3_xattn_bq"][k * REP * HD:(k + 1) * REP * HD].rearrange("(r d) -> d r", r=REP)[:, reps],
                         allow_slow_non_contiguous=True)
            load(bk[:, :], io["L3_xattn_bk"].rearrange("(p a) -> p a", a=1))
            load(bv[:, :, :, :].rearrange("p a h d -> p (a h d)"), io["L3_xattn_bv"].partition_broadcast(P))
            load(b3_raw[:, :], io["L3_xattn_bo"].partition_broadcast(P))
            load(router_bias[:, :], io["L3_ffn_br"].partition_broadcast(P))
            act.sem_inc(a_emptied, 2)
            act.wait_ge(small_in, SMALL * DMA)
            nc.scalar.activation(tgates[:, :], gates[:, :], ACT.Tanh).then_inc(gates_ready, 1)

            def full(label, i=0):
                act.wait_ge(a_filled, A.full(label, i))
                return A.bank(label)[:, :]

            nc.scalar.activation(w_low[:, :, 0:LOW], split4(full(("low_a", 0))), ACT.Copy).then_inc(a_emptied, 1)
            nc.scalar.activation(w_low[:, :, LOW:LOW + H3], full(("low_r", 0))[:, 0:C * H3].rearrange("p (c h) -> p c h", c=C),
                                 ACT.Copy).then_inc(a_emptied, 1)
            nc.scalar.activation(w_up[:, :], full(("low_b", 0)), ACT.Copy).then_inc(a_emptied, 1)
            act.wait_ge(a_filled, A.full(("none", 0)))
            act.sem_inc(a_emptied, 1)

            def step(m, i):
                for j in range(SLOTS):
                    t, n = unit(m, j, 1)
                    if is_tile(t):
                        act.wait_ge(s_emptied, S.done((f"s{n}", t), i))
                        heads.act_exp(SLOTS * (t % 2) + n).then_inc(heads.exp_made, 1)
                    t, n = unit(m, j, 2)
                    if is_tile(t):
                        nc.scalar.activation(heads.probs_t[:, n % 2], full((f"pt{n}", t), i), ACT.Copy).then_inc(a_emptied, 1)
                    if j == 0 and is_tile(m - 3):
                        nc.scalar.activation(xnt["e"][:, :, :], split4(full(("xe", m - 3), i)), ACT.Copy).then_inc(a_emptied, 1)
                    if j == 0 and is_tile(m - 4):
                        t = m - 4
                        act.wait_ge(router_max_made, t + 1 + i * U)
                        nc.scalar.activation(logits[:, t % 2], logits[:, t % 2], ACT.Exp, bias=router_max[:, t % 2:t % 2 + 1],
                                             accum_out=router_sum[:, t % 2:t % 2 + 1]).then_inc(router_exp_made, 1)
                    if j == 1 and is_tile(m + 1):
                        nc.scalar.activation(xnt["d"][:, :, :], split4(full(("xd", m + 1), i)), ACT.Copy).then_inc(a_emptied, 1)
                    if j == 2 and is_tile(m + 1):
                        t = m + 1
                        src = full(("q", t), i).rearrange("p (r b s) -> p r b s", r=REP, b=2)
                        for r in range(REP):
                            last = nc.scalar.activation(heads.qt[:, t % 2 * 2:t % 2 * 2 + 2, r, :], src[:, r], ACT.Identity,
                                                        bias=bq[:, r:r + 1])
                        last.then_inc(a_emptied, 1)
                    if j == 2 and is_tile(m - 4):
                        nc.scalar.activation(low_t[:, m % 2, :], full(("lowt", m - 4), i)[:, 0:P], ACT.Copy).then_inc(a_emptied, 1)
                if is_tile(m - 5):
                    t = m - 5
                    act.wait_ge(d_emptied, Dr.done(("f3", t), i))
                    act.dma_start(out_tiles[t + i * U], x_c[:, t % 4, :]).then_inc(x_stored[t % 4], DMA)

            for m in FILL:
                step(m, 0)
            with act.Fori(0, TURNS) as i:
                for m in TURN:
                    step(m, i)
            for m in DRAIN:
                step(m, 0)

        @block.tensor
        def _(pe):
            pe.wait_ge(consts_made, 4)
            pe.wait_ge(router_in, DMA)
            for label, raw in (("low_a", weights.low_raw), ("low_r", router_raw), ("low_b", weights.up_raw)):
                pe.wait_ge(a_emptied, A.free((label, 0)))
                out = A.bank((label, 0))
                for c in range(C):
                    if label == "low_r":
                        last = nc.tensor.transpose(out[:, c * H3:(c + 1) * H3], raw[0:H3, c * P:(c + 1) * P], ident[0:H3, 0:H3])
                    else:
                        src = raw[:, c * P:(c + 1) * P] if label == "low_a" else raw[:, c, :]
                        last = nc.tensor.transpose(out[:, c * P:(c + 1) * P], src, ident[:, :])
                last.then_inc(a_filled, 1)
            pe.wait_ge(a_emptied, A.done(("low_b", 0)))
            pe.sem_inc(a_filled, 1)
            pe.wait_ge(wq_ordered, C * REP)
            pe.wait_ge(masks_made, 4)

            def step(m, i):
                def turn_x(kind, t):
                    pe.wait_ge(xn_made, ln(kind, t, i))
                    pe.wait_ge(a_emptied, A.free((f"x{kind}", t), i))
                    turned(nc, A.bank((f"x{kind}", t)), xn[kind][:, :], ident).then_inc(a_filled, 1)

                for j in range(SLOTS):
                    if is_tile(m):
                        if j == 0:
                            pe.wait_ge(a_emptied, A.done(("q", m), i))
                            pe.wait_ge(d_emptied, Dr.done(("kv", m), i))
                        label = (f"s{j}", m)
                        pe.wait_ge(s_emptied, S.free(label, i))
                        heads.pe_scores(S.bank(label), SLOTS * (m % 2) + j).then_inc(s_filled, 1)
                    t, n = unit(m, j, 2)
                    if is_tile(t):
                        label = (f"pt{n}", t)
                        pe.wait_ge(heads.exp_made, units(t, n, i))
                        pe.wait_ge(a_emptied, A.free(label, i))
                        heads.pe_turn_probs(A.bank(label), SLOTS * (t % 2) + n, ident).then_inc(a_filled, 1)
                    t, n = unit(m, j, 3)
                    if is_tile(t):
                        pe.wait_ge(a_emptied, A.done((f"pt{n}", t), i))
                        pe.wait_ge(o_emptied, O.free((f"av{n}", t), i))
                        heads.pe_attend(O.bank((f"av{n}", t)), SLOTS * (t % 2) + n).then_inc(o_filled, 1)
                    t, n = unit(m, j, 4)
                    if is_tile(t):
                        pe.wait_ge(o_emptied, O.done((f"av{n}", t), i))
                        pe.wait_ge(o_emptied, O.free((f"ot{n}", t), i))
                        heads.pe_turn_back(O.bank((f"ot{n}", t)), SLOTS * (t % 2) + n, ident).then_inc(o_filled, 1)
                    if j == 0 and is_tile(m - 3):
                        turn_x("e", m - 3)
                    if j == 1 and is_tile(m - 2):
                        t = m - 2
                        pe.wait_ge(o_emptied, O.done(("ot3", t), i))
                        pe.wait_ge(d_emptied, Dr.free(("out", t), i))
                        heads.pe_project(Dr.bank(("out", t)), t % 2, wo).then_inc(d_filled, 1)
                    if j == 1 and is_tile(m + 1):
                        turn_x("d", m + 1)
                    if j == 2 and is_tile(m + 1):
                        t = m + 1
                        pe.wait_ge(ctx_loaded[t % 4], DMA * (t // 4 + 1) + i * DMA)
                        pe.wait_ge(d_emptied, Dr.free(("kv", t), i))
                        out = Dr.bank(("kv", t))
                        for c in range(C):
                            nc.tensor.matmul(out[:, 0:P], wk[:, c, :], ctxt[:, t % 4, c, :], start=(c == 0), stop=(c == C - 1))
                        for c in range(C):
                            last = nc.tensor.matmul(out[:, P:2 * P], ctxt[:, t % 4, c, :], wv[:, c, :],
                                                    start=(c == 0), stop=(c == C - 1))
                        last.then_inc(d_filled, 1)
                        pe.wait_ge(a_emptied, A.done(("xd", t), i))
                        pe.wait_ge(a_emptied, A.free(("q", t), i))
                        for r in range(REP):
                            for c in range(C):
                                last = nc.tensor.matmul(A.bank(("q", t))[:, r * P:(r + 1) * P], wq[:, c, r * P:(r + 1) * P],
                                                        xnt["d"][:, c, :], start=(c == 0), stop=(c == C - 1))
                        last.then_inc(a_filled, 1)
                    if j == 2 and is_tile(m - 4):
                        t = m - 4
                        pe.wait_ge(d_emptied, Dr.done(("route", t), i))
                        pe.wait_ge(a_emptied, A.free(("lowt", t), i))
                        nc.tensor.transpose(A.bank(("lowt", t))[:, 0:P], low[:, t % 2].rearrange("p h r -> p (h r)"),
                                            ident[:, :]).then_inc(a_filled, 1)
                    if j == 3 and is_tile(m - 3):
                        t = m - 3
                        pe.wait_ge(a_emptied, A.done(("xe", t), i))
                        pe.wait_ge(d_emptied, Dr.free(("route", t), i))
                        for c in range(C):
                            last = nc.tensor.matmul(Dr.bank(("route", t))[:, 0:LOW + H3], xnt["e"][:, c, :],
                                                    w_low[:, c, :], start=(c == 0), stop=(c == C - 1))
                        last.then_inc(d_filled, 1)
                    if j == 3 and is_tile(m - 4):
                        t = m - 4
                        pe.wait_ge(a_emptied, A.done(("lowt", t), i))
                        pe.wait_ge(d_emptied, Dr.free(("f3", t), i))
                        nc.tensor.matmul(Dr.bank(("f3", t))[:, :], low_t[:, t % 2, :], w_up[:, :],
                                         start=True, stop=True).then_inc(d_filled, 1)

            for m in FILL:
                step(m, 0)
            with pe.Fori(0, TURNS) as i:
                for m in TURN:
                    step(m, i)
            for m in DRAIN:
                step(m, 0)

        @block.vector
        def _(dve):
            for emptied in (d_emptied, s_emptied, o_emptied):
                dve.sem_inc(emptied, 2)
            dve.wait_ge(masks_made, 4)
            dve.wait_ge(gated_made, 1)

            def step(m, i):
                def statistics(kind, t, x):
                    k = "de".index(kind)
                    nc.vector.bn_stats(stats[:, k, :], x).then_inc(stats_made, 1)
                    dve.wait_ge(stats_made, ln(kind, t, i))
                    dve.sem_inc(gate, 1)
                    nc.vector.bn_aggr(mv[:, k, :], stats[:, k, :]).then_inc(mv_made, 1)

                def normalise(kind, t, x):
                    k = "de".index(kind)
                    dve.wait_ge(rstd_made, ln(kind, t, i))
                    nc.vector.tensor_scalar(xn[kind][:, :], x, mv[:, k, 0:1], rstd[:, k:k + 1],
                                            ALU.subtract, ALU.mult).then_inc(xn_made, 1)

                def route(t):
                    n = t % 2
                    dve.wait_ge(d_filled, Dr.full(("route", t), i))
                    nc.vector.tensor_tensor(logits[:, n], Dr.bank(("route", t))[:, LOW:LOW + H3], router_bias[:, :],
                                            ALU.add).then_inc(logits_made, 1)
                    dve.wait_ge(logits_made, t + 1 + i * U)
                    nc.vector.tensor_reduce(router_max[:, n:n + 1], logits[:, n], AX_X, ALU.max, negate=True)\
                        .then_inc(router_max_made, 1)

                def mix_low(t):
                    n, count = t % 2, t + 1 + i * U
                    dve.wait_ge(router_exp_made, count)
                    nc.vector.reciprocal(router_inv[:, n:n + 1], router_sum[:, n:n + 1]).then_inc(router_inv_made, 1)
                    dve.wait_ge(router_inv_made, count)
                    nc.vector.tensor_scalar(mix[:, n], logits[:, n], router_inv[:, n:n + 1], 2.0 * H3,
                                            ALU.mult, ALU.mult).then_inc(mix_made, 1)
                    dve.wait_ge(mix_made, count)
                    nc.vector.tensor_tensor(low[:, n], Dr.bank(("route", t))[:, 0:LOW].rearrange("p (h r) -> p h r", h=H3),
                                            along(mix[:, n], R3), ALU.mult).then_inc(d_emptied, 1)

                def spread_keys_and_values(t):
                    bank = Dr.bank(("kv", t))
                    dve.wait_ge(d_filled, Dr.full(("kv", t), i))
                    for b in range(2):
                        keys = bank[:, b * SEQ:(b + 1) * SEQ].unsqueeze(1).to_broadcast([P, KV, SEQ])
                        nc.vector.scalar_tensor_tensor(out=heads.kbd[:, t % 2 * 2 + b, :, :], in0=keys, scalar=bk[:, 0:1],
                                                       in1=along(heads.kmask[:, :], SEQ), op0=ALU.add, op1=ALU.mult)
                    values = bank[:, P:2 * P].rearrange("p (a h d) -> p a h d", a=KV // 2, h=2, d=HD)
                    for b in range(2):
                        rows = slice(b * SEQ, (b + 1) * SEQ)
                        for h in range(2):
                            out = heads.vbd[h * SEQ:(h + 1) * SEQ, t % 2 * 2 + b, :, h * HD:(h + 1) * HD]
                            last = nc.vector.tensor_tensor(out, values[rows, :, h, :], bv[rows, :, h, :], ALU.add)
                    last.then_inc(d_emptied, 1)

                for j in range(SLOTS):
                    if is_tile(m):
                        label, u = (f"s{j}", m), SLOTS * (m % 2) + j
                        dve.wait_ge(s_filled, S.full(label, i))
                        heads.dve_max(S.bank(label), u).then_inc(heads.max_made, 1)
                    t, n = unit(m, j, 3)
                    if is_tile(t):
                        dve.wait_ge(o_filled, O.full((f"av{n}", t), i))
                        heads.dve_inverse(O.bank((f"av{n}", t)), n).then_inc(heads.inv_made, 1)
                    if is_tile(m):
                        dve.wait_ge(heads.max_made, units(m, j, i))
                        heads.dve_shift(S.bank(label), u).then_inc(s_emptied, 1)
                    if is_tile(t):
                        dve.wait_ge(heads.inv_made, units(t, n, i))
                        heads.dve_norm(O.bank((f"av{n}", t)), n).then_inc(o_emptied, 1)
                    t, n = unit(m, j, 4)
                    if is_tile(t):
                        dve.wait_ge(o_filled, O.full((f"ot{n}", t), i))
                        heads.dve_copy_back(O.bank((f"ot{n}", t)), SLOTS * (t % 2) + n).then_inc(o_emptied, 1)
                    if j == 0 and is_tile(m - 4):
                        route(m - 4)
                    if j == 1 and is_tile(m - 4):
                        mix_low(m - 4)
                    if j == 1 and is_tile(m - 5):
                        t = m - 5
                        dve.wait_ge(x_stored[t % 4], 1 + DMA * (t // 4) + i * DMA)
                        dve.wait_ge(d_filled, Dr.full(("f3", t), i))
                        nc.vector.scalar_tensor_tensor(out=x_c[:, t % 4, :], in0=Dr.bank(("f3", t))[:, :], scalar=tgates[:, 1:2],
                                                       in1=x_b[:, t % 4, :], op0=ALU.mult, op1=ALU.add).then_inc(d_emptied, 1)
                    if j == 2 and is_tile(m - 2):
                        t = m - 2
                        dve.wait_ge(bias_added, t + 1 + i * U)
                        dve.wait_ge(d_filled, Dr.full(("out", t), i))
                        nc.vector.scalar_tensor_tensor(out=x_b[:, t % 4, :], in0=Dr.bank(("out", t))[:, :], scalar=tgates[:, 0:1],
                                                       in1=x_a[:, t % 4, :], op0=ALU.mult, op1=ALU.add).then_inc(d_emptied, 1)
                        dve.wait_ge(d_emptied, Dr.done(("out", t), i))
                        dve.sem_inc(a_used, 1)
                        statistics("e", t, x_b[:, t % 4, :])
                    if j == 2 and is_tile(m + 2):
                        t = m + 2
                        dve.wait_ge(ln_loaded[t % 4], DMA * (t // 4 + 1) + i * DMA)
                        statistics("d", t, x_ln[:, t % 4, :])
                    if j == 3:
                        if is_tile(m + 1):
                            spread_keys_and_values(m + 1)
                            dve.wait_ge(d_emptied, Dr.done(("kv", m + 1), i))
                            dve.sem_inc(ctx_used, 1)
                        if is_tile(m - 2):
                            normalise("e", m - 2, x_b[:, (m - 2) % 4, :])
                        if is_tile(m + 2):
                            normalise("d", m + 2, x_ln[:, (m + 2) % 4, :])
                            dve.wait_ge(xn_made, ln("d", m + 2, i))
                            dve.sem_inc(ln_used, 1)

            for m in FILL:
                step(m, 0)
            with dve.Fori(0, TURNS) as i:
                for m in TURN:
                    step(m, i)
            for m in DRAIN:
                step(m, 0)


UNUSED = ("L0_ffn_lut8",)


def flamingo_layers(nc, io, out):
    ctx_t = nc.dram_tensor("ctx_transposed", (TOKENS // 256, P, C, 256), F32, kind="Internal").ap()
    x_1 = nc.dram_tensor("x_after_layer_0", (TOKENS, D), F32, kind="Internal").ap()
    x_2 = nc.dram_tensor("x_after_latents", (TOKENS, D), F32, kind="Internal").ap()
    x_3 = nc.dram_tensor("x_after_layer_2", (TOKENS, D), F32, kind="Internal").ap()
    with ExitStack() as ctx:
        early = ctx.enter_context(nc.sbuf_tensor("early", [P, 4 * C * D], F32))
        cross_attention_and_quantised_ffn(nc, io, io["x"], io["ctx_4096"], x_1, ctx_t, early)
        latent_attention(nc, io, x_1, ctx_t, x_2, early)
    with ExitStack() as ctx:
        last_weights = LastWeights(nc, ctx)
        window_attention(nc, io, x_2, io["ctx_4096"], x_3, last_weights)
        last_layer(nc, io, x_3, ctx_t, out, last_weights)


def fourier_rows(n):
    import numpy as np
    j = np.arange(n)
    rows = np.empty((n, n))
    rows[0] = 1 / np.sqrt(n)
    for m in range(1, (n - 1) // 2 + 1):
        rows[2 * m - 1] = np.sqrt(2 / n) * np.cos(2 * np.pi * ((m * j) % n) / n)
        rows[2 * m] = np.sqrt(2 / n) * np.sin(2 * np.pi * ((m * j) % n) / n)
    if n % 2 == 0:
        rows[n - 1] = (-1.0) ** j / np.sqrt(n)
    return rows.astype(np.float32)


def kernel(**inputs):
    import numpy as np
    import concourse.bacc as bacc
    from concourse import mybir as mb
    from concourse.bass_utils import run_bass_kernel_spmd

    nc = bacc.Bacc("TRN2", target_bir_lowering=False, num_devices=1)
    arrays, io = {}, {}
    for name, value in inputs.items():
        if name in UNUSED:
            continue
        a = np.ascontiguousarray(value)
        if a.dtype == np.bool_:
            a = a.view(np.int32)
        if name in ("x", "ctx_4096"):
            a = a.reshape(TOKENS, D)
        if a.ndim == 0:
            a = a.reshape(1)
        arrays[f"in_{name}"] = a
        io[name] = nc.dram_tensor(f"in_{name}", a.shape, mb.dt.from_np(a.dtype), kind="ExternalInput").ap()
    arrays["in_fourier"] = fourier_rows(D)
    io["fourier"] = nc.dram_tensor("in_fourier", (D, D), mb.dt.float32, kind="ExternalInput").ap()
    out = nc.dram_tensor("out_x", (TOKENS, D), mb.dt.float32, kind="ExternalOutput").ap()
    flamingo_layers(nc, io, out)
    result = run_bass_kernel_spmd(nc, [arrays], core_ids=[0])
    return result.results[0]["out_x"].reshape(32, SEQ, D)
```
